# Optimizing a Trainium2 kernel written in Bass

```python
import numpy as np
import jax
import jax.numpy as jnp

def _softmax(x, axis=-1):
    return jax.nn.softmax(x, axis=axis)

def _gelu(x):
    return jax.nn.gelu(x, approximate=True)

def _silu(x):
    return jax.nn.silu(x)

def _sigmoid(x):
    return jax.nn.sigmoid(x)

def _layernorm(x, axis=-1, eps=1e-05):
    m = jnp.mean(x, axis=axis, keepdims=True)
    v = jnp.var(x, axis=axis, keepdims=True)
    return (x - m) / jnp.sqrt(v + eps)

def _scatter_add(tgt, idx, src, axis=0):
    return tgt.at[idx].add(src)

def _segment_sum(src, seg, n):
    return jax.ops.segment_sum(src, seg, n)
kernel_name = 'mk_xattn_ffn_d2_seqx_r8_1a2919'

def setup_inputs(seed: int=0):
    np.random.seed(seed)
    _w = jnp.asarray

    def _rec_inputs():
        import jax
        import jax.numpy as jnp
        _rk = jax.random.key(seed)
        x = 0.0002417 + 0.9998 * jax.random.normal(jax.random.fold_in(_rk, 1), (8, 128, 128), jnp.float32)
        _lenS = 128 - jax.random.randint(jax.random.fold_in(_rk, 7), (8,), 0, max(1, 128 // 4) + 1, jnp.int32)
        _lenS2 = 120 - jax.random.randint(jax.random.fold_in(_rk, 8), (8,), 0, max(1, 120 // 4) + 1, jnp.int32)
        _ctx_1024P = jax.random.normal(jax.random.fold_in(_rk, 11), (8, 16, 128), jnp.float32)
        _ctx_1024c = jax.random.dirichlet(jax.random.fold_in(_rk, 511), 0.3 * jnp.ones((16,), jnp.float32), (8, 120))
        _ctx_1024t = jnp.einsum('bsk,bkd->bsd', _ctx_1024c, _ctx_1024P)
        _ctx_1024t = _ctx_1024t * jax.lax.rsqrt(jnp.mean(jnp.square(_ctx_1024t)) + 1e-12) * 0.953939
        ctx_1024 = 7.22013e-05 + 1.00017 * (_ctx_1024t + 0.3 * jax.random.normal(jax.random.fold_in(_rk, 611), (8, 120, 128), jnp.float32))
        _validS = jnp.arange(128)[None, :] < _lenS[:, None]
        _validS2 = jnp.arange(120)[None, :] < _lenS2[:, None]
        _causal = jnp.tril(jnp.ones((128, 128), dtype=bool))
        mask_BxS2_bk0 = jnp.logical_not(jnp.broadcast_to(_validS2[:, :], (8, 120)))
        return (x, ctx_1024, mask_BxS2_bk0)
    x, ctx_1024, mask_BxS2_bk0 = _rec_inputs()

    def _L0_xattn_setup():
        import jax, jax.numpy as jnp
        import numpy as np
        EMBED = 128
        HEADS = 16
        HEAD_DIM = EMBED // HEADS
        key = jax.random.key(seed)
        ks = jax.random.split(key, 8)
        N, L = (4, 256)
        values = jax.random.normal(ks[0], (N, L, EMBED), dtype=jnp.float32)
        keys_ = jax.random.normal(ks[1], (N, L, EMBED), dtype=jnp.float32)
        queries = jax.random.normal(ks[2], (N, L, EMBED), dtype=jnp.float32)
        s = 1.0 / np.sqrt(HEAD_DIM)
        Wv = jax.random.normal(ks[3], (HEAD_DIM, HEAD_DIM), dtype=jnp.float32) * s
        Wk = jax.random.normal(ks[4], (HEAD_DIM, HEAD_DIM), dtype=jnp.float32) * s
        Wq = jax.random.normal(ks[5], (HEAD_DIM, HEAD_DIM), dtype=jnp.float32) * s
        Wo = jax.random.normal(ks[6], (EMBED, EMBED), dtype=jnp.float32) * (1.0 / np.sqrt(EMBED))
        bo = jnp.zeros((EMBED,), dtype=jnp.float32)
        return {'values': values, 'keys': keys_, 'queries': queries, 'Wv': Wv, 'Wk': Wk, 'Wq': Wq, 'Wo': Wo, 'bo': bo}
    _L0_xattn_all = _L0_xattn_setup()
    _L0_xattn_in = {k: v for k, v in _L0_xattn_all.items() if k in ('Wv', 'Wk', 'Wq', 'Wo', 'bo')}
    del _L0_xattn_all

    def _L0_ffn_setup():
        import jax, jax.numpy as jnp
        import numpy as np
        H_DIM, E_DIM = (128, 64)
        N_SHARED, N_ROUTED, TOP_K = (2, 16, 4)
        B, S = (4, 256)
        key = jax.random.key(seed)
        ks = jax.random.split(key, 6)
        sc = 1.0 / np.sqrt(H_DIM)
        ec = 1.0 / np.sqrt(E_DIM)
        return {'x': jax.random.normal(ks[0], (B, S, H_DIM), dtype=jnp.float32), 'shared_up': jax.random.uniform(ks[1], (N_SHARED, E_DIM, H_DIM), jnp.float32, -sc, sc), 'shared_down': jax.random.uniform(ks[2], (N_SHARED, H_DIM, E_DIM), jnp.float32, -ec, ec), 'routed_up': jax.random.uniform(ks[3], (N_ROUTED, E_DIM, H_DIM), jnp.float32, -sc, sc), 'routed_down': jax.random.uniform(ks[4], (N_ROUTED, H_DIM, E_DIM), jnp.float32, -ec, ec), 'router_w': jax.random.uniform(ks[5], (N_ROUTED, H_DIM), jnp.float32, -sc, sc)}
    _L0_ffn_all = _L0_ffn_setup()
    _L0_ffn_in = {k: v for k, v in _L0_ffn_all.items() if k in ('shared_up', 'shared_down', 'routed_up', 'routed_down', 'router_w')}
    del _L0_ffn_all

    def _L1_xattn_setup():
        import jax, jax.numpy as jnp
        import numpy as np
        B, LQ, LKV = (8, 128, 256)
        QDIM, KDIM, HID = (128, 128, 128)
        key = jax.random.key(seed)
        ks = jax.random.split(key, 12)
        s = lambda d: 1.0 / np.sqrt(d)
        return {'query': jax.random.normal(ks[0], (B, LQ, QDIM), jnp.float32), 'key_value': jax.random.normal(ks[1], (B, LKV, KDIM), jnp.float32), 'key_mask': jax.random.randint(ks[2], (B, LKV), 0, 2).astype(bool), 'Wq': jax.random.uniform(ks[3], (QDIM, HID), jnp.float32, -s(QDIM), s(QDIM)), 'bq': jax.random.uniform(ks[4], (HID,), jnp.float32, -s(QDIM), s(QDIM)), 'Wk': jax.random.uniform(ks[5], (KDIM, HID), jnp.float32, -s(KDIM), s(KDIM)), 'bk': jax.random.uniform(ks[6], (HID,), jnp.float32, -s(KDIM), s(KDIM)), 'Wv': jax.random.uniform(ks[7], (KDIM, HID), jnp.float32, -s(KDIM), s(KDIM)), 'bv': jax.random.uniform(ks[8], (HID,), jnp.float32, -s(KDIM), s(KDIM)), 'Wo': jax.random.uniform(ks[9], (HID, QDIM), jnp.float32, -s(HID), s(HID)), 'bo': jax.random.uniform(ks[10], (QDIM,), jnp.float32, -s(HID), s(HID))}
    _L1_xattn_all = _L1_xattn_setup()
    _L1_xattn_in = {k: v for k, v in _L1_xattn_all.items() if k in ('Wq', 'bq', 'Wk', 'bk', 'Wv', 'bv', 'Wo', 'bo')}
    del _L1_xattn_all

    def _L1_ffn_setup():
        import jax, jax.numpy as jnp
        import numpy as np
        LATENT = 128
        LEAF_W = 64
        DEPTH = 4
        N_LEAVES = 2 ** DEPTH
        N_NODES = 2 ** DEPTH - 1
        B, S = (4, 256)

        def _fff_params(key, prefix):
            ks = jax.random.split(key, 4)
            d, h, l, n = (LATENT, LEAF_W, N_LEAVES, N_NODES)
            s_in = 1.0 / np.sqrt(d).astype(np.float32)
            s_h = 1.0 / np.sqrt(h).astype(np.float32)
            return {f'{prefix}_node_w': jax.random.normal(ks[0], (n, d), jnp.float32) * s_in, f'{prefix}_node_b': jax.random.normal(ks[1], (n,), jnp.float32) * s_in, f'{prefix}_w1': jax.random.normal(ks[2], (l, d, h), jnp.float32) * s_in, f'{prefix}_b1': jnp.zeros((l, h), jnp.float32), f'{prefix}_w2': jax.random.normal(ks[3], (l, h, d), jnp.float32) * s_h, f'{prefix}_b2': jnp.zeros((l, d), jnp.float32)}

        def _fff(x, node_w, node_b, w1, b1, w2, b2):
            Bx, Sx, D = x.shape
            xf = x.reshape(-1, D)
            N = xf.shape[0]
            cur = jnp.zeros((N,), jnp.int32)
            for _ in range(DEPTH):
                pw = node_w[cur]
                score = jnp.einsum('nd,nd->n', xf, pw) + node_b[cur]
                cur = 2 * cur + 1 + (score >= 0).astype(jnp.int32)
            leaf = cur - N_NODES
            sel = jax.nn.one_hot(leaf, N_LEAVES, dtype=xf.dtype)
            hidden_all = jax.nn.relu(jnp.einsum('nd,ldh->lnh', xf, w1) + b1[:, None, :])
            hidden = hidden_all * sel.T[:, :, None]
            out = jnp.einsum('lnh,lho->no', hidden, w2) + sel @ b2
            return out.reshape(Bx, Sx, D)
        key = jax.random.key(seed)
        kx, kq, kk, kv = jax.random.split(key, 4)
        inp = {'x': jax.random.normal(kx, (B, S, LATENT), jnp.float32)}
        inp.update(_fff_params(kq, 'q'))
        inp.update(_fff_params(kk, 'k'))
        inp.update(_fff_params(kv, 'v'))
        return inp
    _L1_ffn_all = _L1_ffn_setup()
    _L1_ffn_in = {k: v for k, v in _L1_ffn_all.items() if k in ('q_node_w', 'q_node_b', 'q_w1', 'q_b1', 'q_w2', 'q_b2', 'k_node_w', 'k_node_b', 'k_w1', 'k_b1', 'k_w2', 'k_b2', 'v_node_w', 'v_node_b', 'v_w1', 'v_b1', 'v_w2', 'v_b2')}
    del _L1_ffn_all
    return {'x': x, 'ctx_1024': ctx_1024, 'mask_BxS2_bk0': mask_BxS2_bk0, 'L0_xattn_Wv': _L0_xattn_in['Wv'], 'L0_xattn_Wk': _L0_xattn_in['Wk'], 'L0_xattn_Wq': _L0_xattn_in['Wq'], 'L0_xattn_Wo': _L0_xattn_in['Wo'], 'L0_xattn_bo': _L0_xattn_in['bo'], 'L0_ffn_shared_up': _L0_ffn_in['shared_up'], 'L0_ffn_shared_down': _L0_ffn_in['shared_down'], 'L0_ffn_routed_up': _L0_ffn_in['routed_up'], 'L0_ffn_routed_down': _L0_ffn_in['routed_down'], 'L0_ffn_router_w': _L0_ffn_in['router_w'], 'L1_xattn_Wq': _L1_xattn_in['Wq'], 'L1_xattn_bq': _L1_xattn_in['bq'], 'L1_xattn_Wk': _L1_xattn_in['Wk'], 'L1_xattn_bk': _L1_xattn_in['bk'], 'L1_xattn_Wv': _L1_xattn_in['Wv'], 'L1_xattn_bv': _L1_xattn_in['bv'], 'L1_xattn_Wo': _L1_xattn_in['Wo'], 'L1_xattn_bo': _L1_xattn_in['bo'], 'L1_ffn_q_node_w': _L1_ffn_in['q_node_w'], 'L1_ffn_q_node_b': _L1_ffn_in['q_node_b'], 'L1_ffn_q_w1': _L1_ffn_in['q_w1'], 'L1_ffn_q_b1': _L1_ffn_in['q_b1'], 'L1_ffn_q_w2': _L1_ffn_in['q_w2'], 'L1_ffn_q_b2': _L1_ffn_in['q_b2'], 'L1_ffn_k_node_w': _L1_ffn_in['k_node_w'], 'L1_ffn_k_node_b': _L1_ffn_in['k_node_b'], 'L1_ffn_k_w1': _L1_ffn_in['k_w1'], 'L1_ffn_k_b1': _L1_ffn_in['k_b1'], 'L1_ffn_k_w2': _L1_ffn_in['k_w2'], 'L1_ffn_k_b2': _L1_ffn_in['k_b2'], 'L1_ffn_v_node_w': _L1_ffn_in['v_node_w'], 'L1_ffn_v_node_b': _L1_ffn_in['v_node_b'], 'L1_ffn_v_w1': _L1_ffn_in['v_w1'], 'L1_ffn_v_b1': _L1_ffn_in['v_b1'], 'L1_ffn_v_w2': _L1_ffn_in['v_w2'], 'L1_ffn_v_b2': _L1_ffn_in['v_b2']}

def reference(x, ctx_1024, mask_BxS2_bk0, L0_xattn_Wv, L0_xattn_Wk, L0_xattn_Wq, L0_xattn_Wo, L0_xattn_bo, L0_ffn_shared_up, L0_ffn_shared_down, L0_ffn_routed_up, L0_ffn_routed_down, L0_ffn_router_w, L1_xattn_Wq, L1_xattn_bq, L1_xattn_Wk, L1_xattn_bk, L1_xattn_Wv, L1_xattn_bv, L1_xattn_Wo, L1_xattn_bo, L1_ffn_q_node_w, L1_ffn_q_node_b, L1_ffn_q_w1, L1_ffn_q_b1, L1_ffn_q_w2, L1_ffn_q_b2, L1_ffn_k_node_w, L1_ffn_k_node_b, L1_ffn_k_w1, L1_ffn_k_b1, L1_ffn_k_w2, L1_ffn_k_b2, L1_ffn_v_node_w, L1_ffn_v_node_b, L1_ffn_v_w1, L1_ffn_v_b1, L1_ffn_v_w2, L1_ffn_v_b2):
    import jax
    import jax.numpy as jnp

    def _L0_xattn_ref(values, keys, queries, Wv, Wk, Wq, Wo, bo):
        import jax, jax.numpy as jnp
        import numpy as np
        EMBED = 128
        HEADS = 16
        HEAD_DIM = EMBED // HEADS
        N, L, _ = queries.shape
        v = values.reshape(N, -1, HEADS, HEAD_DIM)
        k = keys.reshape(N, -1, HEADS, HEAD_DIM)
        q = queries.reshape(N, L, HEADS, HEAD_DIM)
        v = jnp.einsum('nlhd,ed->nlhe', v, Wv)
        k = jnp.einsum('nlhd,ed->nlhe', k, Wk)
        q = jnp.einsum('nqhd,ed->nqhe', q, Wq)
        scores = jnp.einsum('nqhd,nkhd->nhqk', q, k) / jnp.sqrt(jnp.float32(EMBED))
        attn = jax.nn.softmax(scores, axis=-1)
        out = jnp.einsum('nhqk,nkhd->nqhd', attn, v).reshape(N, L, EMBED)
        return out @ Wo.T + bo

    def _L0_ffn_ref(x, shared_up, shared_down, routed_up, routed_down, router_w):
        import jax, jax.numpy as jnp
        import numpy as np
        H_DIM, E_DIM = (128, 64)
        N_SHARED, N_ROUTED, TOP_K = (2, 16, 4)
        B, S = (4, 256)
        b, s, h = x.shape
        xt = x.reshape(-1, h)
        up_s = jnp.einsum('th,seh->tse', xt, shared_up)
        shared = jnp.einsum('tse,she->th', jax.nn.gelu(up_s, approximate=False), shared_down)
        probs = jax.nn.softmax(xt @ router_w.T, axis=-1)
        topk_p, topk_i = jax.lax.top_k(probs, TOP_K)
        gate = jnp.zeros_like(probs).at[jnp.arange(xt.shape[0])[:, None], topk_i].add(topk_p)
        up_r = jnp.einsum('th,reh->tre', xt, routed_up)
        act = jax.nn.gelu(up_r, approximate=False) * gate[:, :, None]
        routed = jnp.einsum('tre,rhe->th', act, routed_down)
        return (shared + routed).reshape(b, s, h)

    def _L1_xattn_ref(query, key_value, key_mask, Wq, bq, Wk, bk, Wv, bv, Wo, bo):
        import jax, jax.numpy as jnp
        import numpy as np
        B, LQ, LKV = (8, 128, 256)
        QDIM, KDIM, HID = (128, 128, 128)
        Q = query @ Wq + bq
        K = key_value @ Wk + bk
        V = key_value @ Wv + bv
        hid = Q.shape[-1]
        scores = jnp.einsum('bqh,bkh->bqk', Q, K) / jnp.sqrt(jnp.float32(hid))
        scores = jnp.where(key_mask[:, None, :], scores, jnp.float32(-1000000000.0))
        attn = jax.nn.softmax(scores, axis=-1)
        context = jnp.einsum('bqk,bkh->bqh', attn, V)
        return context @ Wo + bo

    def _L1_ffn_ref(x, q_node_w, q_node_b, q_w1, q_b1, q_w2, q_b2, k_node_w, k_node_b, k_w1, k_b1, k_w2, k_b2, v_node_w, v_node_b, v_w1, v_b1, v_w2, v_b2):
        import jax, jax.numpy as jnp
        import numpy as np
        LATENT = 128
        LEAF_W = 64
        DEPTH = 4
        N_LEAVES = 2 ** DEPTH
        N_NODES = 2 ** DEPTH - 1
        B, S = (4, 256)

        def _fff_params(key, prefix):
            ks = jax.random.split(key, 4)
            d, h, l, n = (LATENT, LEAF_W, N_LEAVES, N_NODES)
            s_in = 1.0 / np.sqrt(d).astype(np.float32)
            s_h = 1.0 / np.sqrt(h).astype(np.float32)
            return {f'{prefix}_node_w': jax.random.normal(ks[0], (n, d), jnp.float32) * s_in, f'{prefix}_node_b': jax.random.normal(ks[1], (n,), jnp.float32) * s_in, f'{prefix}_w1': jax.random.normal(ks[2], (l, d, h), jnp.float32) * s_in, f'{prefix}_b1': jnp.zeros((l, h), jnp.float32), f'{prefix}_w2': jax.random.normal(ks[3], (l, h, d), jnp.float32) * s_h, f'{prefix}_b2': jnp.zeros((l, d), jnp.float32)}

        def _fff(x, node_w, node_b, w1, b1, w2, b2):
            Bx, Sx, D = x.shape
            xf = x.reshape(-1, D)
            N = xf.shape[0]
            cur = jnp.zeros((N,), jnp.int32)
            for _ in range(DEPTH):
                pw = node_w[cur]
                score = jnp.einsum('nd,nd->n', xf, pw) + node_b[cur]
                cur = 2 * cur + 1 + (score >= 0).astype(jnp.int32)
            leaf = cur - N_NODES
            sel = jax.nn.one_hot(leaf, N_LEAVES, dtype=xf.dtype)
            hidden_all = jax.nn.relu(jnp.einsum('nd,ldh->lnh', xf, w1) + b1[:, None, :])
            hidden = hidden_all * sel.T[:, :, None]
            out = jnp.einsum('lnh,lho->no', hidden, w2) + sel @ b2
            return out.reshape(Bx, Sx, D)
        q = _fff(x, q_node_w, q_node_b, q_w1, q_b1, q_w2, q_b2)
        k = _fff(x, k_node_w, k_node_b, k_w1, k_b1, k_w2, k_b2)
        v = _fff(x, v_node_w, v_node_b, v_w1, v_b1, v_w2, v_b2)
        scale = 1.0 / np.sqrt(LATENT).astype(np.float32)
        attn = jax.nn.softmax(jnp.einsum('bqd,bkd->bqk', q, k) * scale, axis=-1)
        return jnp.einsum('bqk,bkd->bqd', attn, v)
    x = x + _L0_xattn_ref(ctx_1024, ctx_1024, _layernorm(x, axis=-1), L0_xattn_Wv, L0_xattn_Wk, L0_xattn_Wq, L0_xattn_Wo, L0_xattn_bo)
    x = x + _L0_ffn_ref(_layernorm(x, axis=-1), L0_ffn_shared_up, L0_ffn_shared_down, L0_ffn_routed_up, L0_ffn_routed_down, L0_ffn_router_w)
    x = x + _L1_xattn_ref(_layernorm(x, axis=-1), ctx_1024, mask_BxS2_bk0, L1_xattn_Wq, L1_xattn_bq, L1_xattn_Wk, L1_xattn_bk, L1_xattn_Wv, L1_xattn_bv, L1_xattn_Wo, L1_xattn_bo)
    x = x + _L1_ffn_ref(_layernorm(x, axis=-1), L1_ffn_q_node_w, L1_ffn_q_node_b, L1_ffn_q_w1, L1_ffn_q_b1, L1_ffn_q_w2, L1_ffn_q_b2, L1_ffn_k_node_w, L1_ffn_k_node_b, L1_ffn_k_w1, L1_ffn_k_b1, L1_ffn_k_w2, L1_ffn_k_b2, L1_ffn_v_node_w, L1_ffn_v_node_b, L1_ffn_v_w1, L1_ffn_v_b1, L1_ffn_v_w2, L1_ffn_v_b2)
    return x

_drawn_inputs = setup_inputs


def setup_inputs(seed=0):
    import zlib

    import numpy as np

    out = dict(_drawn_inputs(seed))
    spreads = {'L0_xattn_bo': (0.0, 0.1),
     'L1_ffn_q_b1': (0.0, 0.8),
     'L1_ffn_q_b2': (0.0, 0.8),
     'L1_ffn_k_b1': (0.0, 0.8),
     'L1_ffn_k_b2': (0.0, 0.8),
     'L1_ffn_v_b1': (0.0, 0.475),
     'L1_ffn_v_b2': (0.0, 0.285)}
    factors = {'L1_xattn_bq': 8.0, 'L1_xattn_bk': 8.0, 'L1_ffn_q_node_b': 5.879, 'L1_ffn_k_node_b': 7.907}
    for name, (base, spread) in spreads.items():
        noise = np.random.default_rng([zlib.crc32(name.encode()), seed]).standard_normal(out[name].shape)
        drawn = base * np.exp(spread * noise) if base else spread * noise
        out[name] = jnp.asarray(drawn.astype(out[name].dtype))
    for name, factor in factors.items():
        out[name] = (out[name] * factor).astype(out[name].dtype)
    return out
```

```python
from contextlib import ExitStack

import concourse.bass as bass
from concourse import mybir

F32 = mybir.dt.float32
F32R = mybir.dt.float32r
BF16 = mybir.dt.bfloat16
U8 = mybir.dt.uint8
ALU = mybir.AluOpType
ACT = mybir.ActivationFunctionType
AX = mybir.AxisListType

B, T, D = 8, 128, 128
S2 = 120
HEADS, HD = 16, 8
BLOCKS, TILES = 4, 4
HALF = B // 2
NT = HALF * T
NK = HALF * S2
UNITS = B * TILES
EXPERTS, TOPK, PAIRS = 16, 4, 9
NETS, LEAVES, NODES, CHUNKS = 3, 16, 15, 8
UPB = NETS * CHUNKS
SEL = 64
EPS = 1e-5
SCALE = float(D) ** -0.5
NEG = -1e9
BIG = 2.0 ** 100

C_ID, C_SX, C_BX, C_SK, C_BK, C_PART, C_LEAF, C_END = 0, 128, 129, 130, 131, 132, 135, 151
V_BK, V_BV, V_BQ, V_END = 0, 1, 2, 3
R_BO0, R_BO1, R_NB, R_END = 0, 128, 256, 256 + NETS * NODES


def build(nc: bass.Bass, x, ctx, ctxT, mask, consts, gsel, blockw, woT, up0, down0, router,
          attnw, cols, rows, w1, w2, nodew, leafb, out):
    stack = ExitStack()
    with stack:
        def sb(name, shape, dt=F32):
            return stack.enter_context(nc.sbuf_tensor(name, shape, dt))

        def sem(name):
            return stack.enter_context(nc.semaphore(name))

        bank = [stack.enter_context(nc.psum_tensor(f"bank{i}", [128, 512], F32)) for i in range(8)]
        T0, T1, Y, Z = bank[0], bank[1], bank[2], bank[3]
        U = bank[4:6]
        G = bank[6:8]
        W4 = bank[4:8]

        c_sb = sb("c_sb", [128, C_END])
        ident = c_sb[:, C_ID:C_ID + 128]
        idb = sb("idb", [128, 128], BF16)
        gsel_sb = sb("gsel_sb", [48, PAIRS - 1, 128], BF16)
        x0 = sb("x0", [T, B, D])
        ctx_sb = sb("ctx_sb", [S2, B, D])
        ctxT_sb = sb("ctxT_sb", [D, B * S2])
        blockw_sb = sb("blockw_sb", [128, 3, 128])
        woT_sb = sb("woT_sb", [128, 128])
        staged = sb("staged", [128, UPB * 128])
        router_sb = sb("router_sb", [128, EXPERTS])
        attnw_sb = sb("attnw_sb", [128, 4, 128])
        cols_sb = sb("cols_sb", [128, V_END])
        rows_sb = sb("rows_sb", [128, R_END])
        mask_u8 = sb("mask_u8", [128, B * S2], U8)
        nodew_sb = sb("nodew_sb", [128, NETS * NODES])
        leafb_sb = sb("leafb_sb", [128, 2, 64 + 128])

        up0h, up0l = sb("up0h", [128, PAIRS * 128], F32R), sb("up0l", [128, PAIRS * 128], F32R)
        down0h, down0l = sb("down0h", [128, PAIRS * 128], F32R), sb("down0l", [128, PAIRS * 128], F32R)
        w1h, w1l = sb("w1h", [128, UPB * 128], F32R), sb("w1l", [128, UPB * 128], F32R)
        w2h, w2l = sb("w2h", [128, UPB * 128], F32R), sb("w2l", [128, UPB * 128], F32R)
        W0 = PAIRS * 128
        SPLITS = [(staged[:, 0:W0], up0h, up0l), (staged[:, W0:2 * W0], down0h, down0l),
                  (staged[:, :], w1h, w1l), (staged[:, :], w2h, w2l)]

        xres = sb("xres", [T, B, D])
        xs = [x0, xres, xres, xres]
        stats = sb("stats", [T, 8, HALF, 6])
        meanvar = sb("meanvar", [T, 8, HALF, 2])
        vareps = sb("vareps", [T, 8, HALF])
        rstd = sb("rstd", [T, 8, HALF])
        minushalf = sb("minushalf", [T, HALF])
        xn = sb("xn", [T, HALF, D])
        xnT = sb("xnT", [D, NT])
        xh, xl = sb("xh", [D, NT], F32R), sb("xl", [D, NT], F32R)

        brep = sb("brep", [128, BLOCKS, 128])
        cvo = sb("cvo", [128, 128])
        xrep = sb("xrep", [T, BLOCKS * TILES, 4, HD])
        usplit = sb("usplit", [128, 2, NT], F32R)
        ring = sb("ring", [128, 8 * NT], F32R)
        kst = ring[:, 0:BLOCKS * B * S2].rearrange("p (j k) -> p j k", j=BLOCKS)
        xst = sb("xst", [128, 2, BLOCKS, T], F32R)
        vaug = sb("vaug", [S2, B, HEADS, HD + 1])
        negmax = sb("negmax", [T, 4, BLOCKS], BF16)
        probs_buf = sb("probs_buf", [128, 3, BLOCKS * T])
        probT = probs_buf[0:S2, :, :]
        rden = sb("rden", [T, HEADS])
        onorm = sb("onorm", [T, D])
        onT = sb("onT", [D, T])

        lmax = sb("lmax", [T, HALF])
        lshift = sb("lshift", [T, HALF, EXPERTS])
        lexp = sb("lexp", [T, HALF, EXPERTS])
        lsum = sb("lsum", [T, HALF])
        lrec = sb("lrec", [T, HALF])
        probs = sb("probs", [T, HALF, EXPERTS])
        top8 = sb("top8", [T, HALF, 8])
        rest = sb("rest", [T, HALF, EXPERTS])
        gate = sb("gate", [T, HALF, EXPERTS])
        gres = sb("gres", [T, HALF, EXPERTS])
        gparts = sb("gparts", [T, HALF, 3, EXPERTS], BF16)
        gT = sb("gT", [48, NT], BF16)
        shared = sb("shared", [128, 8 * NT])
        gelu = shared[:, 0:2 * NT].rearrange("p (i t) -> p i t", i=2)
        gated = shared[:, 2 * NT:4 * NT].rearrange("p (i t) -> p i t", i=2)
        gsel_f32 = shared[0:48, 0:2 * NT].rearrange("p (c m) -> p c m", c=PAIRS - 1)
        acth = ring[:, 0:4 * NT].rearrange("p (i t) -> p i t", i=4)
        actl = ring[:, 4 * NT:8 * NT].rearrange("p (i t) -> p i t", i=4)
        yT = sb("yT", [D, NT])

        maskf, kT1, vT1, cB = (shared[:, i * B * S2:(i + 1) * B * S2] for i in range(4))
        mscale = sb("mscale", [128, B * S2])
        mneg = maskf
        aK = sb("aK", [128, B * S2])
        cmask = sb("cmask", [128, B * S2])
        vo = ctx_sb
        aexp = probs_buf[:, 0, :].rearrange("t (b k) -> t b k", b=HALF)
        apT = probs_buf[:, 1, :].rearrange("t (b k) -> t b k", b=HALF)
        sc1 = probs_buf[:, 2, 0:NK]
        sc2 = sb("sc2", [T, NK])
        amax = sb("amax", [T, HALF])
        asum = sb("asum", [T, HALF])
        arec = sb("arec", [T, HALF])

        spart = sb("spart", [128, 3, 2, 192], BF16)
        sres = sb("sres", [128, 2, 192])
        scomb = sb("scomb", [128, 2, 192])
        lup = sb("lup", [128, 2, LEAVES, 64], BF16)
        ldown = sb("ldown", [128, 2, 128], BF16)
        nscore = sb("nscore", [T, HALF, NETS * NODES])
        right = sb("right", [T, HALF * NETS, NODES])
        lev = [None, sb("lev1", [T, HALF * NETS, 2]), sb("lev2", [T, HALF * NETS, 4]),
               sb("lev3", [T, HALF * NETS, 8]), sb("lev4", [T, HALF * NETS, 16])]
        selrow = sb("selrow", [T, HALF, 4, 4, LEAVES], BF16)
        selT = sb("selT", [128, 2, NT], BF16)
        qkvT = shared[:, 0:NETS * NT].rearrange("p (n t) -> p n t", n=NETS)
        vnat = shared[:, NETS * NT:(NETS + 1) * NT].rearrange("p (b d) -> p b d", b=HALF)
        dmax = sb("dmax", [T, HALF])

        s_early, s_x, s_ctx, s_mid = sem("early_loaded"), sem("x_loaded"), sem("ctx_loaded"), sem("mid_loaded")
        s_w1, s_w2 = sem("w1_loaded"), sem("w2_loaded")
        s_moe, s_late, s_stored = sem("moe_loaded"), sem("late_loaded"), sem("stored")
        s_consts = sem("consts_bf16")
        s_memset = sem("memset_done")
        s_fold, s_brep, s_cvo = sem("folded"), sem("brep_ready"), sem("cvo_ready")
        s_kraw, s_ksign, s_kst = sem("k_stack_raw"), sem("k_signed"), sem("k_stack")
        s_stats, s_mv, s_ve, s_rstd, s_xn = sem("stats"), sem("meanvar"), sem("vareps"), sem("rstd"), sem("xn")
        s_xrep, s_xraw, s_xsign, s_xst = sem("xrep"), sem("x_stack_raw"), sem("x_signed"), sem("x_stack")
        s_vaug, s_xbo = sem("vaug"), sem("xbo")
        s_sc, s_nm, s_sT, s_p, s_pv = sem("scores"), sem("negmax"), sem("scoresT"), sem("probT"), sem("pv")
        s_rd, s_on, s_onp, s_onT, s_y0, s_x1 = (sem("rden"), sem("onorm"), sem("onT_psum"), sem("onT"),
                                                sem("attn0_out"), sem("x1"))
        s_hi, s_lo = sem("weight_hi"), sem("weight_lo")
        s_tp, s_xnT, s_xh, s_xl = sem("xn_transposed"), sem("xnT"), sem("xh"), sem("xl")
        s_lg, s_lsh, s_lex, s_gstep, s_gp, s_gTp, s_gT = (
            sem("logits"), sem("logits_shifted"), sem("logits_exp"), sem("gate_step"), sem("gate_parts"),
            sem("gateT_psum"), sem("gateT"))
        s_up, s_gb, s_ge, s_ga, s_ah, s_al, s_dn = (
            sem("moe_up"), sem("gate_spread"), sem("gelu"), sem("gated"), sem("act_hi"), sem("act_lo"), sem("moe_down"))
        s_yT, s_yb, s_x2 = sem("moe_yT"), sem("moe_y"), sem("x2")
        s_ck, s_ckr, s_mk = sem("ctx_product"), sem("ctx_product_read"), sem("mask_step")
        s_as, s_am, s_ae, s_apT, s_aT, s_av, s_ar, s_x3 = (
            sem("attn1_scores"), sem("attn1_step"), sem("attn1_exp"), sem("attn1_pT_psum"), sem("attn1_pT"),
            sem("attn1_out"), sem("attn1_rec"), sem("x3"))
        s_lb, s_ns, s_tree, s_selp, s_selT = (
            sem("leaf_bias_step"), sem("node_scores"), sem("tree_step"), sem("selT_psum"), sem("selT"))
        s_fu, s_fh, s_fl, s_fd, s_net, s_vp, s_vn = (
            sem("ffn_up"), sem("ffn_hi"), sem("ffn_lo"), sem("ffn_down"), sem("net_out"), sem("v_psum"), sem("v_nat"))
        s_ds, s_dm, s_de, s_dpT, s_dT, s_do, s_dr, s_out = (
            sem("self_scores"), sem("self_step"), sem("self_exp"), sem("self_pT_psum"), sem("self_pT"),
            sem("self_out"), sem("self_rec"), sem("out_ready"))

        block = stack.enter_context(nc.Block())

        def cols4(t, i, n=T):
            return t[:, i * n:(i + 1) * n]

        @block.sync
        def _(sp):
            sp.dma_start(blockw_sb[:, :, :], blockw).then_inc(s_early, 16)
            sp.dma_start(c_sb[:, :], consts).then_inc(s_early, 16)
            sp.dma_start(ctxT_sb[:, :], ctxT).then_inc(s_early, 16)
            sp.dma_start(woT_sb[:, :], woT).then_inc(s_early, 16)
            sp.dma_start(ctx_sb[:, :, :], ctx.rearrange("b s d -> s b d")).then_inc(s_ctx, 16)
            sp.dma_start(SPLITS[0][0], up0).then_inc(s_moe, 16)
            sp.dma_start(SPLITS[1][0], down0).then_inc(s_moe, 16)
            sp.wait_ge(s_lo, 2)
            sp.dma_start(staged[:, :], w1).then_inc(s_w1, 16)
            sp.wait_ge(s_lo, 3)
            sp.dma_start(staged[:, :], w2).then_inc(s_w2, 16)
            for b in range(B):
                sp.wait_ge(s_out, b + 1)
                sp.dma_start(out[b, :, :], xres[:, b, :]).then_inc(s_stored, 16)
            sp.wait_ge(s_stored, 16 * B)

        @block.gpsimd
        def _(pool):
            pool.memset(minushalf[:, :], -0.5).then_inc(s_memset, 1)
            pool.memset(vaug[:, :, :, HD:HD + 1], 1.0).then_inc(s_memset, 1)
            pool.wait_ge(s_memset, 2)

            def reciprocal_deviation(k):
                pool.wait_ge(s_mv, k + 1)
                pool.tensor_scalar(vareps[:, k, :], meanvar[:, k, :, 1], EPS, None, ALU.add).then_inc(s_ve, 1)
                pool.wait_ge(s_ve, k + 1)
                pool.tensor_tensor(rstd[:, k, :], vareps[:, k, :], minushalf[:, :], ALU.pow).then_inc(s_rstd, 1)

            def weight_lo(k, c0, c1):
                w, hi, lo = SPLITS[k]
                pool.tensor_tensor(lo[:, c0:c1], w[:, c0:c1], hi[:, c0:c1].bitcast(F32), ALU.subtract).then_inc(s_lo, 1)

            reciprocal_deviation(0)
            reciprocal_deviation(1)
            pool.wait_ge(s_early, 16 * 4)
            pool.tensor_copy(idb[:, :], ident).then_inc(s_consts, 1)
            pool.wait_ge(s_ctx, 16)
            for b in range(B):
                pool.tensor_copy(vaug[:, b, :, 0:HD], ctx_sb[:, b, :].rearrange("s (h e) -> s h e", e=HD)).then_inc(s_vaug, 1)
            pool.wait_ge(s_x, 16)
            pool.wait_ge(s_mid, 16 * 6)
            pool.tensor_tensor(xres[:, :, :], x0[:, :, :], rows_sb[:, None, R_BO0:R_BO0 + D].broadcast_to([T, B, D]),
                               ALU.add).then_inc(s_xbo, 1)
            pool.tensor_copy(gsel_sb[:, :, :], gsel_f32).then_inc(s_consts, 1)
            for k in range(2):
                pool.wait_ge(s_hi, k + 1)
                weight_lo(k, 0, PAIRS * 128)
            reciprocal_deviation(2)
            reciprocal_deviation(3)
            for k in range(2, 4):
                pool.wait_ge(s_hi, k + 1)
                weight_lo(k, 0, UPB * 128)
                reciprocal_deviation(2 + k)
            reciprocal_deviation(6)
            reciprocal_deviation(7)

        @block.scalar
        def _(act):
            act.dma_start(x0[:, :, :], x.rearrange("b t d -> t b d")).then_inc(s_x, 16)
            act.dma_start(rows_sb[:, :], rows.broadcast_to([128, R_END])).then_inc(s_mid, 16)
            act.dma_start(router_sb[:, :], router).then_inc(s_mid, 16)
            act.dma_start(attnw_sb[:, :, :], attnw).then_inc(s_mid, 16)
            act.dma_start(cols_sb[:, :], cols).then_inc(s_mid, 16)
            act.dma_start(mask_u8[:, :], mask.broadcast_to([128, B * S2])).then_inc(s_mid, 16)
            act.dma_start(gsel_f32, gsel).then_inc(s_mid, 16)
            act.dma_start(nodew_sb[:, :], nodew).then_inc(s_late, 16)
            act.dma_start(leafb_sb[:, :, :], leafb).then_inc(s_late, 16)

            act.wait_ge(s_early, 16 * 4)
            for m in range(2 * BLOCKS):
                act.wait_ge(s_kraw, m + 1)
                if m >= 2:
                    act.wait_ge(s_kst, m - 1)
                act.activation(usplit[:, m % 2, 0:NK], W4[m % 4][:, 0:NK], ACT.Identity,
                               scale=c_sb[:, C_SK:C_SK + 1]).then_inc(s_ksign, 1)

            def sign_x(b):
                act.wait_ge(s_xraw, b + 1)
                act.wait_ge(s_kst, 2 * BLOCKS)
                if b >= 2:
                    act.wait_ge(s_xst, b - 1)
                act.activation(usplit[:, b % 2, :], T0[:, :], ACT.Identity, scale=c_sb[:, C_SX:C_SX + 1]).then_inc(s_xsign, 1)

            def exp_unit(n):
                act.wait_ge(s_sT, n + 1)
                if n >= 3:
                    act.wait_ge(s_pv, n - 2)
                act.activation(probT[:, n % 3, :], G[n % 2][0:S2, :], ACT.Exp, scale=SCALE).then_inc(s_p, 1)

            def turn_out(b):
                act.wait_ge(s_onp, b + 1)
                if b >= 1:
                    act.wait_ge(s_y0, b)
                act.activation(onT[:, :], T1[:, 0:T], ACT.Copy).then_inc(s_onT, 1)

            sign_x(0)
            for n in range(UNITS):
                b, p = divmod(n, TILES)
                if p == 1 and b + 1 < B:
                    sign_x(b + 1)
                exp_unit(n)
                if p == 1 and b >= 1:
                    turn_out(b - 1)
                if n == 4:
                    act.wait_ge(s_moe, 32)
                    act.activation(up0h[:, :], SPLITS[0][0], ACT.Copy).then_inc(s_hi, 1)
                if n == 8:
                    act.activation(down0h[:, :], SPLITS[1][0], ACT.Copy).then_inc(s_hi, 1)
            turn_out(B - 1)

            def context_products():
                for m, (dst, bias) in enumerate([(kT1, V_BK), (vT1, V_BV), (aK, None), (cB, None)]):
                    for h in range(2):
                        act.wait_ge(s_ck, 2 * m + h + 1)
                        kw = {} if bias is None else {"bias": cols_sb[:, bias:bias + 1]}
                        act.activation(dst[:, h * NK:(h + 1) * NK], W4[(2 * m + h) % 4][:, 0:NK], ACT.Identity,
                                       **kw).then_inc(s_ckr, 1)

            def split_x(k):
                act.wait_ge(s_xnT, k + 1)
                if k == 1:
                    act.wait_ge(s_up, PAIRS)
                if k == 4:
                    act.wait_ge(s_up, 2 * PAIRS)
                if k == 5:
                    act.wait_ge(s_fu, UPB)
                act.activation(xh[:, :], xnT[:, :], ACT.Copy).then_inc(s_xh, 1)

            def moe_pre(h):
                split_x(h)
                act.wait_ge(s_lsh, h + 1)
                if h:
                    act.wait_ge(s_gstep, 17 * h)
                act.activation(lexp[:, :, :], lshift[:, :, :], ACT.Exp).then_inc(s_lex, 1)

            def moe_hi(m):
                c = m % PAIRS
                if c:
                    act.wait_ge(s_ga, m - m // PAIRS)
                else:
                    act.wait_ge(s_ge, m + 1)
                if m >= 4:
                    act.wait_ge(s_dn, m - 3)
                src = gated if c else gelu
                act.activation(acth[:, m % 4, :], src[:, m % 2, :], ACT.Copy).then_inc(s_ah, 1)

            def moe_main(h):
                for c in range(PAIRS):
                    m = PAIRS * h + c
                    act.wait_ge(s_up, m + 1)
                    if m >= 2:
                        act.wait_ge(s_al, m - 1)
                    act.activation(gelu[:, m % 2, :], U[m % 2][:, :], ACT.Gelu).then_inc(s_ge, 1)
                    if c >= 1:
                        moe_hi(m - 1)
                moe_hi(PAIRS * h + PAIRS - 1)
                act.wait_ge(s_dn, PAIRS * (h + 1))
                if h:
                    act.wait_ge(s_yb, h)
                act.activation(yT[:, :], Y[:, :], ACT.Copy).then_inc(s_yT, 1)

            def attn1(h):
                for i in range(HALF):
                    act.wait_ge(s_am, 4 * h + 3)
                    if h:
                        act.wait_ge(s_apT, h)
                    act.activation(aexp[:, i, 0:S2], sc2[:, i * S2:(i + 1) * S2], ACT.Exp, bias=amax[:, i:i + 1],
                                   accum_out=asum[:, i:i + 1]).then_inc(s_ae, 1)
                act.wait_ge(s_apT, h + 1)
                if h:
                    act.wait_ge(s_av, h)
                act.activation(apT[0:S2, :, :].rearrange("p b t -> p (b t)"), T1[0:S2, :], ACT.Copy).then_inc(s_aT, 1)

            def ffn_main(h):
                for c in range(UPB):
                    m = UPB * h + c
                    act.wait_ge(s_fu, m + 1)
                    if m >= 4:
                        act.wait_ge(s_fd, m - 3)
                    act.activation(acth[:, m % 4, :], W4[m % 4][:, :], ACT.Relu).then_inc(s_fh, 1)
                    if c % CHUNKS == 3 and c >= CHUNKS:
                        take_net(3 * h + c // CHUNKS - 1)
                take_net(3 * h + 2)

            def take_net(j):
                act.wait_ge(s_net, j + 1)
                if j % 3 == 0 and j:
                    act.wait_ge(s_ds, j // 3)
                if j % 3 == 2 and j > 2:
                    act.wait_ge(s_vp, j // 3)
                act.activation(qkvT[:, j % 3, :], [Y, Z][j % 2][:, :], ACT.Copy).then_inc(s_vn, 1)

            def self_attn(h):
                for i in range(HALF):
                    act.wait_ge(s_dm, 2 * h + 2)
                    if h:
                        act.wait_ge(s_dpT, h)
                    act.activation(aexp[:, i, :], U[0][:, i * T:(i + 1) * T], ACT.Exp, scale=SCALE, bias=amax[:, i:i + 1],
                                   accum_out=asum[:, i:i + 1]).then_inc(s_de, 1)
                act.wait_ge(s_dpT, h + 1)
                if h:
                    act.wait_ge(s_do, h)
                act.activation(apT[:, :, :].rearrange("p b t -> p (b t)"), T1[:, :], ACT.Copy).then_inc(s_dT, 1)

            act.wait_ge(s_consts, 2)
            context_products()
            moe_pre(0)
            moe_main(0)
            moe_pre(1)
            moe_main(1)
            act.wait_ge(s_w1, 16)
            act.activation(w1h[:, :], staged[:, :], ACT.Copy).then_inc(s_hi, 1)
            attn1(0)
            act.wait_ge(s_w2, 16)
            act.activation(w2h[:, :], staged[:, :], ACT.Copy).then_inc(s_hi, 1)
            attn1(1)
            split_x(4)
            ffn_main(0)
            self_attn(0)
            split_x(5)
            ffn_main(1)
            self_attn(1)

        @block.vector
        def _(dve):
            def ln_stats(k):
                l, h = divmod(k, 2)
                if l == 0:
                    dve.wait_ge(s_x, 16)
                if l == 1:
                    dve.wait_ge(s_x1, HALF * (h + 1))
                if l == 2:
                    dve.wait_ge(s_x2, h + 1)
                if l == 3:
                    dve.wait_ge(s_x3, HALF * (h + 1))
                for i in range(HALF):
                    dve.bn_stats(stats[:, k, i, :], xs[l][:, HALF * h + i, :]).then_inc(s_stats, 1)
                dve.wait_ge(s_stats, HALF * (k + 1))
                for i in range(HALF):
                    last = dve.bn_aggr(meanvar[:, k, i, :], stats[:, k, i, :])
                last.then_inc(s_mv, 1)

            def normalize(k):
                l, h = divmod(k, 2)
                dve.wait_ge(s_rstd, k + 1)
                if k > 2:
                    dve.wait_ge(s_tp, k - 2)
                for i in range(HALF):
                    dve.tensor_scalar(xn[:, i, :], xs[l][:, HALF * h + i, :], meanvar[:, k, i, 0:1], rstd[:, k, i:i + 1],
                                      ALU.subtract, ALU.mult).then_inc(s_xn, 1)

            def take_xnT(k):
                dve.wait_ge(s_tp, k + 1)
                if k:
                    dve.wait_ge(*[None, (s_lg, 1), (s_lg, 2), (s_as, 1), (s_as, 2), (s_ns, 1)][k])
                    if k in (1, 2):
                        dve.wait_ge(s_xl, k)
                    if k == 5:
                        dve.wait_ge(s_xl, 3)
                dve.tensor_copy(xnT[:, :], T0[:, :]).then_inc(s_xnT, 1)

            def xlo(k, n):
                dve.wait_ge(s_xh, n + 1)
                dve.wait_ge(s_xnT, k + 1)
                dve.tensor_tensor(xl[:, :], xnT[:, :], xh[:, :].bitcast(F32), ALU.subtract).then_inc(s_xl, 1)

            ln_stats(0)
            ln_stats(1)
            dve.wait_ge(s_early, 16 * 4)
            dve.wait_ge(s_fold, 2)
            dve.tensor_copy(brep[:, :, :].rearrange("p j (t c e) -> p (j t) c e", t=TILES, c=4),
                            T1[:, 0:D].rearrange("p (g e) -> p g e", e=HD)[:, :, None, :].broadcast_to([128, 16, 4, HD])
                            ).then_inc(s_brep, 1)
            dve.tensor_copy(cvo[:, :], T1[:, D:2 * D]).then_inc(s_cvo, 1)
            for m in range(2 * BLOCKS):
                h, j = divmod(m, BLOCKS)
                dve.wait_ge(s_ksign, m + 1)
                dve.scalar_tensor_tensor(kst[:, j, h * NK:(h + 1) * NK], W4[m % 4][:, 0:NK], c_sb[:, C_BK:C_BK + 1],
                                         usplit[:, m % 2, 0:NK].bitcast(F32), ALU.mult, ALU.add).then_inc(s_kst, 1)

            def repeat_x(b):
                k, i = divmod(b, HALF)
                dve.wait_ge(s_rstd, k + 1)
                if b:
                    dve.wait_ge(s_xraw, b)
                dve.tensor_scalar(xrep[:, :, :, :],
                                  x0[:, b, :].rearrange("t (g e) -> t g e", e=HD)[:, :, None, :].broadcast_to([T, 16, 4, HD]),
                                  meanvar[:, k, i, 0:1], rstd[:, k, i:i + 1], ALU.subtract, ALU.mult).then_inc(s_xrep, 1)

            def stack_x(b):
                dve.wait_ge(s_xsign, b + 1)
                if b >= 2:
                    dve.wait_ge(s_sT, 4 * b - 4)
                dve.scalar_tensor_tensor(xst[:, b % 2, :, :].rearrange("p j t -> p (j t)"), T0[:, :],
                                         c_sb[:, C_BX:C_BX + 1], usplit[:, b % 2, :].bitcast(F32), ALU.mult, ALU.add
                                         ).then_inc(s_xst, 1)

            def max_unit(n):
                dve.wait_ge(s_sc, n + 1)
                if n >= 4:
                    dve.wait_ge(s_sT, n - 3)
                dve.tensor_reduce(negmax[:, n % 4, :], U[n % 2][:, 0:BLOCKS * S2].rearrange("t (j k) -> t j k", k=S2),
                                  AX.X, ALU.max, negate=True).then_inc(s_nm, 1)

            def normalize_out(b):
                O = [Y, Z][b % 2][:, 0:HEADS * (HD + 1)].rearrange("t (h e) -> t h e", e=HD + 1)
                dve.wait_ge(s_pv, TILES * (b + 1))
                dve.reciprocal(rden[:, :], O[:, :, HD]).then_inc(s_rd, 1)
                dve.wait_ge(s_rd, b + 1)
                if b:
                    dve.wait_ge(s_onp, b)
                dve.tensor_tensor(onorm[:, :].rearrange("t (h e) -> t h e", e=HD), O[:, :, 0:HD],
                                  rden[:, :, None].broadcast_to([T, HEADS, HD]), ALU.mult).then_inc(s_on, 1)

            def add_x1(b):
                dve.wait_ge(s_y0, b + 1)
                dve.wait_ge(s_xbo, 1)
                dve.tensor_tensor(xs[1][:, b, :], T1[:, D:2 * D], xres[:, b, :], ALU.add).then_inc(s_x1, 1)

            repeat_x(0)
            stack_x(0)
            for n in range(UNITS):
                b, p = divmod(n, TILES)
                max_unit(n)
                if p == 0:
                    if b + 1 < B:
                        repeat_x(b + 1)
                    if b:
                        normalize_out(b - 1)
                if p == 2 and b + 1 < B:
                    stack_x(b + 1)
                if p == 3 and b:
                    add_x1(b - 1)
            normalize_out(B - 1)
            add_x1(B - 1)

            dve.wait_ge(s_mid, 16 * 6)
            dve.wait_ge(s_consts, 2)
            dve.tensor_copy(maskf[:, :], mask_u8[:, :]).then_inc(s_mk, 1)
            dve.wait_ge(s_mk, 1)
            dve.tensor_scalar(mscale[:, :], maskf[:, :], SCALE, None, ALU.mult).then_inc(s_mk, 1)
            dve.tensor_scalar(mneg[:, :], maskf[:, :], -NEG, NEG, ALU.mult, ALU.add).then_inc(s_mk, 1)
            dve.wait_ge(s_ckr, 8)
            dve.wait_ge(s_mk, 3)
            dve.tensor_tensor(cmask[:, :], cB[:, :], mscale[:, :], ALU.mult).then_inc(s_mk, 1)
            dve.wait_ge(s_mk, 4)
            dve.tensor_tensor(cmask[:, :], cmask[:, :], mneg[:, :], ALU.add).then_inc(s_mk, 1)
            for h in range(2):
                dve.wait_ge(s_ck, 9 + h)
                dve.tensor_tensor(vo[:, HALF * h:HALF * (h + 1), :],
                                  T1[0:S2, :].rearrange("s (b d) -> s b d", d=D),
                                  rows_sb[0:S2, None, R_BO1:R_BO1 + D].broadcast_to([S2, HALF, D]), ALU.add
                                  ).then_inc(s_ckr, 1)

            def moe_pre(h):
                ln_stats(2 + h)
                normalize(2 + h)
                take_xnT(h)
                g0 = 17 * h
                dve.wait_ge(s_lg, h + 1)
                L = T1[:, 0:HALF * EXPERTS].rearrange("t (b e) -> t b e", e=EXPERTS)
                dve.tensor_reduce(lmax[:, :], L, AX.X, ALU.max).then_inc(s_gstep, 1)
                dve.wait_ge(s_gstep, g0 + 1)
                if h:
                    dve.wait_ge(s_lex, h)
                dve.tensor_tensor(lshift[:, :, :], L, lmax[:, :, None].broadcast_to([T, HALF, EXPERTS]), ALU.subtract
                                  ).then_inc(s_lsh, 1)
                xlo(h, h)
                dve.wait_ge(s_lex, h + 1)
                dve.tensor_reduce(lsum[:, :], lexp[:, :, :], AX.X, ALU.add).then_inc(s_gstep, 1)
                dve.wait_ge(s_gstep, g0 + 2)
                dve.reciprocal(lrec[:, :], lsum[:, :]).then_inc(s_gstep, 1)
                dve.wait_ge(s_gstep, g0 + 3)
                dve.tensor_tensor(probs[:, :, :], lexp[:, :, :], lrec[:, :, None].broadcast_to([T, HALF, EXPERTS]), ALU.mult
                                  ).then_inc(s_gstep, 1)
                dve.wait_ge(s_gstep, g0 + 4)
                for i in range(HALF):
                    dve.max(top8[:, i, :], probs[:, i, :]).then_inc(s_gstep, 1)
                dve.wait_ge(s_gstep, g0 + 8)
                dve.memset(top8[:, :, TOPK:8], -1.0).then_inc(s_gstep, 1)
                dve.wait_ge(s_gstep, g0 + 9)
                for i in range(HALF):
                    dve.match_replace(rest[:, i, :], top8[:, i, :], probs[:, i, :], 0.0).then_inc(s_gstep, 1)
                dve.wait_ge(s_gstep, g0 + 13)
                dve.tensor_tensor(gate[:, :, :], probs[:, :, :], rest[:, :, :], ALU.subtract).then_inc(s_gstep, 1)
                dve.wait_ge(s_gstep, g0 + 14)
                if h:
                    dve.wait_ge(s_gTp, h)
                dve.tensor_copy(gparts[:, :, 0, :], gate[:, :, :]).then_inc(s_gstep, 1)
                dve.wait_ge(s_gstep, g0 + 15)
                dve.tensor_tensor(gres[:, :, :], gate[:, :, :], gparts[:, :, 0, :], ALU.subtract).then_inc(s_gstep, 1)
                dve.wait_ge(s_gstep, g0 + 16)
                dve.tensor_copy(gparts[:, :, 1, :], gres[:, :, :]).then_inc(s_gstep, 1)
                dve.wait_ge(s_gstep, g0 + 17)
                dve.tensor_tensor(gparts[:, :, 2, :], gres[:, :, :], gparts[:, :, 1, :], ALU.subtract).then_inc(s_gp, 1)
                dve.wait_ge(s_gTp, h + 1)
                if h:
                    dve.wait_ge(s_gb, 8 * h)
                dve.tensor_copy(gT[:, :], T1[0:48, :].bitcast(BF16)[:, 0:NT]).then_inc(s_gT, 1)

            def moe_main(h):
                for c in range(PAIRS):
                    m = PAIRS * h + c
                    r = m - m // PAIRS - 1
                    dve.wait_ge(s_ge, m + 1)
                    if c:
                        dve.wait_ge(s_gb, r + 1)
                        if m >= 2:
                            dve.wait_ge(s_ah, m - 1)
                            dve.wait_ge(s_al, m - 1)
                        dve.tensor_tensor(gated[:, m % 2, :], gelu[:, m % 2, :], G[r % 2][:, :], ALU.mult).then_inc(s_ga, 1)
                        dve.wait_ge(s_ga, r + 1)
                    dve.wait_ge(s_ah, m + 1)
                    if m >= 4:
                        dve.wait_ge(s_dn, m - 3)
                    src = gated if c else gelu
                    dve.tensor_tensor(actl[:, m % 4, :], src[:, m % 2, :], acth[:, m % 4, :].bitcast(F32), ALU.subtract
                                      ).then_inc(s_al, 1)
                dve.wait_ge(s_yb, h + 1)
                dve.tensor_tensor(xs[2][:, HALF * h:HALF * (h + 1), :].rearrange("t b d -> t (b d)"), Z[:, :],
                                  xs[1][:, HALF * h:HALF * (h + 1), :].rearrange("t b d -> t (b d)"), ALU.add
                                  ).then_inc(s_x2, 1)

            def attn1(h):
                ln_stats(4 + h)
                normalize(4 + h)
                take_xnT(2 + h)
                dve.wait_ge(s_as, h + 1)
                if h:
                    dve.wait_ge(s_am, 4 * h - 1)
                dve.wait_ge(s_mk, 5)
                dve.tensor_tensor(sc1[:, :], U[0][:, 0:NK], mscale[:, h * NK:(h + 1) * NK], ALU.mult).then_inc(s_am, 1)
                dve.wait_ge(s_am, 4 * h + 1)
                if h:
                    dve.wait_ge(s_ae, HALF * h)
                dve.tensor_tensor(sc2[:, :], sc1[:, :], cmask[:, h * NK:(h + 1) * NK], ALU.add).then_inc(s_am, 1)
                dve.wait_ge(s_am, 4 * h + 2)
                dve.tensor_reduce(amax[:, :], sc2[:, :].rearrange("t (b k) -> t b k", k=S2), AX.X, ALU.max, negate=True
                                  ).then_inc(s_am, 1)
                dve.wait_ge(s_ae, HALF * (h + 1))
                if h:
                    dve.wait_ge(s_x3, HALF * h)
                dve.reciprocal(arec[:, :], asum[:, :]).then_inc(s_am, 1)
                dve.wait_ge(s_am, 4 * h + 4)
                dve.wait_ge(s_av, h + 1)
                for i in range(HALF):
                    b = HALF * h + i
                    dve.scalar_tensor_tensor(xs[3][:, b, :], Z[:, i * T:(i + 1) * T], arec[:, i:i + 1], xs[2][:, b, :],
                                             ALU.mult, ALU.add).then_inc(s_x3, 1)

            def leaf_bias():
                dve.wait_ge(s_late, 32)
                dve.tensor_copy(spart[:, 0, :, :], leafb_sb[:, :, :]).then_inc(s_lb, 1)
                dve.wait_ge(s_lb, 1)
                dve.tensor_tensor(sres[:, :, :], leafb_sb[:, :, :], spart[:, 0, :, :], ALU.subtract).then_inc(s_lb, 1)
                dve.wait_ge(s_lb, 2)
                dve.tensor_copy(spart[:, 1, :, :], sres[:, :, :]).then_inc(s_lb, 1)
                dve.wait_ge(s_lb, 3)
                dve.tensor_tensor(spart[:, 2, :, :], sres[:, :, :], spart[:, 1, :, :], ALU.subtract).then_inc(s_lb, 1)
                dve.tensor_scalar(scomb[:, :, :], spart[:, 0, :, :], c_sb[:, C_PART:C_PART + 1], None, ALU.mult).then_inc(s_lb, 1)
                for s in (1, 2):
                    dve.wait_ge(s_lb, 4 + s)
                    dve.scalar_tensor_tensor(scomb[:, :, :].rearrange("p a n -> p (a n)"),
                                             spart[:, s, :, :].rearrange("p a n -> p (a n)"), c_sb[:, C_PART + s:C_PART + s + 1],
                                             scomb[:, :, :].rearrange("p a n -> p (a n)"), ALU.mult, ALU.add).then_inc(s_lb, 1)
                dve.wait_ge(s_lb, 7)
                dve.tensor_copy(ldown[:, :, :], scomb[:, :, 64:192]).then_inc(s_lb, 1)
                for a in range(2):
                    dve.tensor_tensor(lup[:, a, :, :], scomb[:, a, None, 0:64].broadcast_to([128, LEAVES, 64]),
                                      c_sb[:, C_LEAF:C_LEAF + LEAVES, None].broadcast_to([128, LEAVES, 64]), ALU.mult
                                      ).then_inc(s_lb, 1)

            def route(h):
                t0 = 11 * h
                dve.wait_ge(s_ns, h + 1)
                dve.tensor_tensor(nscore[:, :, :], T1[:, 0:HALF * NETS * NODES].rearrange("t (b n) -> t b n", b=HALF),
                                  rows_sb[:, None, R_NB:R_NB + NETS * NODES].broadcast_to([T, HALF, NETS * NODES]), ALU.add
                                  ).then_inc(s_tree, 1)
                dve.wait_ge(s_tree, t0 + 1)
                dve.tensor_scalar(right[:, :, :].rearrange("t g n -> t (g n)"), nscore[:, :, :].rearrange("t b n -> t (b n)"),
                                  0.0, None, ALU.is_ge).then_inc(s_tree, 1)
                dve.wait_ge(s_tree, t0 + 2)
                dve.tensor_copy(lev[1][:, :, 1], right[:, :, 0]).then_inc(s_tree, 1)
                dve.tensor_scalar(lev[1][:, :, 0], right[:, :, 0], -1.0, 1.0, ALU.mult, ALU.add).then_inc(s_tree, 1)
                for d in range(1, 4):
                    n = 2 ** d
                    dve.wait_ge(s_tree, t0 + 2 + 2 * d)
                    kids = lev[d + 1][:, :, :].rearrange("t g (n two) -> t g n two", two=2)
                    dve.tensor_tensor(kids[:, :, :, 1], lev[d][:, :, :], right[:, :, n - 1:2 * n - 1], ALU.mult).then_inc(s_tree, 1)
                    dve.wait_ge(s_tree, t0 + 3 + 2 * d)
                    dve.tensor_tensor(kids[:, :, :, 0], lev[d][:, :, :], kids[:, :, :, 1], ALU.subtract).then_inc(s_tree, 1)
                dve.wait_ge(s_tree, t0 + 10)
                leaf = lev[4][:, :, :].rearrange("t (b n) l -> t b n l", b=HALF)
                if h == 0:
                    dve.memset(selrow[:, :, 3, :, :], 0.0).then_inc(s_memset, 1)
                else:
                    dve.wait_ge(s_selp, h)
                dve.tensor_scalar(selrow[:, :, 0:3, 0, :], leaf, -1.0, 1.0, ALU.mult, ALU.add).then_inc(s_tree, 1)
                for s in (1, 2, 3):
                    last = dve.tensor_copy(selrow[:, :, 0:3, s, :], leaf)
                last.then_inc(s_gp, 1)
                dve.wait_ge(s_selp, h + 1)
                if h:
                    dve.wait_ge(s_net, NETS * h)
                dve.tensor_copy(selT[:, :, :], T1[:, :].bitcast(BF16).rearrange("p (a t) -> p a t", a=2)).then_inc(s_selT, 1)

            def ffn_pre(h):
                ln_stats(6 + h)
                normalize(6 + h)
                take_xnT(4 + h)
                xlo(4 + h, 2 + h)
                route(h)

            def ffn_main(h):
                for c in range(UPB):
                    m = UPB * h + c
                    dve.wait_ge(s_fh, m + 1)
                    if m >= 4:
                        dve.wait_ge(s_fd, m - 3)
                    dve.scalar_tensor_tensor(actl[:, m % 4, :], W4[m % 4][:, :], 0.0, acth[:, m % 4, :].bitcast(F32),
                                             ALU.max, ALU.subtract).then_inc(s_fl, 1)

            def self_attn(h):
                dve.wait_ge(s_vp, h + 1)
                if h:
                    dve.wait_ge(s_do, h)
                dve.tensor_copy(vnat[:, :, :].rearrange("t b d -> t (b d)"), T0[:, :]).then_inc(s_dr, 1)
                dve.wait_ge(s_ds, h + 1)
                dve.tensor_reduce(dmax[:, :], U[0][:, :].rearrange("t (b k) -> t b k", k=T), AX.X, ALU.max).then_inc(s_dm, 1)
                dve.wait_ge(s_dm, 2 * h + 1)
                dve.tensor_scalar(amax[:, :], dmax[:, :], -SCALE, None, ALU.mult).then_inc(s_dm, 1)
                dve.wait_ge(s_de, HALF * (h + 1))
                dve.reciprocal(arec[:, :], asum[:, :]).then_inc(s_ar, 1)
                dve.wait_ge(s_ar, h + 1)
                dve.wait_ge(s_do, h + 1)
                for i in range(HALF):
                    b = HALF * h + i
                    dve.scalar_tensor_tensor(xres[:, b, :], Z[:, i * T:(i + 1) * T], arec[:, i:i + 1], xs[3][:, b, :],
                                             ALU.mult, ALU.add).then_inc(s_out, 1)

            moe_pre(0)
            moe_main(0)
            moe_pre(1)
            moe_main(1)
            attn1(0)
            attn1(1)
            leaf_bias()
            ffn_pre(0)
            ffn_main(0)
            self_attn(0)
            ffn_pre(1)
            ffn_main(1)
            self_attn(1)

        @block.tensor
        def _(pe):
            def split_product(dst, lo_hi_w, lo_hi_x, w_cols, first, last):
                (wh, wl), (xhi, xlo_) = lo_hi_w, lo_hi_x
                pe.matmul(dst, wl[:, w_cols], xhi, start=first, stop=False)
                pe.matmul(dst, wh[:, w_cols], xlo_, start=False, stop=False)
                return pe.matmul(dst, wh[:, w_cols], xhi, start=False, stop=last)

            pe.wait_ge(s_early, 16 * 4)
            pe.matmul(T1[:, 0:D], blockw_sb[:, 1, :], blockw_sb[:, 0, :], start=True, stop=True).then_inc(s_fold, 1)
            pe.matmul(T1[:, D:2 * D], blockw_sb[:, 2, :], woT_sb[:, :], start=True, stop=True).then_inc(s_fold, 1)
            pe.wait_ge(s_brep, 1)
            for m in range(2 * BLOCKS):
                h, j = divmod(m, BLOCKS)
                if m >= 4:
                    pe.wait_ge(s_kst, m - 3)
                pe.matmul(W4[m % 4][:, 0:NK], brep[:, j, :], ctxT_sb[:, h * NK:(h + 1) * NK], start=True, stop=True
                          ).then_inc(s_kraw, 1)

            def turn_x(b):
                pe.wait_ge(s_xrep, b + 1)
                if b:
                    pe.wait_ge(s_xst, b)
                rep = xrep[:, :, :, :].rearrange("t g c e -> t (g c e)")
                for j in range(BLOCKS):
                    last = pe.transpose(T0[:, j * T:(j + 1) * T], rep[:, j * 128:(j + 1) * 128], ident)
                last.then_inc(s_xraw, 1)

            def keys(p, j, b):
                return kst[32 * p:32 * p + 32, j, b * S2:(b + 1) * S2]

            def queries(p, j, b):
                return xst[32 * p:32 * p + 32, b % 2, j, :]

            def scores(n):
                b, p = divmod(n, TILES)
                pe.wait_ge(s_xst, b + 1)
                pe.wait_ge(s_kst, 2 * BLOCKS)
                if n >= 2:
                    pe.wait_ge(s_nm, n - 1)
                for j in range(BLOCKS):
                    last = pe.matmul(U[n % 2][:, j * S2:(j + 1) * S2], queries(p, j, b), keys(p, j, b), start=True, stop=True,
                                     tile_position=(32 * p, 0))
                last.then_inc(s_sc, 1)

            def scoresT(n):
                b, p = divmod(n, TILES)
                pe.wait_ge(s_nm, n + 1)
                if n >= 2:
                    pe.wait_ge(s_p, n - 1)
                for j in range(BLOCKS):
                    pe.matmul(G[n % 2][0:S2, j * T:(j + 1) * T], negmax[:, n % 4, j:j + 1].broadcast_to([T, S2]), idb[:, :],
                              start=(j == 0), stop=False, skip_group_check=True)
                for j in range(BLOCKS):
                    last = pe.matmul(G[n % 2][0:S2, j * T:(j + 1) * T], keys(p, j, b), queries(p, j, b),
                                     start=False, stop=True, tile_position=(32 * p, 0), skip_group_check=True)
                last.then_inc(s_sT, 1)

            def values(n):
                b, p = divmod(n, TILES)
                pe.wait_ge(s_p, n + 1)
                if n == 0:
                    pe.wait_ge(s_vaug, B)
                if p == 0 and b >= 2:
                    pe.wait_ge(s_on, b - 1)
                for j in range(BLOCKS):
                    h = BLOCKS * j + p
                    last = pe.matmul([Y, Z][b % 2][:, h * (HD + 1):(h + 1) * (HD + 1)], probT[:, n % 3, j * T:(j + 1) * T],
                                     vaug[:, b, h, :], start=True, stop=True)
                last.then_inc(s_pv, 1)

            def turn_out(b):
                pe.wait_ge(s_on, b + 1)
                if b:
                    pe.wait_ge(s_x1, b)
                pe.transpose(T1[:, 0:T], onorm[:, :], ident).then_inc(s_onp, 1)

            def project_out(b):
                pe.wait_ge(s_onT, b + 1)
                pe.matmul(T1[:, D:2 * D], onT[:, :], cvo[:, :], start=True, stop=True).then_inc(s_y0, 1)

            turn_x(0)
            scores(0)
            pe.wait_ge(s_cvo, 1)
            pe.wait_ge(s_consts, 1)
            for n in range(UNITS):
                b, p = divmod(n, TILES)
                if p == 1 and b + 1 < B:
                    turn_x(b + 1)
                if n + 1 < UNITS:
                    scores(n + 1)
                scoresT(n)
                if n:
                    values(n - 1)
                if p == 1 and b:
                    turn_out(b - 1)
                if p == 2 and b:
                    project_out(b - 1)
            values(UNITS - 1)
            turn_out(B - 1)
            project_out(B - 1)

            pe.wait_ge(s_mid, 16 * 6)
            pe.wait_ge(s_nm, UNITS)
            pe.wait_ge(s_p, UNITS)

            def context_product(m, h, lhsT, rhs):
                if m >= 2:
                    pe.wait_ge(s_ckr, 2 * m + h - 3)
                pe.matmul(W4[(2 * m + h) % 4][:, 0:NK], lhsT, rhs[:, h * NK:(h + 1) * NK], start=True, stop=True
                          ).then_inc(s_ck, 1)

            for h in range(2):
                context_product(0, h, attnw_sb[:, 1, :], ctxT_sb)
            for h in range(2):
                context_product(1, h, attnw_sb[:, 2, :], ctxT_sb)
            pe.wait_ge(s_ckr, 2)
            for h in range(2):
                context_product(2, h, attnw_sb[:, 0, :], kT1)
            for h in range(2):
                context_product(3, h, cols_sb[:, V_BQ:V_BQ + 1].broadcast_to([128, 128]), kT1)
            pe.wait_ge(s_x1, B)
            for h in range(2):
                if h:
                    pe.wait_ge(s_ckr, 9)
                for i in range(HALF):
                    b = HALF * h + i
                    last = pe.matmul(T1[0:S2, i * D:(i + 1) * D], vT1[:, b * S2:(b + 1) * S2], attnw_sb[:, 3, :],
                                     start=True, stop=True)
                last.then_inc(s_ck, 1)

            def turn_xn(k):
                pe.wait_ge(s_xn, HALF * (k + 1))
                if k:
                    pe.wait_ge(s_xnT, k)
                else:
                    pe.wait_ge(s_xst, B)
                for i in range(HALF):
                    last = pe.transpose(T0[:, i * T:(i + 1) * T], xn[:, i, :], ident)
                last.then_inc(s_tp, 1)

            def moe_pre(h):
                turn_xn(h)
                pe.wait_ge(s_xnT, h + 1)
                if h:
                    pe.wait_ge(s_gT, h)
                else:
                    pe.wait_ge(s_ckr, 10)
                for i in range(HALF):
                    last = pe.matmul(T1[:, i * EXPERTS:(i + 1) * EXPERTS], xnT[:, i * T:(i + 1) * T], router_sb[:, :],
                                     start=True, stop=True)
                last.then_inc(s_lg, 1)

            def gateT(h):
                pe.wait_ge(s_gp, h + 1)
                for i in range(HALF):
                    last = pe.transpose(T1[0:48, :].bitcast(BF16)[:, i * T:(i + 1) * T],
                                        gparts[:, i, :, :].rearrange("t s e -> t (s e)"), idb[:, :])
                last.then_inc(s_gTp, 1)

            def moe_up(m):
                c = m % PAIRS
                if m >= 2:
                    pe.wait_ge(s_ge, m - 1)
                split_product(U[m % 2][:, :], (up0h, up0l), (xh[:, :], xl[:, :]), slice(c * 128, (c + 1) * 128), True, True
                              ).then_inc(s_up, 1)

            def moe_gate(m):
                r = m - m // PAIRS - 1
                if r >= 2:
                    pe.wait_ge(s_ga, r - 1)
                pe.matmul(G[r % 2][:, :], gsel_sb[:, m % PAIRS - 1, :], gT[:, :], start=True, stop=True).then_inc(s_gb, 1)

            def moe_down(m):
                h, c = divmod(m, PAIRS)
                pe.wait_ge(s_al, m + 1)
                if c == 0:
                    if h:
                        pe.wait_ge(s_yT, h)
                split_product(Y[:, :], (down0h, down0l), (acth[:, m % 4, :], actl[:, m % 4, :]),
                              slice(c * 128, (c + 1) * 128), c == 0, c == PAIRS - 1).then_inc(s_dn, 1)

            def moe_main(h):
                pe.wait_ge(s_xl, h + 1)
                if h == 0:
                    pe.wait_ge(s_lo, 2)
                    pe.wait_ge(s_ckr, 8)
                for c in range(PAIRS + 2):
                    m = PAIRS * h + c
                    if c < PAIRS:
                        moe_up(m)
                        if c == 1:
                            gateT(h)
                            pe.wait_ge(s_gT, h + 1)
                        if c:
                            moe_gate(m)
                    if c >= 2:
                        moe_down(m - 2)
                pe.wait_ge(s_yT, h + 1)
                if h:
                    pe.wait_ge(s_x2, h)
                for i in range(HALF):
                    last = pe.transpose(Z[:, i * T:(i + 1) * T], yT[:, i * T:(i + 1) * T], ident)
                last.then_inc(s_yb, 1)

            def attn1(h):
                turn_xn(2 + h)
                pe.wait_ge(s_xnT, 3 + h)
                if h:
                    pe.wait_ge(s_am, 4 * h - 3)
                else:
                    pe.wait_ge(s_ge, 2 * PAIRS)
                for i in range(HALF):
                    b = HALF * h + i
                    last = pe.matmul(U[0][:, i * S2:(i + 1) * S2], xnT[:, i * T:(i + 1) * T], aK[:, b * S2:(b + 1) * S2],
                                     start=True, stop=True)
                last.then_inc(s_as, 1)
                pe.wait_ge(s_ae, HALF * (h + 1))
                if h:
                    pe.wait_ge(s_aT, h)
                for i in range(HALF):
                    last = pe.transpose(T1[0:S2, i * T:(i + 1) * T], aexp[:, i, 0:S2], ident)
                last.then_inc(s_apT, 1)
                pe.wait_ge(s_aT, h + 1)
                if h:
                    pe.wait_ge(s_x3, HALF * h)
                else:
                    pe.wait_ge(s_x2, 2)
                for i in range(HALF):
                    b = HALF * h + i
                    last = pe.matmul(Z[:, i * T:(i + 1) * T], apT[0:S2, i, :], vo[:, b, :], start=True, stop=True)
                last.then_inc(s_av, 1)

            def ffn_pre(h):
                turn_xn(4 + h)
                pe.wait_ge(s_xnT, 5 + h)
                pe.wait_ge(s_late, 32)
                if h:
                    pe.wait_ge(s_dT, h)
                else:
                    pe.wait_ge(s_aT, 2)
                for i in range(HALF):
                    last = pe.matmul(T1[:, i * NETS * NODES:(i + 1) * NETS * NODES], xnT[:, i * T:(i + 1) * T],
                                     nodew_sb[:, :], start=True, stop=True)
                last.then_inc(s_ns, 1)
                pe.wait_ge(s_gp, 3 + h)
                if h == 0:
                    pe.wait_ge(s_memset, 3)
                for a in range(2):
                    for i in range(HALF):
                        last = pe.transpose(T1[:, :].bitcast(BF16)[:, a * NT + i * T:a * NT + (i + 1) * T],
                                            selrow[:, i, 2 * a:2 * a + 2, :, :].rearrange("t n s l -> t (n s l)"), idb[:, :])
                last.then_inc(s_selp, 1)

            def net_rows(net):
                return slice(SEL * (net % 2), SEL * (net % 2) + SEL), net // 2

            def ffn_up(m):
                net, c = divmod(m % UPB, CHUNKS)
                rows_, a = net_rows(net)
                if m >= 4:
                    pe.wait_ge(s_fl, m - 3)
                w = slice((m % UPB) * 128, (m % UPB + 1) * 128)
                split_product(W4[m % 4][:, :], (w1h, w1l), (xh[:, :], xl[:, :]), w, True, False)
                pe.matmul(W4[m % 4][:, :], lup[rows_, a, 2 * c:2 * c + 2, :].rearrange("r l e -> r (l e)"), selT[rows_, a, :],
                          start=False, stop=True).then_inc(s_fu, 1)

            def ffn_down(m):
                h, k = divmod(m, UPB)
                net, c = divmod(k, CHUNKS)
                j = NETS * h + net
                acc = [Y, Z][j % 2]
                rows_, a = net_rows(net)
                pe.wait_ge(s_fl, m + 1)
                if c == 0 and j >= 2:
                    pe.wait_ge(s_vn, j - 1)
                if j % 2 and c == 0 and j > 1 and h:
                    pe.wait_ge(s_out, HALF * h)
                split_product(acc[:, :], (w2h, w2l), (acth[:, m % 4, :], actl[:, m % 4, :]), slice(k * 128, (k + 1) * 128),
                              c == 0, False).then_inc(s_fd, 1)
                if c == CHUNKS - 1:
                    pe.matmul(acc[:, :], ldown[rows_, a, :], selT[rows_, a, :], start=False, stop=True).then_inc(s_net, 1)

            def ffn_main(h):
                pe.wait_ge(s_xl, 3 + h)
                pe.wait_ge(s_selT, h + 1)
                if h == 0:
                    pe.wait_ge(s_lo, 4)
                    pe.wait_ge(s_lb, 10)
                    pe.wait_ge(s_am, 5)
                    pe.wait_ge(s_x3, B)
                else:
                    pe.wait_ge(s_de, HALF * h)
                for k in range(UPB + 2):
                    m = UPB * h + k
                    if k < UPB:
                        ffn_up(m)
                    if k >= 2:
                        ffn_down(m - 2)

            def self_attn(h):
                pe.wait_ge(s_vn, NETS * (h + 1))
                pe.wait_ge(s_xnT, 5 + h)
                for i in range(HALF):
                    last = pe.transpose(T0[:, i * T:(i + 1) * T], qkvT[:, 2, i * T:(i + 1) * T], ident)
                last.then_inc(s_vp, 1)
                for i in range(HALF):
                    last = pe.matmul(U[0][:, i * T:(i + 1) * T], qkvT[:, 0, i * T:(i + 1) * T], qkvT[:, 1, i * T:(i + 1) * T],
                                     start=True, stop=True)
                last.then_inc(s_ds, 1)
                pe.wait_ge(s_de, HALF * (h + 1))
                pe.wait_ge(s_selT, h + 1)
                for i in range(HALF):
                    last = pe.transpose(T1[:, i * T:(i + 1) * T], aexp[:, i, :], ident)
                last.then_inc(s_dpT, 1)
                pe.wait_ge(s_dT, h + 1)
                pe.wait_ge(s_dr, h + 1)
                for i in range(HALF):
                    last = pe.matmul(Z[:, i * T:(i + 1) * T], apT[:, i, :], vnat[:, i, :], start=True, stop=True)
                last.then_inc(s_do, 1)

            moe_pre(0)
            moe_main(0)
            moe_pre(1)
            moe_main(1)
            attn1(0)
            attn1(1)
            ffn_pre(0)
            ffn_main(0)
            self_attn(0)
            ffn_pre(1)
            ffn_main(1)
            self_attn(1)


def _constants():
    import numpy as np
    row = np.arange(128)
    kind = (row // HD) % 4
    c = np.zeros((128, C_END), np.float32)
    c[:, C_ID:C_ID + 128] = np.eye(128)
    x_lo, k_lo = kind >= 2, kind % 2 == 1
    c[:, C_SX], c[:, C_BX] = np.where(x_lo, -1, 1), x_lo
    c[:, C_SK], c[:, C_BK] = np.where(k_lo, -1, 1), k_lo
    group = (row % SEL) // LEAVES
    c[:, C_PART] = group <= 1
    c[:, C_PART + 1] = group == 2
    c[:, C_PART + 2] = group == 3
    c[:, C_LEAF:C_LEAF + LEAVES] = (row % LEAVES)[:, None] == np.arange(LEAVES)[None, :]
    g = np.zeros((48, PAIRS - 1, 2, 64), np.float32)
    for e in range(EXPERTS):
        g[e::EXPERTS, e // 2, e % 2, :] = 1
    return c, g.reshape(48, PAIRS - 1, 128)


def _layout(a):
    import numpy as np
    f = {n: np.asarray(v) for n, v in a.items()}
    consts, gsel = _constants()
    blockw = np.zeros((128, 3, 128), np.float32)
    for h in range(HEADS):
        s = slice(h * HD, (h + 1) * HD)
        for k, n in enumerate(("Wq", "Wk", "Wv")):
            blockw[s, k, s] = f["L0_xattn_" + n]
    up = np.concatenate([f["L0_ffn_shared_up"], f["L0_ffn_routed_up"]])
    down = np.concatenate([f["L0_ffn_shared_down"], f["L0_ffn_routed_down"]])
    w1 = np.stack([f[f"L1_ffn_{n}_w1"] for n in "qkv"])
    w2 = np.stack([f[f"L1_ffn_{n}_w2"] for n in "qkv"])
    leafb = np.zeros((4, 4, LEAVES, 192), np.float32)
    leafb[:, 0, :, 0:64] = -BIG
    for j, n in enumerate("qkv"):
        leafb[j, 1:, :, 0:64] = f[f"L1_ffn_{n}_b1"]
        leafb[j, 1:, :, 64:] = f[f"L1_ffn_{n}_b2"]
    arrays = {
        "x": f["x"], "ctx": f["ctx_1024"],
        "ctxT": f["ctx_1024"].transpose(2, 0, 1).reshape(D, B * S2),
        "mask": f["mask_BxS2_bk0"].reshape(1, B * S2),
        "consts": consts, "gsel": gsel, "blockw": blockw,
        "woT": f["L0_xattn_Wo"].T,
        "up0": up.transpose(2, 0, 1).reshape(D, PAIRS * 128),
        "down0": down.transpose(0, 2, 1).reshape(PAIRS, 128, D).transpose(1, 0, 2).reshape(128, PAIRS * D),
        "router": f["L0_ffn_router_w"].T,
        "attnw": np.stack([f["L1_xattn_Wq"].T, f["L1_xattn_Wk"], f["L1_xattn_Wv"], f["L1_xattn_Wo"]], 1),
        "cols": np.stack([f["L1_xattn_bk"], f["L1_xattn_bv"], f["L1_xattn_bq"]], 1),
        "rows": np.concatenate([f["L0_xattn_bo"], f["L1_xattn_bo"]] + [f[f"L1_ffn_{n}_node_b"] for n in "qkv"])[None],
        "w1": w1.transpose(2, 0, 1, 3).reshape(D, UPB * 128),
        "w2": w2.reshape(NETS * CHUNKS, 128, D).transpose(1, 0, 2).reshape(128, UPB * D),
        "nodew": np.concatenate([f[f"L1_ffn_{n}_node_w"] for n in "qkv"]).T,
        "leafb": leafb.reshape(2, 128, 192).transpose(1, 0, 2),
    }
    return {n: np.ascontiguousarray(v) for n, v in arrays.items()}


def kernel(**inputs):
    import numpy as _np
    import concourse.bacc as _bacc
    from concourse import mybir as _mybir
    from concourse.bass_utils import run_bass_kernel_spmd as _run

    nc = _bacc.Bacc("TRN2", target_bir_lowering=False, num_devices=1)
    arrays, args = {}, []
    for name, a in _layout(inputs).items():
        arrays[f"in_{name}_dram"] = a
        args.append(nc.dram_tensor(f"in_{name}_dram", a.shape, _mybir.dt.from_np(a.dtype), kind="ExternalInput").ap())
    args.append(nc.dram_tensor("out_0_dram", (B, T, D), _mybir.dt.from_np(_np.dtype("float32")), kind="ExternalOutput").ap())
    build(nc, *args)
    r = _run(nc, [arrays], core_ids=[0])
    return r.results[0]["out_0_dram"]
```

```python
from contextlib import ExitStack

import concourse.bass as bass
from concourse import mybir

F32 = mybir.dt.float32
F32R = mybir.dt.float32r
F16 = mybir.dt.float16
BF16 = mybir.dt.bfloat16
U8 = mybir.dt.uint8
ALU = mybir.AluOpType
ACT = mybir.ActivationFunctionType
AX = mybir.AxisListType

B, T, D = 8, 128, 128
S2 = 120
HEADS, HD = 16, 8
BLOCKS, TILES = 4, 4
HALF = B // 2
NT = HALF * T
NK = HALF * S2
UNITS = B * TILES
VCOLS = 3 * HD + 1
EXPERTS, TOPK, PAIRS = 16, 4, 9
NETS, LEAVES, NODES, CHUNKS = 3, 16, 15, 8
UPB = NETS * CHUNKS
SEL = 64
EPS = 1e-5
SCALE = float(D) ** -0.5
NEG = -1e9
RING, LAG = 4, 2
CUTS, CUT = 3, 1024
BIG = 2.0 ** 100

NORMS = ((0, 0), (0, 1), (1, 0), (1, 1), (2, 0), (3, 0), (2, 1), (3, 1))
C_ID, C_SX, C_BX, C_SK, C_BK, C_PART, C_LEAF, C_END = 0, 128, 129, 130, 131, 132, 135, 151
V_BK, V_BV, V_BQ, V_END = 0, 1, 2, 3
R_BO0, R_BO1, R_NB, R_END = 0, 128, 256, 256 + NETS * NODES


def build(nc: bass.Bass, x, ctx, ctxT, mask, consts, gsel, blockw, woT, up0, down0, router,
          attnw, cols, rows, w1, w2, nodew, leafb, out):
    stack = ExitStack()
    with stack:
        def sb(name, shape, dt=F32):
            return stack.enter_context(nc.sbuf_tensor(name, shape, dt))

        def sem(name):
            return stack.enter_context(nc.semaphore(name))

        bank = [stack.enter_context(nc.psum_tensor(f"bank{i}", [128, 512], F32)) for i in range(8)]
        TA, OUT = bank[0], bank[1]
        SC, SCT = (bank[2], bank[4]), (bank[3], bank[5])
        CTX = bank[6:8]
        UP, GATE, ACC = (bank[4], bank[5]), (bank[6], bank[3]), bank[7]
        FUP, FACC = bank[4:7], (bank[7], bank[3])
        TURN, SIDE, MIX = bank[0], bank[1], bank[2]

        c_sb = sb("c_sb", [128, C_END])
        ident = c_sb[:, C_ID:C_ID + 128]
        idb = sb("idb", [128, 128], BF16)
        gsel_sb = sb("gsel_sb", [48, PAIRS - 1, 128], BF16)
        x0 = sb("x0", [T, B, D])
        ctx_sb = sb("ctx_sb", [S2, B, D])
        ctxT_sb = sb("ctxT_sb", [D, B * S2])
        blockw_sb = sb("blockw_sb", [128, 3, 128])
        woT_sb = sb("woT_sb", [128, 128])
        staged = sb("staged", [128, UPB * 128])
        router_sb = sb("router_sb", [128, EXPERTS])
        attnw_sb = sb("attnw_sb", [128, 4, 128])
        cols_sb = sb("cols_sb", [128, V_END])
        rows_sb = sb("rows_sb", [128, R_END])
        mask_u8 = sb("mask_u8", [128, B * S2], U8)
        nodew_sb = sb("nodew_sb", [128, NETS * NODES])
        leafb_sb = sb("leafb_sb", [128, 2, 64 + 128])

        up0h, up0l = sb("up0h", [128, PAIRS * 128], F32R), sb("up0l", [128, PAIRS * 128], F32R)
        down0h, down0l = sb("down0h", [128, PAIRS * 128], F32R), sb("down0l", [128, PAIRS * 128], F32R)
        w1h, w1l = sb("w1h", [128, UPB * 128], F32R), sb("w1l", [128, UPB * 128], F32R)
        w2h, w2l = sb("w2h", [128, UPB * 128], F32R), sb("w2l", [128, UPB * 128], F32R)
        W0 = PAIRS * 128
        UP0, DOWN0 = slice(0, W0), slice(W0, 2 * W0)

        xres = sb("xres", [T, B, D])
        xs = [x0, xres, xres, xres]
        stats = sb("stats", [T, HALF, 6])
        meanvar = sb("meanvar", [T, len(NORMS), HALF, 2])
        vareps = sb("vareps", [T, len(NORMS), HALF])
        rstd = sb("rstd", [T, len(NORMS), HALF])
        minushalf = sb("minushalf", [T, HALF])
        xn = sb("xn", [T, HALF, D])
        xnT = sb("xnT", [D, NT])
        xh, xl = sb("xh", [D, 2, NT], F32R), sb("xl", [D, 2, NT], F32R)

        brep = sb("brep", [128, BLOCKS, 128])
        cvo = sb("cvo", [128, 128])
        xrep = sb("xrep", [T, BLOCKS * TILES, 4, HD])
        ring = sb("ring", [128, 2 * RING, NT], F32R)
        acth, actl = ring[:, 0:RING, :], ring[:, RING:2 * RING, :]
        usplit = ring[:, 0:2, :]
        kst = ring[:, 2:4, 0:BLOCKS * S2].rearrange("p i (j k) -> p i j k", j=BLOCKS)
        xst = ring[:, 4:6, :].rearrange("p i (j t) -> p i j t", j=BLOCKS)
        vparts = sb("vparts", [S2, B, HEADS, VCOLS], BF16)
        negmax = sb("negmax", [T, 4, BLOCKS], BF16)
        probs_buf = sb("probs_buf", [128, 3, BLOCKS * T])
        probT = probs_buf[0:S2, :, :]
        probh, probl = sb("probh", [S2, 3, BLOCKS * T], F16), sb("probl", [S2, 3, BLOCKS * T], F16)
        rden = sb("rden", [T, HEADS])
        osum = sb("osum", [T, D])
        onorm = sb("onorm", [T, D])
        onT = sb("onT", [D, T])

        lmax = sb("lmax", [T, HALF])
        lshift = sb("lshift", [T, HALF, EXPERTS])
        lexp = sb("lexp", [T, HALF, EXPERTS])
        lsum = sb("lsum", [T, HALF])
        lrec = sb("lrec", [T, HALF])
        probs = sb("probs", [T, HALF, EXPERTS])
        top8 = sb("top8", [T, HALF, 8])
        rest = sb("rest", [T, HALF, EXPERTS])
        gate = sb("gate", [T, HALF, EXPERTS])
        gres = sb("gres", [T, HALF, EXPERTS])
        gparts = sb("gparts", [T, HALF, 3, EXPERTS], BF16)
        gT = sb("gT", [48, 2, NT], BF16)
        shared = sb("shared", [128, 8 * NT])
        gelu = shared[:, 0:2 * NT].rearrange("p (i t) -> p i t", i=2)
        gated = shared[:, 2 * NT:4 * NT].rearrange("p (i t) -> p i t", i=2)
        gsel_f32 = shared[0:48, 0:2 * NT].rearrange("p (c m) -> p c m", c=PAIRS - 1)
        maskf, kT1, vT1, cB = (shared[:, i * B * S2:(i + 1) * B * S2] for i in range(4))
        qkvT = shared[:, 0:NETS * NT].rearrange("p (n t) -> p n t", n=NETS)
        vnat = shared[:, NETS * NT:(NETS + 1) * NT].rearrange("p (b d) -> p b d", b=HALF)
        yT = sb("yT", [D, NT])

        mscale = sb("mscale", [128, B * S2])
        mneg = maskf
        aK = sb("aK", [128, B * S2])
        cmask = sb("cmask", [128, B * S2])
        vo = ctx_sb
        aexp = probs_buf[:, 0, :].rearrange("t (b k) -> t b k", b=HALF)
        apT = probs_buf[:, 1, :].rearrange("t (b k) -> t b k", b=HALF)
        sc1 = probs_buf[:, 2, 0:NK]
        sc2 = sb("sc2", [T, NK])
        amax = sb("amax", [T, HALF])
        asum = sb("asum", [T, HALF])
        arec = sb("arec", [T, HALF])

        sres = kT1[:, 0:384].rearrange("p (a n) -> p a n", a=2)
        scomb = kT1[:, 384:768].rearrange("p (a n) -> p a n", a=2)
        spart = vT1[:, 0:576].bitcast(BF16).rearrange("p (s a n) -> p s a n", s=3, a=2)
        lup = sb("lup", [128, 2, LEAVES, 64], BF16)
        ldown = sb("ldown", [128, 2, 128], BF16)
        nscore = sb("nscore", [T, HALF, NETS * NODES])
        right = sb("right", [T, HALF * NETS, NODES])
        lev = [None, sb("lev1", [T, HALF * NETS, 2]), sb("lev2", [T, HALF * NETS, 4]),
               sb("lev3", [T, HALF * NETS, 8]), sb("lev4", [T, HALF * NETS, 16])]
        selrow = sb("selrow", [T, HALF, 4, 4, LEAVES], BF16)
        selT = shared[:, 4 * NT:6 * NT].bitcast(BF16).rearrange("p (h a t) -> p h a t", h=2, a=2)
        dmax = sb("dmax", [T, HALF])

        s_early, s_x, s_ctx, s_mid = sem("early_loaded"), sem("x_loaded"), sem("ctx_loaded"), sem("mid_loaded")
        s_w0, s_w1, s_w2 = sem("w0_loaded"), sem("w1_loaded"), sem("w2_loaded")
        s_late, s_stored = sem("late_loaded"), sem("stored")
        s_idb, s_gsel, s_memset, s_selzero = sem("idb_ready"), sem("gsel_ready"), sem("memset_done"), sem("selrow_zeroed")
        s_fold, s_brep, s_cvo = sem("folded"), sem("brep_ready"), sem("cvo_ready")
        s_kraw, s_ksign, s_kst = sem("k_stack_raw"), sem("k_signed"), sem("k_stack")
        s_stats, s_mv, s_ve, s_rstd, s_xn = sem("stats"), sem("meanvar"), sem("vareps"), sem("rstd"), sem("xn")
        s_xrep, s_xraw, s_xsign, s_xst = sem("xrep"), sem("x_stack_raw"), sem("x_signed"), sem("x_stack")
        s_vp, s_xbo = sem("value_parts"), sem("xbo")
        s_sc, s_nm, s_sT, s_p, s_ph, s_pl, s_pv = (
            sem("scores"), sem("negmax"), sem("scoresT"), sem("probT"), sem("prob_hi"), sem("prob_lo"), sem("pv"))
        s_rd, s_on, s_onp, s_onT, s_y0, s_x1 = (
            sem("out_step"), sem("onorm"), sem("onT_psum"), sem("onT"), sem("attn0_out"), sem("x1"))
        s_hi0, s_lo0, s_hi1, s_lo1, s_hi2, s_lo2 = (
            sem("w0_hi"), sem("w0_lo"), sem("w1_hi"), sem("w1_lo"), sem("w2_hi"), sem("w2_lo"))
        s_tp, s_xnT, s_xh, s_xl = sem("xn_transposed"), sem("xnT"), sem("xh"), sem("xl")
        s_lg, s_lsh, s_lex, s_gstep, s_gp, s_gTp, s_gT = (
            sem("logits"), sem("logits_shifted"), sem("logits_exp"), sem("gate_step"), sem("gate_parts"),
            sem("gateT_psum"), sem("gateT"))
        s_up, s_gb, s_ge, s_ga, s_ah, s_al, s_dn = (
            sem("moe_up"), sem("gate_spread"), sem("gelu"), sem("gated"), sem("act_hi"), sem("act_lo"), sem("moe_down"))
        s_yT, s_yb, s_x2 = sem("moe_yT"), sem("moe_y"), sem("x2")
        s_ck, s_ckr, s_vo, s_mk = sem("ctx_product"), sem("ctx_product_read"), sem("vo_ready"), sem("mask_step")
        s_as, s_am, s_ae, s_apT, s_aT, s_av, s_x3 = (
            sem("attn1_scores"), sem("attn1_step"), sem("attn1_exp"), sem("attn1_pT_psum"), sem("attn1_pT"),
            sem("attn1_out"), sem("x3"))
        s_lb, s_ns, s_tree, s_selrow, s_selp, s_selT = (
            sem("leaf_bias_step"), sem("node_scores"), sem("tree_step"), sem("selrow"), sem("selT_psum"), sem("selT"))
        s_fu, s_fh, s_fl, s_fd, s_net, s_qkv = (
            sem("ffn_up"), sem("ffn_hi"), sem("ffn_lo"), sem("ffn_down"), sem("net_out"), sem("net_taken"))
        s_vb, s_vn, s_ds, s_dm, s_de, s_dpT, s_dT, s_do, s_dr, s_out = (
            sem("v_back"), sem("v_rows"), sem("self_scores"), sem("self_step"), sem("self_exp"), sem("self_pT_psum"),
            sem("self_pT"), sem("self_out"), sem("self_rec"), sem("out_ready"))

        block = stack.enter_context(nc.Block())

        @block.sync
        def _(sp):
            sp.dma_start(blockw_sb[:, :, :], blockw).then_inc(s_early, 16)
            sp.dma_start(c_sb[:, :], consts).then_inc(s_early, 16)
            sp.dma_start(ctxT_sb[:, :], ctxT).then_inc(s_early, 16)
            sp.dma_start(woT_sb[:, :], woT).then_inc(s_early, 16)
            sp.dma_start(ctx_sb[:, :, :], ctx.rearrange("b s d -> s b d")).then_inc(s_ctx, 16)
            sp.dma_start(staged[:, UP0], up0).then_inc(s_w0, 16)
            sp.dma_start(staged[:, DOWN0], down0).then_inc(s_w0, 16)
            sp.wait_ge(s_lo0, 2)
            sp.dma_start(staged[:, :], w1).then_inc(s_w1, 16)
            sp.wait_ge(s_lo1, CUTS)
            sp.dma_start(staged[:, :], w2).then_inc(s_w2, 16)
            for b in range(B):
                sp.wait_ge(s_out, b + 1)
                sp.dma_start(out[b, :, :], xres[:, b, :]).then_inc(s_stored, 16)
            sp.wait_ge(s_stored, 16 * B)

        @block.gpsimd
        def _(pool):
            def reciprocal_deviation(k):
                pool.wait_ge(s_mv, k + 1)
                pool.tensor_scalar(vareps[:, k, :], meanvar[:, k, :, 1], EPS, None, ALU.add).then_inc(s_ve, 1)
                pool.wait_ge(s_ve, k + 1)
                pool.tensor_tensor(rstd[:, k, :], vareps[:, k, :], minushalf[:, :], ALU.pow).then_inc(s_rstd, 1)

            def prob_lo(n):
                pool.wait_ge(s_ph, n + 1)
                if n >= 3:
                    pool.wait_ge(s_pv, n - 2)
                pool.tensor_tensor(probl[:, n % 3, :], probT[:, n % 3, :], probh[:, n % 3, :], ALU.subtract).then_inc(s_pl, 1)

            def xlo(k):
                pool.wait_ge(s_xh, k + 1)
                pool.tensor_tensor(xl[:, k % 2, :], xnT[:, :], xh[:, k % 2, :].bitcast(F32), ALU.subtract).then_inc(s_xl, 1)

            def moe_lo(m):
                pool.wait_ge(s_ah, m + 1)
                if m >= RING:
                    pool.wait_ge(s_dn, m - RING + 1)
                src = gated if m % PAIRS else gelu
                pool.tensor_tensor(actl[:, m % RING, :], src[:, m % 2, :], acth[:, m % RING, :].bitcast(F32), ALU.subtract
                                   ).then_inc(s_al, 1)

            pool.memset(minushalf[:, :], -0.5).then_inc(s_memset, 1)
            pool.memset(vparts[:, :, :, 3 * HD:VCOLS], 1.0).then_inc(s_memset, 1)
            pool.memset(selrow[:, :, 3, :, :], 0.0).then_inc(s_selzero, 1)
            pool.wait_ge(s_memset, 1)
            reciprocal_deviation(0)
            pool.wait_ge(s_early, 16 * 4)
            pool.tensor_copy(idb[:, :], ident).then_inc(s_idb, 1)
            reciprocal_deviation(1)
            for n in range(UNITS):
                prob_lo(n)
                if n == 0:
                    pool.wait_ge(s_x, 16)
                    pool.wait_ge(s_mid, 16 * 6)
                    pool.tensor_tensor(xres[:, :, :], x0[:, :, :], rows_sb[:, None, R_BO0:R_BO0 + D].broadcast_to([T, B, D]),
                                       ALU.add).then_inc(s_xbo, 1)
                    pool.tensor_copy(gsel_sb[:, :, :], gsel_f32).then_inc(s_gsel, 1)
                if n in (4, 6):
                    k = (n - 4) // 2
                    pool.wait_ge(s_hi0, k + 1)
                    lo, hi, c = [(up0l, up0h, UP0), (down0l, down0h, DOWN0)][k]
                    pool.tensor_tensor(lo[:, :], staged[:, c], hi[:, :].bitcast(F32), ALU.subtract).then_inc(s_lo0, 1)
                if n >= 12 and n % 3 == 0:
                    k = n // 3 - 4
                    if k < CUTS:
                        pool.wait_ge(s_hi1, k + 1)
                        c = slice(k * CUT, (k + 1) * CUT)
                        pool.tensor_tensor(w1l[:, c], staged[:, c], w1h[:, c].bitcast(F32), ALU.subtract).then_inc(s_lo1, 1)
                if n == 21:
                    reciprocal_deviation(2)
                if n == 25:
                    xlo(0)
            for m in range(PAIRS):
                moe_lo(m)
                if m == 2:
                    reciprocal_deviation(3)
                if m == 4:
                    xlo(1)
            for m in range(PAIRS, 2 * PAIRS):
                moe_lo(m)
                if m == PAIRS + 1:
                    reciprocal_deviation(4)
            reciprocal_deviation(5)
            xlo(2)
            reciprocal_deviation(6)
            reciprocal_deviation(7)
            xlo(3)

        @block.scalar
        def _(act):
            act.dma_start(x0[:, :, :], x.rearrange("b t d -> t b d")).then_inc(s_x, 16)
            act.dma_start(rows_sb[:, :], rows.broadcast_to([128, R_END])).then_inc(s_mid, 16)
            act.dma_start(router_sb[:, :], router).then_inc(s_mid, 16)
            act.dma_start(attnw_sb[:, :, :], attnw).then_inc(s_mid, 16)
            act.dma_start(cols_sb[:, :], cols).then_inc(s_mid, 16)
            act.dma_start(mask_u8[:, :], mask.broadcast_to([128, B * S2])).then_inc(s_mid, 16)
            act.dma_start(gsel_f32, gsel).then_inc(s_mid, 16)
            act.dma_start(nodew_sb[:, :], nodew).then_inc(s_late, 16)
            act.dma_start(leafb_sb[:, :, :], leafb).then_inc(s_late, 16)

            def sign_x(b):
                act.wait_ge(s_xraw, b + 1)
                if b:
                    act.wait_ge(s_xst, b)
                act.activation(usplit[:, 0, :], TA[:, :], ACT.Identity, scale=c_sb[:, C_SX:C_SX + 1]).then_inc(s_xsign, 1)

            def sign_k(b):
                act.wait_ge(s_kraw, b + 1)
                if b:
                    act.wait_ge(s_kst, b)
                act.activation(usplit[:, 1, 0:BLOCKS * S2], TA[:, 0:BLOCKS * S2], ACT.Identity, scale=c_sb[:, C_SK:C_SK + 1]
                               ).then_inc(s_ksign, 1)

            def value_part(k):
                act.wait_ge(s_ctx, 16)
                if k:
                    act.wait_ge(s_vp, 2)
                src = ctx_sb if k == 0 else shared[0:S2, 4 * NT:6 * NT].rearrange("s (b d) -> s b d", b=B)
                act.activation(vparts[:, :, :, k * HD:(k + 1) * HD].rearrange("s b h e -> s (b h) e"),
                               src[:, :, :].rearrange("s b (h e) -> s (b h) e", e=HD), ACT.Copy).then_inc(s_vp, 1)

            def exp_unit(n):
                act.wait_ge(s_sT, n + 1)
                if n >= 3:
                    act.wait_ge(s_pl, n - 2)
                act.activation(probT[:, n % 3, :], SCT[n % 2][0:S2, :], ACT.Exp, scale=SCALE).then_inc(s_p, 1)

            def turn_out(b):
                act.wait_ge(s_onp, b + 1)
                if b:
                    act.wait_ge(s_y0, b)
                act.activation(onT[:, :], TA[:, 0:T], ACT.Copy).then_inc(s_onT, 1)

            def context_product(i):
                act.wait_ge(s_ck, i + 1)
                if i == 0:
                    act.wait_ge(s_gsel, 1)
                    act.wait_ge(s_vp, 4)
                dst, bias = [(kT1, V_BK), (vT1, V_BV), (aK, None), (cB, None)][i // 2]
                h = i % 2
                kw = {} if bias is None else {"bias": cols_sb[:, bias:bias + 1]}
                act.activation(dst[:, h * NK:(h + 1) * NK], CTX[i % 2][:, 0:NK], ACT.Identity, **kw).then_inc(s_ckr, 1)

            def split_x(k):
                q = (0, 1, 3, 5)[k]
                act.wait_ge(s_xnT, q + 1)
                if k >= 2:
                    act.wait_ge(s_up, PAIRS * (k - 1))
                act.activation(xh[:, k % 2, :], xnT[:, :], ACT.Copy).then_inc(s_xh, 1)

            def exp_logits(h):
                act.wait_ge(s_lsh, h + 1)
                act.activation(lexp[:, :, :], lshift[:, :, :], ACT.Exp).then_inc(s_lex, 1)

            sign_x(0)
            sign_k(0)
            value_part(0)
            value_part(1)
            for n in range(UNITS):
                b, p = divmod(n, TILES)
                if p == 0 and b >= 2:
                    turn_out(b - 2)
                if p == 0 and b + 1 < B:
                    sign_x(b + 1)
                if p == 1 and b + 1 < B:
                    sign_k(b + 1)
                exp_unit(n)
                if n == 2:
                    act.wait_ge(s_w0, 32)
                    act.activation(up0h[:, :], staged[:, UP0], ACT.Copy).then_inc(s_hi0, 1)
                if n == 3:
                    act.activation(down0h[:, :], staged[:, DOWN0], ACT.Copy).then_inc(s_hi0, 1)
                if n >= 12 and n % 3 == 2 and n // 3 - 4 < CUTS:
                    k = n // 3 - 4
                    if k == 0:
                        act.wait_ge(s_w1, 16)
                    c = slice(k * CUT, (k + 1) * CUT)
                    act.activation(w1h[:, c], staged[:, c], ACT.Copy).then_inc(s_hi1, 1)
                if 4 <= n < 12:
                    context_product(n - 4)
                if n == 25:
                    split_x(0)
                if n == 27:
                    exp_logits(0)
            turn_out(B - 2)

            def moe_hi(m):
                if m % PAIRS:
                    act.wait_ge(s_ga, m - m // PAIRS)
                else:
                    act.wait_ge(s_ge, m + 1)
                if m >= RING:
                    act.wait_ge(s_dn, m - RING + 1)
                src = gated if m % PAIRS else gelu
                act.activation(acth[:, m % RING, :], src[:, m % 2, :], ACT.Copy).then_inc(s_ah, 1)

            def moe_gelu(m):
                act.wait_ge(s_up, m + 1)
                if m == 0:
                    act.wait_ge(s_lb, 10)
                if m >= 2:
                    act.wait_ge(s_al, m - 1)
                act.activation(gelu[:, m % 2, :], UP[m % 2][:, :], ACT.Gelu).then_inc(s_ge, 1)

            def take_y(h):
                act.wait_ge(s_dn, PAIRS * (h + 1))
                if h:
                    act.wait_ge(s_yb, h)
                act.activation(yT[:, :], ACC[:, :], ACT.Copy).then_inc(s_yT, 1)

            def w2_hi(k):
                if k == 0:
                    act.wait_ge(s_w2, 16)
                c = slice(k * CUT, (k + 1) * CUT)
                act.activation(w2h[:, c], staged[:, c], ACT.Copy).then_inc(s_hi2, 1)

            def attn1_exp(h):
                act.wait_ge(s_am, 4 * h + 3)
                if h:
                    act.wait_ge(s_apT, h)
                for i in range(HALF):
                    act.activation(aexp[:, i, 0:S2], sc2[:, i * S2:(i + 1) * S2], ACT.Exp, bias=amax[:, i:i + 1],
                                   accum_out=asum[:, i:i + 1]).then_inc(s_ae, 1)

            def attn1_pT(h):
                act.wait_ge(s_apT, h + 1)
                if h:
                    act.wait_ge(s_av, h)
                act.activation(apT[0:S2, :, :].rearrange("p b t -> p (b t)"), TURN[0:S2, :], ACT.Copy).then_inc(s_aT, 1)

            def ffn_hi(m):
                act.wait_ge(s_fu, m + 1)
                if m >= RING:
                    act.wait_ge(s_fd, m - RING + 1)
                act.activation(acth[:, m % RING, :], FUP[m % 3][:, :], ACT.Relu).then_inc(s_fh, 1)

            def take_net(j):
                act.wait_ge(s_net, j + 1)
                if j == 3:
                    act.wait_ge(s_ds, 1)
                if j == 5:
                    act.wait_ge(s_vb, 1)
                act.activation(qkvT[:, j % 3, :], FACC[j % 2][:, :], ACT.Copy).then_inc(s_qkv, 1)

            def self_exp(h):
                act.wait_ge(s_dm, 2 * h + 2)
                for i in range(HALF):
                    act.activation(aexp[:, i, :], SIDE[:, i * T:(i + 1) * T], ACT.Exp, scale=SCALE, bias=amax[:, i:i + 1],
                                   accum_out=asum[:, i:i + 1]).then_inc(s_de, 1)

            def self_pT(h):
                act.wait_ge(s_dpT, h + 1)
                if h:
                    act.wait_ge(s_do, h)
                act.activation(apT[:, :, :].rearrange("p b t -> p (b t)"), TURN[:, :], ACT.Copy).then_inc(s_dT, 1)

            for c in range(PAIRS):
                moe_gelu(c)
                if c:
                    moe_hi(c - 1)
                if c == 1:
                    turn_out(B - 1)
                if c == 5:
                    split_x(1)
                if c == 7:
                    exp_logits(1)
            moe_hi(PAIRS - 1)
            for c in range(PAIRS):
                m = PAIRS + c
                moe_gelu(m)
                if c:
                    moe_hi(m - 1)
                if c == 1:
                    take_y(0)
                if c == 6:
                    attn1_exp(0)
            moe_hi(2 * PAIRS - 1)
            for k in range(CUTS):
                w2_hi(k)
            take_y(1)
            attn1_pT(0)
            split_x(2)
            for k in range(UPB):
                ffn_hi(k)
                if k >= CHUNKS and k % CHUNKS == 4:
                    take_net(k // CHUNKS - 1)
                if k == 9:
                    attn1_exp(1)
                if k == 11:
                    attn1_pT(1)
                if k == 18:
                    split_x(3)
            for k in range(UPB):
                ffn_hi(UPB + k)
                if k == 2:
                    take_net(2)
                if k >= CHUNKS and k % CHUNKS == 4:
                    take_net(3 + k // CHUNKS - 1)
                if k == 5:
                    self_exp(0)
                if k == 7:
                    self_pT(0)
                if k == 22:
                    self_exp(1)
            self_pT(1)
            take_net(5)

        @block.vector
        def _(dve):
            def ln_stats(k):
                l, h = NORMS[k]
                dve.wait_ge(*[(s_x, 16), (s_x1, HALF * (h + 1)), (s_x2, h + 1), (s_x3, HALF * (h + 1))][l])
                for i in range(HALF):
                    dve.bn_stats(stats[:, i, :], xs[l][:, HALF * h + i, :]).then_inc(s_stats, 1)
                dve.wait_ge(s_stats, HALF * (k + 1))
                for i in range(HALF):
                    last = dve.bn_aggr(meanvar[:, k, i, :], stats[:, i, :])
                last.then_inc(s_mv, 1)

            def normalize(k):
                l, h = NORMS[k]
                dve.wait_ge(s_rstd, k + 1)
                if k > 2:
                    dve.wait_ge(s_tp, k - 2)
                for i in range(HALF):
                    dve.tensor_scalar(xn[:, i, :], xs[l][:, HALF * h + i, :], meanvar[:, k, i, 0:1], rstd[:, k, i:i + 1],
                                      ALU.subtract, ALU.mult).then_inc(s_xn, 1)

            def take_xnT(q):
                dve.wait_ge(s_tp, q + 1)
                if q:
                    dve.wait_ge(*[(s_lg, 1), (s_lg, 2), (s_as, 1), (s_ns, 1), (s_as, 2)][q - 1])
                if q in (1, 2, 4):
                    dve.wait_ge(s_xl, {1: 1, 2: 2, 4: 3}[q])
                dve.tensor_copy(xnT[:, :], (CTX[0] if q == 0 else TURN)[:, :]).then_inc(s_xnT, 1)

            def repeat_x(b):
                k, i = divmod(b, HALF)
                dve.wait_ge(s_rstd, k + 1)
                if b:
                    dve.wait_ge(s_xraw, b)
                dve.tensor_scalar(xrep[:, :, :, :],
                                  x0[:, b, :].rearrange("t (g e) -> t g e", e=HD)[:, :, None, :].broadcast_to([T, 16, 4, HD]),
                                  meanvar[:, k, i, 0:1], rstd[:, k, i:i + 1], ALU.subtract, ALU.mult).then_inc(s_xrep, 1)

            def stack_x(b):
                dve.wait_ge(s_xsign, b + 1)
                if b >= 2:
                    dve.wait_ge(s_sT, 4 * b - 4)
                dve.scalar_tensor_tensor(xst[:, b % 2, :, :].rearrange("p j t -> p (j t)"), TA[:, :],
                                         c_sb[:, C_BX:C_BX + 1], usplit[:, 0, :].bitcast(F32), ALU.mult, ALU.add
                                         ).then_inc(s_xst, 1)

            def stack_k(b):
                dve.wait_ge(s_ksign, b + 1)
                if b >= 2:
                    dve.wait_ge(s_sT, 4 * b - 4)
                dve.scalar_tensor_tensor(kst[:, b % 2, :, :].rearrange("p j t -> p (j t)"), TA[:, 0:BLOCKS * S2],
                                         c_sb[:, C_BK:C_BK + 1], usplit[:, 1, 0:BLOCKS * S2].bitcast(F32), ALU.mult, ALU.add
                                         ).then_inc(s_kst, 1)

            def value_rest(k):
                dve.wait_ge(s_vp, 2 * k + 1)
                if k == 0:
                    dve.wait_ge(s_ctx, 16)
                res = shared[0:S2, 4 * NT:6 * NT].rearrange("s (g e) -> s g e", e=HD)
                src = ctx_sb[:, :, :].rearrange("s b (h e) -> s (b h) e", e=HD) if k == 0 else res
                parts = vparts[:, :, :, :].rearrange("s b h v -> s (b h) v")
                dst = res if k == 0 else parts[:, :, 2 * HD:3 * HD]
                dve.tensor_tensor(dst, src, parts[:, :, k * HD:(k + 1) * HD], ALU.subtract).then_inc(s_vp, 1)

            def max_unit(n):
                dve.wait_ge(s_sc, n + 1)
                if n >= 4:
                    dve.wait_ge(s_sT, n - 3)
                dve.tensor_reduce(negmax[:, n % 4, :], SC[n % 2][:, 0:BLOCKS * S2].rearrange("t (j k) -> t j k", k=S2),
                                  AX.X, ALU.max, negate=True).then_inc(s_nm, 1)

            def prob_hi(n):
                dve.wait_ge(s_p, n + 1)
                if n >= 3:
                    dve.wait_ge(s_pv, n - 2)
                dve.tensor_copy(probh[:, n % 3, :], probT[:, n % 3, :]).then_inc(s_ph, 1)

            def normalize_out(b):
                O = OUT[:, 0:HEADS * VCOLS].rearrange("t (h v) -> t h v", v=VCOLS)
                dve.wait_ge(s_pv, TILES * (b + 1))
                dve.reciprocal(rden[:, :], O[:, :, 3 * HD]).then_inc(s_rd, 1)
                dve.tensor_reduce(osum[:, :].rearrange("t (h e) -> t h e", e=HD),
                                  O[:, :, 0:3 * HD].rearrange("t h (s e) -> t h e s", s=3), AX.X, ALU.add).then_inc(s_rd, 1)
                dve.wait_ge(s_rd, 2 * b + 2)
                if b:
                    dve.wait_ge(s_onp, b)
                dve.tensor_tensor(onorm[:, :].rearrange("t (h e) -> t h e", e=HD), osum[:, :].rearrange("t (h e) -> t h e", e=HD),
                                  rden[:, :, None].broadcast_to([T, HEADS, HD]), ALU.mult).then_inc(s_on, 1)

            def add_x1(b):
                dve.wait_ge(s_y0, b + 1)
                dve.wait_ge(s_xbo, 1)
                dve.tensor_tensor(xres[:, b, :], TA[:, D:2 * D], xres[:, b, :], ALU.add).then_inc(s_x1, 1)

            def masks():
                dve.wait_ge(s_mid, 16 * 6)
                dve.wait_ge(s_gsel, 1)
                dve.tensor_copy(maskf, mask_u8[:, :]).then_inc(s_mk, 1)
                dve.wait_ge(s_mk, 1)
                dve.tensor_scalar(mscale[:, :], maskf, SCALE, None, ALU.mult).then_inc(s_mk, 1)
                dve.wait_ge(s_mk, 2)
                dve.tensor_scalar(mneg, maskf, -NEG, NEG, ALU.mult, ALU.add).then_inc(s_mk, 1)

            def mask_bias():
                dve.wait_ge(s_ckr, 8)
                dve.wait_ge(s_mk, 3)
                dve.tensor_tensor(cmask[:, :], cB, mscale[:, :], ALU.mult).then_inc(s_mk, 1)
                dve.wait_ge(s_mk, 4)
                dve.tensor_tensor(cmask[:, :], cmask[:, :], mneg, ALU.add).then_inc(s_mk, 1)

            def take_vo(h):
                dve.wait_ge(s_ck, 9 + h)
                dve.tensor_tensor(vo[:, HALF * h:HALF * (h + 1), :], CTX[h][0:S2, :].rearrange("s (b d) -> s b d", d=D),
                                  rows_sb[0:S2, None, R_BO1:R_BO1 + D].broadcast_to([S2, HALF, D]), ALU.add).then_inc(s_vo, 1)

            def gate_start(h):
                L = (CTX[1] if h == 0 else MIX)[:, 0:HALF * EXPERTS].rearrange("t (b e) -> t b e", e=EXPERTS)
                dve.wait_ge(s_lg, h + 1)
                dve.tensor_reduce(lmax[:, :], L, AX.X, ALU.max).then_inc(s_gstep, 1)
                dve.wait_ge(s_gstep, 17 * h + 1)
                if h:
                    dve.wait_ge(s_lex, h)
                dve.tensor_tensor(lshift[:, :, :], L, lmax[:, :, None].broadcast_to([T, HALF, EXPERTS]), ALU.subtract
                                  ).then_inc(s_lsh, 1)

            def gate_rest(h):
                g0 = 17 * h
                dve.wait_ge(s_lex, h + 1)
                dve.tensor_reduce(lsum[:, :], lexp[:, :, :], AX.X, ALU.add).then_inc(s_gstep, 1)
                dve.wait_ge(s_gstep, g0 + 2)
                dve.reciprocal(lrec[:, :], lsum[:, :]).then_inc(s_gstep, 1)
                dve.wait_ge(s_gstep, g0 + 3)
                dve.tensor_tensor(probs[:, :, :], lexp[:, :, :], lrec[:, :, None].broadcast_to([T, HALF, EXPERTS]), ALU.mult
                                  ).then_inc(s_gstep, 1)
                dve.wait_ge(s_gstep, g0 + 4)
                for i in range(HALF):
                    dve.max(top8[:, i, :], probs[:, i, :]).then_inc(s_gstep, 1)
                dve.wait_ge(s_gstep, g0 + 8)
                dve.memset(top8[:, :, TOPK:8], -1.0).then_inc(s_gstep, 1)
                dve.wait_ge(s_gstep, g0 + 9)
                for i in range(HALF):
                    dve.match_replace(rest[:, i, :], top8[:, i, :], probs[:, i, :], 0.0).then_inc(s_gstep, 1)
                dve.wait_ge(s_gstep, g0 + 13)
                dve.tensor_tensor(gate[:, :, :], probs[:, :, :], rest[:, :, :], ALU.subtract).then_inc(s_gstep, 1)
                dve.wait_ge(s_gstep, g0 + 14)
                if h:
                    dve.wait_ge(s_gTp, h)
                dve.tensor_copy(gparts[:, :, 0, :], gate[:, :, :]).then_inc(s_gstep, 1)
                dve.wait_ge(s_gstep, g0 + 15)
                dve.tensor_tensor(gres[:, :, :], gate[:, :, :], gparts[:, :, 0, :], ALU.subtract).then_inc(s_gstep, 1)
                dve.wait_ge(s_gstep, g0 + 16)
                dve.tensor_copy(gparts[:, :, 1, :], gres[:, :, :]).then_inc(s_gstep, 1)
                dve.wait_ge(s_gstep, g0 + 17)
                dve.tensor_tensor(gparts[:, :, 2, :], gres[:, :, :], gparts[:, :, 1, :], ALU.subtract).then_inc(s_gp, 1)

            def take_gateT(h):
                dve.wait_ge(s_gTp, h + 1)
                dve.tensor_copy(gT[:, h, :], (CTX[1] if h == 0 else MIX)[0:48, :].bitcast(BF16)[:, 0:NT]).then_inc(s_gT, 1)

            def moe_gated(m):
                r = m - m // PAIRS - 1
                dve.wait_ge(s_ge, m + 1)
                dve.wait_ge(s_gb, r + 1)
                if m >= 2:
                    dve.wait_ge(s_al, m - 1)
                dve.tensor_tensor(gated[:, m % 2, :], gelu[:, m % 2, :], GATE[r % 2][:, :], ALU.mult).then_inc(s_ga, 1)

            def add_x2(h):
                dve.wait_ge(s_yb, h + 1)
                half = xres[:, HALF * h:HALF * (h + 1), :].rearrange("t b d -> t (b d)")
                dve.tensor_tensor(half, TURN[:, :], half, ALU.add).then_inc(s_x2, 1)

            def attn1_mask(h):
                dve.wait_ge(s_as, h + 1)
                dve.wait_ge(s_mk, 5)
                dve.tensor_tensor(sc1, SIDE[:, 0:NK], mscale[:, h * NK:(h + 1) * NK], ALU.mult).then_inc(s_am, 1)
                dve.wait_ge(s_am, 4 * h + 1)
                if h:
                    dve.wait_ge(s_ae, HALF * h)
                dve.tensor_tensor(sc2[:, :], sc1, cmask[:, h * NK:(h + 1) * NK], ALU.add).then_inc(s_am, 1)
                dve.wait_ge(s_am, 4 * h + 2)
                dve.tensor_reduce(amax[:, :], sc2[:, :].rearrange("t (b k) -> t b k", k=S2), AX.X, ALU.max, negate=True
                                  ).then_inc(s_am, 1)

            def add_x3(h):
                dve.wait_ge(s_ae, HALF * (h + 1))
                dve.reciprocal(arec[:, :], asum[:, :]).then_inc(s_am, 1)
                dve.wait_ge(s_am, 4 * h + 4)
                dve.wait_ge(s_av, h + 1)
                for i in range(HALF):
                    b = HALF * h + i
                    dve.scalar_tensor_tensor(xres[:, b, :], MIX[:, i * T:(i + 1) * T], arec[:, i:i + 1], xres[:, b, :],
                                             ALU.mult, ALU.add).then_inc(s_x3, 1)

            def leaf_bias():
                dve.wait_ge(s_late, 32)
                dve.tensor_copy(spart[:, 0, :, :], leafb_sb[:, :, :]).then_inc(s_lb, 1)
                dve.wait_ge(s_lb, 1)
                dve.tensor_tensor(sres[:, :, :], leafb_sb[:, :, :], spart[:, 0, :, :], ALU.subtract).then_inc(s_lb, 1)
                dve.wait_ge(s_lb, 2)
                dve.tensor_copy(spart[:, 1, :, :], sres[:, :, :]).then_inc(s_lb, 1)
                dve.wait_ge(s_lb, 3)
                dve.tensor_tensor(spart[:, 2, :, :], sres[:, :, :], spart[:, 1, :, :], ALU.subtract).then_inc(s_lb, 1)
                dve.tensor_scalar(scomb[:, :, :], spart[:, 0, :, :], c_sb[:, C_PART:C_PART + 1], None, ALU.mult).then_inc(s_lb, 1)
                for s in (1, 2):
                    dve.wait_ge(s_lb, 4 + s)
                    dve.scalar_tensor_tensor(scomb[:, :, :].rearrange("p a n -> p (a n)"),
                                             spart[:, s, :, :].rearrange("p a n -> p (a n)"), c_sb[:, C_PART + s:C_PART + s + 1],
                                             scomb[:, :, :].rearrange("p a n -> p (a n)"), ALU.mult, ALU.add).then_inc(s_lb, 1)

            def leaf_rows():
                dve.wait_ge(s_lb, 7)
                dve.tensor_copy(ldown[:, :, :], scomb[:, :, 64:192]).then_inc(s_lb, 1)
                for a in range(2):
                    dve.tensor_tensor(lup[:, a, :, :], scomb[:, a, None, 0:64].broadcast_to([128, LEAVES, 64]),
                                      c_sb[:, C_LEAF:C_LEAF + LEAVES, None].broadcast_to([128, LEAVES, 64]), ALU.mult
                                      ).then_inc(s_lb, 1)

            def w2_lo(k):
                dve.wait_ge(s_hi2, k + 1)
                c = slice(k * CUT, (k + 1) * CUT)
                dve.tensor_tensor(w2l[:, c], staged[:, c], w2h[:, c].bitcast(F32), ALU.subtract).then_inc(s_lo2, 1)

            def route(h):
                t0 = 11 * h
                dve.wait_ge(s_ns, h + 1)
                dve.tensor_tensor(nscore[:, :, :], SIDE[:, 0:HALF * NETS * NODES].rearrange("t (b n) -> t b n", b=HALF),
                                  rows_sb[:, None, R_NB:R_NB + NETS * NODES].broadcast_to([T, HALF, NETS * NODES]), ALU.add
                                  ).then_inc(s_tree, 1)
                dve.wait_ge(s_tree, t0 + 1)
                dve.tensor_scalar(right[:, :, :].rearrange("t g n -> t (g n)"), nscore[:, :, :].rearrange("t b n -> t (b n)"),
                                  0.0, None, ALU.is_ge).then_inc(s_tree, 1)
                dve.wait_ge(s_tree, t0 + 2)
                dve.tensor_copy(lev[1][:, :, 1], right[:, :, 0]).then_inc(s_tree, 1)
                dve.tensor_scalar(lev[1][:, :, 0], right[:, :, 0], -1.0, 1.0, ALU.mult, ALU.add).then_inc(s_tree, 1)
                for d in range(1, 4):
                    n = 2 ** d
                    dve.wait_ge(s_tree, t0 + 2 + 2 * d)
                    kids = lev[d + 1][:, :, :].rearrange("t g (n two) -> t g n two", two=2)
                    dve.tensor_tensor(kids[:, :, :, 1], lev[d][:, :, :], right[:, :, n - 1:2 * n - 1], ALU.mult).then_inc(s_tree, 1)
                    dve.wait_ge(s_tree, t0 + 3 + 2 * d)
                    dve.tensor_tensor(kids[:, :, :, 0], lev[d][:, :, :], kids[:, :, :, 1], ALU.subtract).then_inc(s_tree, 1)
                dve.wait_ge(s_tree, t0 + 10)
                leaf = lev[4][:, :, :].rearrange("t (b n) l -> t b n l", b=HALF)
                if h:
                    dve.wait_ge(s_selp, h)
                dve.tensor_scalar(selrow[:, :, 0:3, 0, :], leaf, -1.0, 1.0, ALU.mult, ALU.add).then_inc(s_tree, 1)
                for s in (1, 2, 3):
                    last = dve.tensor_copy(selrow[:, :, 0:3, s, :], leaf)
                last.then_inc(s_selrow, 1)

            def take_selT(h):
                dve.wait_ge(s_selp, h + 1)
                dve.tensor_copy(selT[:, h, :, :], SIDE[:, :].bitcast(BF16).rearrange("p (a t) -> p a t", a=2)).then_inc(s_selT, 1)

            def ffn_lo(m):
                dve.wait_ge(s_fh, m + 1)
                if m >= RING:
                    dve.wait_ge(s_fd, m - RING + 1)
                dve.scalar_tensor_tensor(actl[:, m % RING, :], FUP[m % 3][:, :], 0.0, acth[:, m % RING, :].bitcast(F32),
                                         ALU.max, ALU.subtract).then_inc(s_fl, 1)

            def self_v(h):
                dve.wait_ge(s_vb, h + 1)
                if h:
                    dve.wait_ge(s_do, h)
                dve.tensor_copy(vnat[:, :, :].rearrange("t b d -> t (b d)"), TURN[:, :]).then_inc(s_vn, 1)

            def self_max(h):
                dve.wait_ge(s_ds, h + 1)
                dve.tensor_reduce(dmax[:, :], SIDE[:, :].rearrange("t (b k) -> t b k", k=T), AX.X, ALU.max).then_inc(s_dm, 1)
                dve.wait_ge(s_dm, 2 * h + 1)
                dve.tensor_scalar(amax[:, :], dmax[:, :], -SCALE, None, ALU.mult).then_inc(s_dm, 1)

            def self_rec(h):
                dve.wait_ge(s_de, HALF * (h + 1))
                dve.reciprocal(arec[:, :], asum[:, :]).then_inc(s_dr, 1)

            def self_out(h):
                dve.wait_ge(s_dr, h + 1)
                dve.wait_ge(s_do, h + 1)
                for i in range(HALF):
                    b = HALF * h + i
                    dve.scalar_tensor_tensor(xres[:, b, :], MIX[:, i * T:(i + 1) * T], arec[:, i:i + 1], xres[:, b, :],
                                             ALU.mult, ALU.add).then_inc(s_out, 1)

            ln_stats(0)
            dve.wait_ge(s_fold, 2)
            dve.tensor_copy(brep[:, :, :].rearrange("p j (t c e) -> p (j t) c e", t=TILES, c=4),
                            OUT[:, 0:D].rearrange("p (g e) -> p g e", e=HD)[:, :, None, :].broadcast_to([128, 16, 4, HD])
                            ).then_inc(s_brep, 1)
            dve.tensor_copy(cvo[:, :], OUT[:, D:2 * D]).then_inc(s_cvo, 1)
            repeat_x(0)
            stack_x(0)
            stack_k(0)
            ln_stats(1)
            value_rest(0)
            value_rest(1)
            repeat_x(1)
            for n in range(UNITS):
                b, p = divmod(n, TILES)
                max_unit(n)
                if n:
                    prob_hi(n - 1)
                if p == 0 and b >= 2:
                    add_x1(b - 2)
                if p == 0 and b + 1 < B:
                    stack_x(b + 1)
                if p == 1 and b + 1 < B:
                    stack_k(b + 1)
                if p == 2 and b:
                    normalize_out(b - 1)
                if p == 3 and b + 2 < B:
                    repeat_x(b + 2)
                if n == 7:
                    masks()
                if n == 13:
                    mask_bias()
                if n in (15, 16):
                    take_vo(n - 15)
                if n == 18:
                    leaf_bias()
                if n == 19:
                    leaf_rows()
                if n == 20:
                    ln_stats(2)
                if n == 22:
                    normalize(2)
                if n == 23:
                    take_xnT(0)
                if n == 25:
                    gate_start(0)
                if n == 28:
                    gate_rest(0)
            prob_hi(UNITS - 1)
            add_x1(B - 2)
            take_gateT(0)
            for c in range(PAIRS):
                if c:
                    moe_gated(c)
                if c == 0:
                    normalize_out(B - 1)
                if c == 2:
                    add_x1(B - 1)
                    ln_stats(3)
                if c == 3:
                    normalize(3)
                if c == 4:
                    take_xnT(1)
                if c == 6:
                    gate_start(1)
                if c == 8:
                    gate_rest(1)
            take_gateT(1)
            for c in range(PAIRS):
                if c:
                    moe_gated(PAIRS + c)
                if c == 2:
                    add_x2(0)
                    ln_stats(4)
                if c == 4:
                    normalize(4)
                    take_xnT(2)
                if c == 5:
                    attn1_mask(0)
            for k in range(CUTS):
                w2_lo(k)
            add_x3(0)
            ln_stats(5)
            normalize(5)
            take_xnT(3)
            route(0)
            take_selT(0)
            for k in range(UPB):
                ffn_lo(k)
                if k == 2:
                    add_x2(1)
                if k == 3:
                    ln_stats(6)
                if k == 5:
                    normalize(6)
                if k == 6:
                    take_xnT(4)
                if k == 8:
                    attn1_mask(1)
                if k == 12:
                    add_x3(1)
                if k == 13:
                    ln_stats(7)
                if k == 15:
                    normalize(7)
                if k == 16:
                    take_xnT(5)
                if k == 18:
                    route(1)
                if k == 22:
                    take_selT(1)
            for k in range(UPB):
                ffn_lo(UPB + k)
                if k == 3:
                    self_v(0)
                    self_max(0)
                if k == 6:
                    self_rec(0)
                if k == 8:
                    self_out(0)
                if k == 20:
                    self_max(1)
            self_rec(1)
            self_v(1)
            self_out(1)

        @block.tensor
        def _(pe):
            def split_product(dst, w, x_, w_cols, first, last):
                (wh, wl), (x_hi, x_lo) = w, x_
                pe.matmul(dst, wl[:, w_cols], x_hi, start=first, stop=False)
                pe.matmul(dst, wh[:, w_cols], x_lo, start=False, stop=False)
                return pe.matmul(dst, wh[:, w_cols], x_hi, start=False, stop=last)

            def turn_x(b):
                pe.wait_ge(s_xrep, b + 1)
                if b >= 3:
                    pe.wait_ge(s_x1, b - 2)
                elif b:
                    pe.wait_ge(s_kst, b)
                rep = xrep[:, :, :, :].rearrange("t g c e -> t (g c e)")
                for j in range(BLOCKS):
                    last = pe.transpose(TA[:, j * T:(j + 1) * T], rep[:, j * 128:(j + 1) * 128], ident)
                last.then_inc(s_xraw, 1)

            def raise_k(b):
                pe.wait_ge(s_brep, 1)
                pe.wait_ge(s_xst, b + 1)
                for j in range(BLOCKS):
                    last = pe.matmul(TA[:, j * S2:(j + 1) * S2], brep[:, j, :], ctxT_sb[:, b * S2:(b + 1) * S2],
                                     start=True, stop=True)
                last.then_inc(s_kraw, 1)

            def keys(p, j, b):
                return kst[32 * p:32 * p + 32, b % 2, j, :]

            def queries(p, j, b):
                return xst[32 * p:32 * p + 32, b % 2, j, :]

            def scores(n):
                b, p = divmod(n, TILES)
                pe.wait_ge(s_xst, b + 1)
                pe.wait_ge(s_kst, b + 1)
                if n >= 2:
                    pe.wait_ge(s_nm, n - 1)
                for j in range(BLOCKS):
                    last = pe.matmul(SC[n % 2][:, j * S2:(j + 1) * S2], queries(p, j, b), keys(p, j, b), start=True, stop=True,
                                     tile_position=(32 * p, 0))
                last.then_inc(s_sc, 1)

            def scoresT(n):
                b, p = divmod(n, TILES)
                pe.wait_ge(s_nm, n + 1)
                if n >= 2:
                    pe.wait_ge(s_p, n - 1)
                for j in range(BLOCKS):
                    pe.matmul(SCT[n % 2][0:S2, j * T:(j + 1) * T], negmax[:, n % 4, j:j + 1].broadcast_to([T, S2]), idb[:, :],
                              start=(j == 0), stop=False, skip_group_check=True)
                for j in range(BLOCKS):
                    last = pe.matmul(SCT[n % 2][0:S2, j * T:(j + 1) * T], keys(p, j, b), queries(p, j, b),
                                     start=False, stop=True, tile_position=(32 * p, 0), skip_group_check=True)
                last.then_inc(s_sT, 1)

            def values(n):
                b, p = divmod(n, TILES)
                pe.wait_ge(s_ph, n + 1)
                pe.wait_ge(s_pl, n + 1)
                if n == 0:
                    pe.wait_ge(s_vp, 4)
                    pe.wait_ge(s_memset, 2)
                    pe.wait_ge(s_cvo, 1)
                if p == 0 and b:
                    pe.wait_ge(s_rd, 2 * b)
                for j in range(BLOCKS):
                    h = BLOCKS * j + p
                    dst = OUT[:, h * VCOLS:(h + 1) * VCOLS]
                    pe.matmul(dst, probl[:, n % 3, j * T:(j + 1) * T], vparts[:, b, h, :], start=True, stop=False)
                    last = pe.matmul(dst, probh[:, n % 3, j * T:(j + 1) * T], vparts[:, b, h, :], start=False, stop=True)
                last.then_inc(s_pv, 1)

            def turn_out(b):
                pe.wait_ge(s_on, b + 1)
                pe.wait_ge(s_kst, min(b + 3, B))
                pe.transpose(TA[:, 0:T], onorm[:, :], ident).then_inc(s_onp, 1)

            def project_out(b):
                pe.wait_ge(s_onT, b + 1)
                pe.matmul(TA[:, D:2 * D], onT[:, :], cvo[:, :], start=True, stop=True).then_inc(s_y0, 1)

            def context_product(i):
                h = i % 2
                if i >= 2:
                    pe.wait_ge(s_ckr, i - 1)
                lhsT, rhs = [(attnw_sb[:, 1, :], ctxT_sb), (attnw_sb[:, 2, :], ctxT_sb), (attnw_sb[:, 0, :], kT1),
                             (cols_sb[:, V_BQ:V_BQ + 1].broadcast_to([128, 128]), kT1)][i // 2]
                pe.matmul(CTX[h][:, 0:NK], lhsT, rhs[:, h * NK:(h + 1) * NK], start=True, stop=True).then_inc(s_ck, 1)

            def context_values(h):
                pe.wait_ge(s_ckr, 7 + h)
                for i in range(HALF):
                    b = HALF * h + i
                    last = pe.matmul(CTX[h][0:S2, i * D:(i + 1) * D], vT1[:, b * S2:(b + 1) * S2], attnw_sb[:, 3, :],
                                     start=True, stop=True)
                last.then_inc(s_ck, 1)

            def turn_xn(q):
                pe.wait_ge(s_xn, HALF * (q + 1))
                pe.wait_ge(*[(s_vo, 1), (s_x1, B), (s_xnT, 2), (s_aT, 1), (s_xnT, 4), (s_aT, 2)][q])
                for i in range(HALF):
                    last = pe.transpose((CTX[0] if q == 0 else TURN)[:, i * T:(i + 1) * T], xn[:, i, :], ident)
                last.then_inc(s_tp, 1)

            def logits(h):
                pe.wait_ge(s_xnT, h + 1)
                if h == 0:
                    pe.wait_ge(s_vo, 2)
                for i in range(HALF):
                    last = pe.matmul((CTX[1] if h == 0 else MIX)[:, i * EXPERTS:(i + 1) * EXPERTS], xnT[:, i * T:(i + 1) * T],
                                     router_sb[:, :], start=True, stop=True)
                last.then_inc(s_lg, 1)

            def gateT(h):
                pe.wait_ge(s_gp, h + 1)
                for i in range(HALF):
                    last = pe.transpose((CTX[1] if h == 0 else MIX)[0:48, :].bitcast(BF16)[:, i * T:(i + 1) * T],
                                        gparts[:, i, :, :].rearrange("t s e -> t (s e)"), idb[:, :])
                last.then_inc(s_gTp, 1)

            def moe_up(m):
                h, c = divmod(m, PAIRS)
                if c == 0:
                    pe.wait_ge(s_xl, h + 1)
                if m >= 2:
                    pe.wait_ge(s_ge, m - 1)
                split_product(UP[m % 2][:, :], (up0h, up0l), (xh[:, h, :], xl[:, h, :]), slice(c * 128, (c + 1) * 128), True, True
                              ).then_inc(s_up, 1)

            def moe_gate(m):
                r = m - m // PAIRS - 1
                if m % PAIRS == 1:
                    pe.wait_ge(s_gT, m // PAIRS + 1)
                if r >= 2:
                    pe.wait_ge(s_ga, r - 1)
                pe.matmul(GATE[r % 2][:, :], gsel_sb[:, m % PAIRS - 1, :], gT[:, m // PAIRS, :], start=True, stop=True
                          ).then_inc(s_gb, 1)

            def moe_down(m):
                h, c = divmod(m, PAIRS)
                pe.wait_ge(s_al, m + 1)
                if c == 0:
                    pe.wait_ge(*((s_yT, h) if h else (s_gT, 1)))
                split_product(ACC[:, :], (down0h, down0l), (acth[:, m % RING, :], actl[:, m % RING, :]),
                              slice(c * 128, (c + 1) * 128), c == 0, c == PAIRS - 1).then_inc(s_dn, 1)

            def turn_y(h):
                pe.wait_ge(s_yT, h + 1)
                pe.wait_ge(s_xnT, 2 * h + 2)
                for i in range(HALF):
                    last = pe.transpose(TURN[:, i * T:(i + 1) * T], yT[:, i * T:(i + 1) * T], ident)
                last.then_inc(s_yb, 1)

            def attn1_scores(h):
                pe.wait_ge(s_xnT, 3 + 2 * h)
                if h:
                    pe.wait_ge(s_selT, 1)
                for i in range(HALF):
                    b = HALF * h + i
                    last = pe.matmul(SIDE[:, i * S2:(i + 1) * S2], xnT[:, i * T:(i + 1) * T], aK[:, b * S2:(b + 1) * S2],
                                     start=True, stop=True)
                last.then_inc(s_as, 1)

            def attn1_pT(h):
                pe.wait_ge(s_ae, HALF * (h + 1))
                for i in range(HALF):
                    last = pe.transpose(TURN[0:S2, i * T:(i + 1) * T], aexp[:, i, 0:S2], ident)
                last.then_inc(s_apT, 1)

            def attn1_values(h):
                pe.wait_ge(s_aT, h + 1)
                pe.wait_ge(*((s_x3, HALF * h) if h else (s_gT, 2)))
                for i in range(HALF):
                    b = HALF * h + i
                    last = pe.matmul(MIX[:, i * T:(i + 1) * T], apT[0:S2, i, :], vo[:, b, :], start=True, stop=True)
                last.then_inc(s_av, 1)

            def node_scores(h):
                pe.wait_ge(s_xnT, 4 + 2 * h)
                pe.wait_ge(s_late, 32)
                pe.wait_ge(s_am, 4 * h + 1)
                for i in range(HALF):
                    last = pe.matmul(SIDE[:, i * NETS * NODES:(i + 1) * NETS * NODES], xnT[:, i * T:(i + 1) * T],
                                     nodew_sb[:, :], start=True, stop=True)
                last.then_inc(s_ns, 1)

            def turn_sel(h):
                pe.wait_ge(s_selrow, h + 1)
                pe.wait_ge(s_selzero, 1)
                for a in range(2):
                    for i in range(HALF):
                        last = pe.transpose(SIDE[:, :].bitcast(BF16)[:, a * NT + i * T:a * NT + (i + 1) * T],
                                            selrow[:, i, 2 * a:2 * a + 2, :, :].rearrange("t n s l -> t (n s l)"), idb[:, :])
                last.then_inc(s_selp, 1)

            def net_rows(net):
                return slice(SEL * (net % 2), SEL * (net % 2) + SEL), net // 2

            def ffn_up(m):
                h, k = divmod(m, UPB)
                net, c = divmod(k, CHUNKS)
                rows_, a = net_rows(net)
                if k == 0:
                    pe.wait_ge(s_xl, 3 + h)
                    pe.wait_ge(s_selT, h + 1)
                if m == 0:
                    pe.wait_ge(s_lo1, CUTS)
                    pe.wait_ge(s_lb, 10)
                    pe.wait_ge(s_ge, 2 * PAIRS)
                if m == 2:
                    pe.wait_ge(s_ga, 2 * (PAIRS - 1))
                if m >= 3:
                    pe.wait_ge(s_fl, m - 2)
                up_ = FUP[m % 3]
                split_product(up_[:, :], (w1h, w1l), (xh[:, h, :], xl[:, h, :]), slice(k * 128, (k + 1) * 128), True, False)
                pe.matmul(up_[:, :], lup[rows_, a, 2 * c:2 * c + 2, :].rearrange("r l e -> r (l e)"), selT[rows_, h, a, :],
                          start=False, stop=True).then_inc(s_fu, 1)

            def ffn_down(m):
                h, k = divmod(m, UPB)
                net, c = divmod(k, CHUNKS)
                j = NETS * h + net
                acc = FACC[j % 2]
                rows_, a = net_rows(net)
                pe.wait_ge(s_fl, m + 1)
                if m == 0:
                    pe.wait_ge(s_lo2, CUTS)
                if c == 0:
                    pe.wait_ge(*((s_qkv, j - 1) if j >= 2 else (s_yT, 2) if j == 0 else (s_ga, 2 * (PAIRS - 1))))
                split_product(acc[:, :], (w2h, w2l), (acth[:, m % RING, :], actl[:, m % RING, :]), slice(k * 128, (k + 1) * 128),
                              c == 0, False).then_inc(s_fd, 1)
                if c == CHUNKS - 1:
                    pe.matmul(acc[:, :], ldown[rows_, a, :], selT[rows_, h, a, :], start=False, stop=True).then_inc(s_net, 1)

            def self_turn_v(h):
                pe.wait_ge(s_qkv, NETS * (h + 1))
                pe.wait_ge(*((s_dT, 2) if h else (s_xnT, 6)))
                for i in range(HALF):
                    last = pe.transpose(TURN[:, i * T:(i + 1) * T], qkvT[:, 2, i * T:(i + 1) * T], ident)
                last.then_inc(s_vb, 1)

            def self_scores(h):
                pe.wait_ge(s_qkv, NETS * h + 2)
                pe.wait_ge(*((s_de, HALF) if h else (s_selT, 2)))
                for i in range(HALF):
                    last = pe.matmul(SIDE[:, i * T:(i + 1) * T], qkvT[:, 0, i * T:(i + 1) * T], qkvT[:, 1, i * T:(i + 1) * T],
                                     start=True, stop=True)
                last.then_inc(s_ds, 1)

            def self_pT(h):
                pe.wait_ge(s_de, HALF * (h + 1))
                pe.wait_ge(s_vn, 1)
                for i in range(HALF):
                    last = pe.transpose(TURN[:, i * T:(i + 1) * T], aexp[:, i, :], ident)
                last.then_inc(s_dpT, 1)

            def self_values(h):
                pe.wait_ge(s_dT, h + 1)
                pe.wait_ge(s_vn, h + 1)
                pe.wait_ge(*((s_out, HALF) if h else (s_x3, B)))
                for i in range(HALF):
                    last = pe.matmul(MIX[:, i * T:(i + 1) * T], apT[:, i, :], vnat[:, i, :], start=True, stop=True)
                last.then_inc(s_do, 1)

            pe.wait_ge(s_early, 16 * 4)
            pe.matmul(OUT[:, 0:D], blockw_sb[:, 1, :], blockw_sb[:, 0, :], start=True, stop=True).then_inc(s_fold, 1)
            pe.matmul(OUT[:, D:2 * D], blockw_sb[:, 2, :], woT_sb[:, :], start=True, stop=True).then_inc(s_fold, 1)
            turn_x(0)
            raise_k(0)
            scores(0)
            pe.wait_ge(s_idb, 1)
            for n in range(UNITS):
                b, p = divmod(n, TILES)
                if p == 0 and b >= 2:
                    project_out(b - 2)
                if p == 0 and b + 1 < B:
                    turn_x(b + 1)
                if p == 1 and b + 1 < B:
                    raise_k(b + 1)
                if n + 1 < UNITS:
                    scores(n + 1)
                scoresT(n)
                if n >= 2:
                    values(n - 2)
                if p == 3 and b:
                    turn_out(b - 1)
                if n == 4:
                    pe.wait_ge(s_mid, 16 * 6)
                if 4 <= n < 12:
                    context_product(n - 4)
                if n in (13, 14):
                    context_values(n - 13)
                if n == 23:
                    turn_xn(0)
                if n == 25:
                    logits(0)
                if n == 31:
                    gateT(0)
            project_out(B - 2)

            pe.wait_ge(s_lo0, 2)
            pe.wait_ge(s_nm, UNITS)
            pe.wait_ge(s_p, UNITS)
            for c in range(PAIRS + LAG):
                if c < PAIRS:
                    moe_up(c)
                    if c:
                        moe_gate(c)
                if c < 2:
                    values(UNITS - 2 + c)
                if c == 2:
                    turn_out(B - 1)
                if c == 3:
                    project_out(B - 1)
                if c == 5:
                    turn_xn(1)
                if c == 6:
                    logits(1)
                if c == 10:
                    gateT(1)
                if c >= LAG:
                    moe_down(c - LAG)

            for c in range(PAIRS + LAG):
                m = PAIRS + c
                if c < PAIRS:
                    moe_up(m)
                    if c == 1:
                        turn_y(0)
                    if c:
                        moe_gate(m)
                if c >= LAG:
                    moe_down(m - LAG)
                if c == 4:
                    turn_xn(2)
                if c == 5:
                    attn1_scores(0)
                if c == 8:
                    attn1_pT(0)
                if c == 10:
                    attn1_values(0)
            turn_xn(3)
            node_scores(0)
            turn_sel(0)

            for k in range(UPB + LAG):
                if k == 2:
                    turn_y(1)
                if k < UPB:
                    ffn_up(k)
                if k >= LAG:
                    ffn_down(k - LAG)
                if k == 6:
                    turn_xn(4)
                if k == 8:
                    attn1_scores(1)
                if k == 10:
                    attn1_pT(1)
                if k == 12:
                    attn1_values(1)
                if k == 16:
                    turn_xn(5)
                if k == 17:
                    node_scores(1)
                if k == 21:
                    turn_sel(1)

            for k in range(UPB + LAG):
                m = UPB + k
                if k < UPB:
                    ffn_up(m)
                if k >= LAG:
                    ffn_down(m - LAG)
                if k == 3:
                    self_turn_v(0)
                    self_scores(0)
                if k == 6:
                    self_pT(0)
                if k == 8:
                    self_values(0)
                if k == 20:
                    self_scores(1)
                if k == 25:
                    self_pT(1)
            self_turn_v(1)
            self_values(1)


def _constants():
    import numpy as np
    row = np.arange(128)
    kind = (row // HD) % 4
    c = np.zeros((128, C_END), np.float32)
    c[:, C_ID:C_ID + 128] = np.eye(128)
    x_lo, k_lo = kind >= 2, kind % 2 == 1
    c[:, C_SX], c[:, C_BX] = np.where(x_lo, -1, 1), x_lo
    c[:, C_SK], c[:, C_BK] = np.where(k_lo, -1, 1), k_lo
    group = (row % SEL) // LEAVES
    c[:, C_PART] = group <= 1
    c[:, C_PART + 1] = group == 2
    c[:, C_PART + 2] = group == 3
    c[:, C_LEAF:C_LEAF + LEAVES] = (row % LEAVES)[:, None] == np.arange(LEAVES)[None, :]
    g = np.zeros((48, PAIRS - 1, 2, 64), np.float32)
    for e in range(EXPERTS):
        g[e::EXPERTS, e // 2, e % 2, :] = 1
    return c, g.reshape(48, PAIRS - 1, 128)


def _layout(a):
    import numpy as np
    f = {n: np.asarray(v) for n, v in a.items()}
    consts, gsel = _constants()
    blockw = np.zeros((128, 3, 128), np.float32)
    for h in range(HEADS):
        s = slice(h * HD, (h + 1) * HD)
        for k, n in enumerate(("Wq", "Wk", "Wv")):
            blockw[s, k, s] = f["L0_xattn_" + n]
    up = np.concatenate([f["L0_ffn_shared_up"], f["L0_ffn_routed_up"]])
    down = np.concatenate([f["L0_ffn_shared_down"], f["L0_ffn_routed_down"]])
    w1 = np.stack([f[f"L1_ffn_{n}_w1"] for n in "qkv"])
    w2 = np.stack([f[f"L1_ffn_{n}_w2"] for n in "qkv"])
    leafb = np.zeros((4, 4, LEAVES, 192), np.float32)
    leafb[:, 0, :, 0:64] = -BIG
    for j, n in enumerate("qkv"):
        leafb[j, 1:, :, 0:64] = f[f"L1_ffn_{n}_b1"]
        leafb[j, 1:, :, 64:] = f[f"L1_ffn_{n}_b2"]
    arrays = {
        "x": f["x"], "ctx": f["ctx_1024"],
        "ctxT": f["ctx_1024"].transpose(2, 0, 1).reshape(D, B * S2),
        "mask": f["mask_BxS2_bk0"].reshape(1, B * S2),
        "consts": consts, "gsel": gsel, "blockw": blockw,
        "woT": f["L0_xattn_Wo"].T,
        "up0": up.transpose(2, 0, 1).reshape(D, PAIRS * 128),
        "down0": down.transpose(0, 2, 1).reshape(PAIRS, 128, D).transpose(1, 0, 2).reshape(128, PAIRS * D),
        "router": f["L0_ffn_router_w"].T,
        "attnw": np.stack([f["L1_xattn_Wq"].T, f["L1_xattn_Wk"], f["L1_xattn_Wv"], f["L1_xattn_Wo"]], 1),
        "cols": np.stack([f["L1_xattn_bk"], f["L1_xattn_bv"], f["L1_xattn_bq"]], 1),
        "rows": np.concatenate([f["L0_xattn_bo"], f["L1_xattn_bo"]] + [f[f"L1_ffn_{n}_node_b"] for n in "qkv"])[None],
        "w1": w1.transpose(2, 0, 1, 3).reshape(D, UPB * 128),
        "w2": w2.reshape(NETS * CHUNKS, 128, D).transpose(1, 0, 2).reshape(128, UPB * D),
        "nodew": np.concatenate([f[f"L1_ffn_{n}_node_w"] for n in "qkv"]).T,
        "leafb": leafb.reshape(2, 128, 192).transpose(1, 0, 2),
    }
    return {n: np.ascontiguousarray(v) for n, v in arrays.items()}


def kernel(**inputs):
    import numpy as _np
    import concourse.bacc as _bacc
    from concourse import mybir as _mybir
    from concourse.bass_utils import run_bass_kernel_spmd as _run

    nc = _bacc.Bacc("TRN2", target_bir_lowering=False, num_devices=1)
    arrays, args = {}, []
    for name, a in _layout(inputs).items():
        arrays[f"in_{name}_dram"] = a
        args.append(nc.dram_tensor(f"in_{name}_dram", a.shape, _mybir.dt.from_np(a.dtype), kind="ExternalInput").ap())
    args.append(nc.dram_tensor("out_0_dram", (B, T, D), _mybir.dt.from_np(_np.dtype("float32")), kind="ExternalOutput").ap())
    build(nc, *args)
    r = _run(nc, [arrays], core_ids=[0])
    return r.results[0]["out_0_dram"]
```

```python
from contextlib import ExitStack

import concourse.bass as bass
from concourse import mybir

F32 = mybir.dt.float32
F32R = mybir.dt.float32r
F16 = mybir.dt.float16
BF16 = mybir.dt.bfloat16
U8 = mybir.dt.uint8
ALU = mybir.AluOpType
ACT = mybir.ActivationFunctionType
AX = mybir.AxisListType

B, T, D = 8, 128, 128
S2 = 120
HEADS, HD = 16, 8
BLOCKS, TILES = 4, 4
HALF = B // 2
NT = HALF * T
NK = HALF * S2
UNITS = B * TILES
VCOLS = 3 * HD + 1
EXPERTS, TOPK, PAIRS = 16, 4, 9
NETS, LEAVES, NODES, CHUNKS = 3, 16, 15, 8
UPB = NETS * CHUNKS
SEL = 64
EPS = 1e-5
SCALE = float(D) ** -0.5
NEG = -1e9
WARM0, WARM1 = 12, 12
RING = 4
LAG0, LAG = 3, 2
CUTS, CUT = 6, 512
CUTS0, CUT0 = 3, 384
BIG = 2.0 ** 100

NORMS = ((0, 0), (0, 1), (1, 0), (1, 1), (2, 0), (3, 0), (2, 1), (3, 1))

C_ID, C_SX, C_BX, C_SK, C_BK, C_PART, C_LEAF, C_END = 0, 128, 129, 130, 131, 132, 135, 151
V_BK, V_BV, V_BQ, V_END = 0, 1, 2, 3
R_BO0, R_BO1, R_NB, R_END = 0, 128, 256, 256 + NETS * NODES


def build(nc: bass.Bass, x, ctx, ctxT, mask, consts, gsel, blockw, woT, up0, down0, router,
          attnw, cols, rows, w1, w2, nodew, leafb, out):
    stack = ExitStack()
    with stack:
        def sb(name, shape, dt=F32):
            return stack.enter_context(nc.sbuf_tensor(name, shape, dt))

        def sem(name):
            return stack.enter_context(nc.semaphore(name))

        bank = [stack.enter_context(nc.psum_tensor(f"bank{i}", [128, 512], F32)) for i in range(8)]
        TA, OUT = bank[0], bank[1]
        SC, SCT = (bank[2], bank[4]), (bank[3], bank[5])
        SIDE0, OTURN = bank[6], bank[7]
        UP, GATE, ACC = (bank[4], bank[5]), (bank[6], bank[3]), bank[7]
        FUP, FACC = bank[4:7], (bank[7], bank[3])
        TURN, SIDE, MIX = bank[0], bank[1], bank[2]

        c_sb = sb("c_sb", [128, C_END])
        ident = c_sb[:, C_ID:C_ID + 128]
        idb = sb("idb", [128, 128], BF16)
        gsel_sb = sb("gsel_sb", [48, PAIRS - 1, 128], BF16)
        x0 = sb("x0", [T, B, D])
        ctx_sb = sb("ctx_sb", [S2, B, D])
        ctxT_sb = sb("ctxT_sb", [D, B * S2])
        blockw_sb = sb("blockw_sb", [128, 3, 128])
        woT_sb = sb("woT_sb", [128, 128])
        staged = sb("staged", [128, UPB * 128])
        router_sb = sb("router_sb", [128, EXPERTS])
        attnw_sb = sb("attnw_sb", [128, 4, 128])
        cols_sb = sb("cols_sb", [128, V_END])
        rows_sb = sb("rows_sb", [128, R_END])
        mask_u8 = sb("mask_u8", [128, B * S2], U8)
        nodew_sb = sb("nodew_sb", [128, NETS * NODES])
        leafb_sb = sb("leafb_sb", [128, 2, 64 + 128])

        up0h, up0l = sb("up0h", [128, PAIRS * 128], F32R), sb("up0l", [128, PAIRS * 128], F32R)
        down0h, down0l = sb("down0h", [128, PAIRS * 128], F32R), sb("down0l", [128, PAIRS * 128], F32R)
        w1h, w1l = sb("w1h", [128, UPB * 128], F32R), sb("w1l", [128, UPB * 128], F32R)
        w2h, w2l = sb("w2h", [128, UPB * 128], F32R), sb("w2l", [128, UPB * 128], F32R)
        W0 = PAIRS * 128
        UP0, DOWN0 = slice(0, W0), slice(W0, 2 * W0)

        xres = sb("xres", [T, B, D])
        xs = [x0, xres, xres, xres]
        stats = sb("stats", [T, HALF, 6])
        meanvar = sb("meanvar", [T, len(NORMS), HALF, 2])
        vareps = sb("vareps", [T, len(NORMS), HALF])
        rstd = sb("rstd", [T, len(NORMS), HALF])
        minushalf = sb("minushalf", [T, HALF])
        xn = sb("xn", [T, HALF, D])
        xnT = sb("xnT", [D, NT])
        xh, xl = sb("xh", [D, 2, NT], F32R), sb("xl", [D, 2, NT], F32R)

        brep = sb("brep", [128, BLOCKS, 128])
        cvo = sb("cvo", [128, 128])
        xrep = sb("xrep", [T, BLOCKS * TILES, 4, HD])
        acth, actl = sb("acth", [128, RING, NT], F32R), sb("actl", [128, RING, NT], F32R)
        yT = sb("yT", [D, NT])
        usplit = yT[:, :].bitcast(F16).rearrange("p (i t) -> p i t", i=2)
        kst = sb("kst", [128, 2, BLOCKS, S2], F16)
        xst = sb("xst", [128, 2, BLOCKS, T], F16)
        vparts = sb("vparts", [S2, B, HEADS, VCOLS], BF16)
        negmax = sb("negmax", [T, 4, BLOCKS], BF16)
        probs_buf = sb("probs_buf", [128, 3, BLOCKS * T])
        probT = probs_buf[0:S2, :, :]
        probh, probl = sb("probh", [S2, 3, BLOCKS * T], F16), sb("probl", [S2, 3, BLOCKS * T], F16)
        rden = sb("rden", [T, HEADS])
        osum = sb("osum", [T, D])
        onorm = sb("onorm", [T, D])
        onT = sb("onT", [D, T])

        lmax = sb("lmax", [T, HALF])
        lshift = sb("lshift", [T, HALF, EXPERTS])
        lexp = sb("lexp", [T, HALF, EXPERTS])
        lsum = sb("lsum", [T, HALF])
        lrec = sb("lrec", [T, HALF])
        probs = sb("probs", [T, HALF, EXPERTS])
        top8 = sb("top8", [T, HALF, 8])
        rest = sb("rest", [T, HALF, EXPERTS])
        gate = sb("gate", [T, HALF, EXPERTS])
        gres = sb("gres", [T, HALF, EXPERTS])
        gparts = sb("gparts", [T, HALF, 3, EXPERTS], BF16)
        gT = sb("gT", [48, 2, NT], BF16)
        shared = sb("shared", [128, 8 * NT])
        gated = shared[:, 0:RING * NT].rearrange("p (i t) -> p i t", i=RING)
        gelu = shared[:, 6 * NT:8 * NT].rearrange("p (i t) -> p i t", i=2)
        gsel_f32 = shared[0:48, 6 * NT:8 * NT].rearrange("p (c m) -> p c m", c=PAIRS - 1)
        maskf, kT1, vT1, cB = (shared[:, i * B * S2:(i + 1) * B * S2] for i in range(4))
        qkvT = shared[:, 0:NETS * NT].rearrange("p (n t) -> p n t", n=NETS)
        vnat = shared[:, NETS * NT:(NETS + 1) * NT].rearrange("p (b d) -> p b d", b=HALF)

        mscale = sb("mscale", [128, B * S2])
        mneg = maskf
        aK = sb("aK", [128, B * S2])
        cmask = sb("cmask", [128, B * S2])
        vo = ctx_sb
        aexp = probs_buf[:, 0, :].rearrange("t (b k) -> t b k", b=HALF)
        apT = probs_buf[:, 1, :].rearrange("t (b k) -> t b k", b=HALF)
        sc1 = probs_buf[:, 2, 0:NK]
        sc2 = sb("sc2", [T, NK])
        amax = sb("amax", [T, HALF])
        asum = sb("asum", [T, HALF])
        arec = sb("arec", [T, HALF])

        sres = shared[:, 4 * NT + 576:4 * NT + 960].rearrange("p (a n) -> p a n", a=2)
        spart = shared[:, 4 * NT:4 * NT + 576].bitcast(BF16).rearrange("p (s a n) -> p s a n", s=3, a=2)
        scomb = xrep[:, 0:12, :, :].rearrange("p g c e -> p (g c e)").rearrange("p (a n) -> p a n", a=2)
        lup = sb("lup", [128, 2, LEAVES, 64], BF16)
        ldown = sb("ldown", [128, 2, 128], BF16)
        nscore = sb("nscore", [T, HALF, NETS * NODES])
        right = sb("right", [T, HALF * NETS, NODES])
        lev = [None, sb("lev1", [T, HALF * NETS, 2]), sb("lev2", [T, HALF * NETS, 4]),
               sb("lev3", [T, HALF * NETS, 8]), sb("lev4", [T, HALF * NETS, 16])]
        selrow = sb("selrow", [T, HALF, 4, 4, LEAVES], BF16)
        selT = shared[:, 4 * NT:6 * NT].bitcast(BF16).rearrange("p (h a t) -> p h a t", h=2, a=2)
        dmax = sb("dmax", [T, HALF])

        s_early, s_x, s_ctx, s_mid = sem("early_loaded"), sem("x_loaded"), sem("ctx_loaded"), sem("mid_loaded")
        s_w0, s_w1, s_w2 = sem("w0_loaded"), sem("w1_loaded"), sem("w2_loaded")
        s_late, s_stored = sem("late_loaded"), sem("stored")
        s_idb, s_gsel, s_memset, s_selzero, s_zero = (
            sem("idb_ready"), sem("gsel_ready"), sem("memset_done"), sem("selrow_zeroed"), sem("zeros_ready"))
        s_fold, s_brep, s_cvo = sem("folded"), sem("brep_ready"), sem("cvo_ready")
        s_kraw, s_ksign, s_kst = sem("k_stack_raw"), sem("k_signed"), sem("k_stack")
        s_stats, s_mv, s_ve, s_rstd, s_xn = sem("stats"), sem("meanvar"), sem("vareps"), sem("rstd"), sem("xn")
        s_xrep, s_xraw, s_xsign, s_xst = sem("xrep"), sem("x_stack_raw"), sem("x_signed"), sem("x_stack")
        s_vp, s_xbo = sem("value_parts"), sem("xbo")
        s_sc, s_nm, s_sT, s_p, s_ph, s_pl, s_pv = (
            sem("scores"), sem("negmax"), sem("scoresT"), sem("probT"), sem("prob_hi"), sem("prob_lo"), sem("pv"))
        s_rd, s_on, s_onp, s_onT, s_y0, s_x1 = (
            sem("out_step"), sem("onorm"), sem("onT_psum"), sem("onT"), sem("attn0_out"), sem("x1"))
        s_hi0, s_lo0, s_hi1, s_lo1, s_hi2, s_lo2 = (
            sem("w0_hi"), sem("w0_lo"), sem("w1_hi"), sem("w1_lo"), sem("w2_hi"), sem("w2_lo"))
        s_tp, s_xnT, s_xh, s_xl = sem("xn_transposed"), sem("xnT"), sem("xh"), sem("xl")
        s_lg, s_lsh, s_lex, s_gstep, s_gp, s_gTp, s_gT = (
            sem("logits"), sem("logits_shifted"), sem("logits_exp"), sem("gate_step"), sem("gate_parts"),
            sem("gateT_psum"), sem("gateT"))
        s_up, s_gb, s_ge, s_ga, s_ah, s_al, s_dn = (
            sem("moe_up"), sem("gate_spread"), sem("gelu"), sem("gated"), sem("act_hi"), sem("act_lo"), sem("moe_down"))
        s_yT, s_yb, s_x2 = sem("moe_yT"), sem("moe_y"), sem("x2")
        s_ck, s_ckr, s_vo, s_mk = sem("ctx_product"), sem("ctx_product_read"), sem("vo_ready"), sem("mask_step")
        s_as, s_am, s_ae, s_apT, s_aT, s_av, s_x3 = (
            sem("attn1_scores"), sem("attn1_step"), sem("attn1_exp"), sem("attn1_pT_psum"), sem("attn1_pT"),
            sem("attn1_out"), sem("x3"))
        s_lb, s_ns, s_tree, s_selrow, s_selp, s_selT = (
            sem("leaf_bias_step"), sem("node_scores"), sem("tree_step"), sem("selrow"), sem("selT_psum"), sem("selT"))
        s_fu, s_fh, s_fl, s_fd, s_net, s_qkv = (
            sem("ffn_up"), sem("ffn_hi"), sem("ffn_lo"), sem("ffn_down"), sem("net_out"), sem("net_taken"))
        s_vb, s_vn, s_ds, s_dm, s_de, s_dpT, s_dT, s_do, s_dr, s_out = (
            sem("v_back"), sem("v_rows"), sem("self_scores"), sem("self_step"), sem("self_exp"), sem("self_pT_psum"),
            sem("self_pT"), sem("self_out"), sem("self_rec"), sem("out_ready"))

        def key_bank(b):
            return TA if b else OTURN

        def out_bank(b):
            return OUT if b % 2 else OTURN

        block = stack.enter_context(nc.Block())

        @block.sync
        def _(sp):
            sp.dma_start(blockw_sb[:, :, :], blockw).then_inc(s_early, 16)
            sp.dma_start(c_sb[:, :], consts).then_inc(s_early, 16)
            sp.dma_start(ctxT_sb[:, :], ctxT).then_inc(s_early, 16)
            sp.dma_start(woT_sb[:, :], woT).then_inc(s_early, 16)
            sp.dma_start(ctx_sb[:, :, :], ctx.rearrange("b s d -> s b d")).then_inc(s_ctx, 16)
            sp.dma_start(staged[:, UP0], up0).then_inc(s_w0, 16)
            sp.dma_start(staged[:, DOWN0], down0).then_inc(s_w0, 16)
            sp.wait_ge(s_lo0, 2 * CUTS0)
            sp.dma_start(staged[:, :], w1).then_inc(s_w1, 16)
            sp.wait_ge(s_lo1, CUTS)
            sp.dma_start(staged[:, :], w2).then_inc(s_w2, 16)
            for b in range(B):
                sp.wait_ge(s_out, b + 1)
                sp.dma_start(out[b, :, :], xres[:, b, :]).then_inc(s_stored, 16)
            sp.wait_ge(s_stored, 16 * B)

        @block.gpsimd
        def _(pool):
            def reciprocal_deviation(k):
                pool.wait_ge(s_ve, k + 1)
                pool.tensor_tensor(rstd[:, k, :], vareps[:, k, :], minushalf[:, :], ALU.pow).then_inc(s_rstd, 1)

            def prob_lo(n):
                pool.wait_ge(s_ph, n + 1)
                if n >= 3:
                    pool.wait_ge(s_pv, n - 2)
                pool.tensor_tensor(probl[:, n % 3, :], probT[:, n % 3, :], probh[:, n % 3, :], ALU.subtract).then_inc(s_pl, 1)

            def xlo(k):
                pool.wait_ge(s_xh, k + 1)
                pool.tensor_tensor(xl[:, k % 2, :], xnT[:, :], xh[:, k % 2, :].bitcast(F32), ALU.subtract).then_inc(s_xl, 1)

            def moe_lo(m):
                pool.wait_ge(s_ah, m + 1)
                if m >= RING:
                    pool.wait_ge(s_dn, m - RING + 1)
                src = gated[:, m % RING, :] if m % PAIRS else gelu[:, m % 2, :]
                pool.tensor_tensor(actl[:, m % RING, :], src, acth[:, m % RING, :].bitcast(F32), ALU.subtract
                                   ).then_inc(s_al, 1)

            def w2_lo(k):
                pool.wait_ge(s_hi2, k + 1)
                c = slice(k * CUT, (k + 1) * CUT)
                pool.tensor_tensor(w2l[:, c], staged[:, c], w2h[:, c].bitcast(F32), ALU.subtract).then_inc(s_lo2, 1)

            pool.memset(minushalf[:, :], -0.5).then_inc(s_memset, 1)
            pool.memset(vparts[:, :, :, 3 * HD:VCOLS], 1.0).then_inc(s_memset, 1)
            pool.memset(selrow[:, :, 3, :, :], 0.0).then_inc(s_selzero, 1)
            pool.wait_ge(s_memset, 1)
            reciprocal_deviation(0)
            pool.wait_ge(s_early, 16 * 4)
            pool.tensor_copy(idb[:, :], ident).then_inc(s_idb, 1)
            reciprocal_deviation(1)
            for n in range(UNITS):
                prob_lo(n)
                if 4 <= n < 4 + 2 * CUTS0:
                    k = n - 4
                    lo, hi = (up0l, down0l)[k // CUTS0], (up0h, down0h)[k // CUTS0]
                    c = slice(k % CUTS0 * CUT0, (k % CUTS0 + 1) * CUT0)
                    pool.wait_ge(s_hi0, k + 1)
                    pool.tensor_tensor(lo[:, c], staged[:, k * CUT0:(k + 1) * CUT0], hi[:, c].bitcast(F32), ALU.subtract
                                       ).then_inc(s_lo0, 1)
                if 15 <= n < 15 + CUTS:
                    k = n - 15
                    pool.wait_ge(s_hi1, k + 1)
                    c = slice(k * CUT, (k + 1) * CUT)
                    pool.tensor_tensor(w1l[:, c], staged[:, c], w1h[:, c].bitcast(F32), ALU.subtract).then_inc(s_lo1, 1)
                if n == 23:
                    reciprocal_deviation(2)
                if n == 27:
                    xlo(0)
            for m in range(2 * PAIRS):
                if m == PAIRS:
                    reciprocal_deviation(4)
                moe_lo(m)
                if m == 2:
                    reciprocal_deviation(3)
                if m == PAIRS - 1:
                    xlo(1)
                if m == PAIRS + 3:
                    reciprocal_deviation(5)
                if m == PAIRS + 7:
                    xlo(2)
            w2_lo(0)
            w2_lo(1)
            reciprocal_deviation(6)
            w2_lo(2)
            w2_lo(3)
            w2_lo(4)
            reciprocal_deviation(7)
            w2_lo(5)
            xlo(3)

        @block.scalar
        def _(act):
            act.dma_start(x0[:, :, :], x.rearrange("b t d -> t b d")).then_inc(s_x, 16)
            act.dma_start(rows_sb[:, :], rows.broadcast_to([128, R_END])).then_inc(s_mid, 16)
            act.dma_start(router_sb[:, :], router).then_inc(s_mid, 16)
            act.dma_start(attnw_sb[:, :, :], attnw).then_inc(s_mid, 16)
            act.dma_start(cols_sb[:, :], cols).then_inc(s_mid, 16)
            act.dma_start(mask_u8[:, :], mask.broadcast_to([128, B * S2])).then_inc(s_mid, 16)
            act.dma_start(gsel_f32, gsel).then_inc(s_mid, 16)
            act.dma_start(nodew_sb[:, :], nodew).then_inc(s_late, 16)
            act.dma_start(leafb_sb[:, :, :], leafb).then_inc(s_late, 16)

            def sign_x(b):
                act.wait_ge(s_xraw, b + 1)
                if b:
                    act.wait_ge(s_xst, b)
                act.activation(usplit[:, 0, :], TA[:, :], ACT.Identity, scale=c_sb[:, C_SX:C_SX + 1]).then_inc(s_xsign, 1)

            def sign_k(b):
                act.wait_ge(s_kraw, b + 1)
                if b:
                    act.wait_ge(s_kst, b)
                act.activation(usplit[:, 1, 0:BLOCKS * S2], key_bank(b)[:, 0:BLOCKS * S2], ACT.Identity, scale=c_sb[:, C_SK:C_SK + 1]
                               ).then_inc(s_ksign, 1)

            def value_part(k):
                act.wait_ge(s_ctx, 16)
                if k:
                    act.wait_ge(s_vp, 2)
                src = ctx_sb if k == 0 else shared[0:S2, 4 * NT:6 * NT].rearrange("s (b d) -> s b d", b=B)
                act.activation(vparts[:, :, :, k * HD:(k + 1) * HD].rearrange("s b h e -> s (b h) e"),
                               src[:, :, :].rearrange("s b (h e) -> s (b h) e", e=HD), ACT.Copy).then_inc(s_vp, 1)

            def exp_unit(n):
                act.wait_ge(s_sT, n + 1)
                if n >= 3:
                    act.wait_ge(s_pl, n - 2)
                act.activation(probT[:, n % 3, :], SCT[n % 2][0:S2, :], ACT.Exp, scale=SCALE).then_inc(s_p, 1)

            def prob_hi(n):
                act.wait_ge(s_p, n + 1)
                if n >= 3:
                    act.wait_ge(s_pv, n - 2)
                act.activation(probh[:, n % 3, :], probT[:, n % 3, :], ACT.Copy).then_inc(s_ph, 1)

            def turn_out(b):
                act.wait_ge(s_onp, b + 1)
                if b:
                    act.wait_ge(s_y0, b)
                act.activation(onT[:, :], out_bank(b)[:, 0:T], ACT.Copy).then_inc(s_onT, 1)

            def context_product(i):
                act.wait_ge(s_ck, i + 1)
                if i == 0:
                    act.wait_ge(s_gsel, 1)
                    act.wait_ge(s_vp, 4)
                dst, bias = [(kT1, V_BK), (vT1, V_BV), (aK, None), (cB, None)][i // 2]
                h = i % 2
                kw = {} if bias is None else {"bias": cols_sb[:, bias:bias + 1]}
                act.activation(dst[:, h * NK:(h + 1) * NK], SIDE0[:, 0:NK], ACT.Identity, **kw).then_inc(s_ckr, 1)

            def split_x(k):
                q = (0, 1, 3, 5)[k]
                act.wait_ge(s_xnT, q + 1)
                if k >= 2:
                    act.wait_ge(s_up, PAIRS * (k - 1))
                act.activation(xh[:, k % 2, :], xnT[:, :], ACT.Copy).then_inc(s_xh, 1)

            def exp_logits(h):
                act.wait_ge(s_lsh, h + 1)
                act.activation(lexp[:, :, :], lshift[:, :, :], ACT.Exp).then_inc(s_lex, 1)

            def w0_hi(k):
                if k == 0:
                    act.wait_ge(s_w0, 32)
                hi, c = (up0h, down0h)[k // CUTS0], slice(k % CUTS0 * CUT0, (k % CUTS0 + 1) * CUT0)
                act.activation(hi[:, c], staged[:, k * CUT0:(k + 1) * CUT0], ACT.Copy).then_inc(s_hi0, 1)

            def w1_hi(k):
                if k == 0:
                    act.wait_ge(s_w1, 16)
                c = slice(k * CUT, (k + 1) * CUT)
                act.activation(w1h[:, c], staged[:, c], ACT.Copy).then_inc(s_hi1, 1)

            def w2_hi(k):
                if k == 0:
                    act.wait_ge(s_w2, 16)
                c = slice(k * CUT, (k + 1) * CUT)
                act.activation(w2h[:, c], staged[:, c], ACT.Copy).then_inc(s_hi2, 1)

            value_part(0)
            sign_k(0)
            sign_x(0)
            value_part(1)
            for n in range(UNITS):
                b, p = divmod(n, TILES)
                if n == 0:
                    sign_x(1)
                if p == 3 and b + 2 < B:
                    sign_x(b + 2)
                if p == 1 and b + 1 < B:
                    sign_k(b + 1)
                exp_unit(n)
                prob_hi(n)
                if p == 0 and b >= 2:
                    turn_out(b - 2)
                if 2 <= n < 2 + 2 * CUTS0:
                    w0_hi(n - 2)
                if 14 <= n < 14 + CUTS:
                    w1_hi(n - 14)
                if n in range(4, 20, 2):
                    context_product((n - 4) // 2)
                if n == 27:
                    split_x(0)
                if n == 29:
                    exp_logits(0)
            turn_out(B - 2)

            def moe_hi(m):
                if m % PAIRS:
                    act.wait_ge(s_ga, m - m // PAIRS)
                else:
                    act.wait_ge(s_ge, m + 1)
                if m >= RING:
                    act.wait_ge(s_dn, m - RING + 1)
                src = gated[:, m % RING, :] if m % PAIRS else gelu[:, m % 2, :]
                act.activation(acth[:, m % RING, :], src, ACT.Copy).then_inc(s_ah, 1)

            def moe_gelu(m):
                act.wait_ge(s_up, m + 1)
                if m == 0:
                    act.wait_ge(s_mk, 4)
                if m >= 2 and (m - 2) % PAIRS:
                    act.wait_ge(s_ga, m - 2 - (m - 2) // PAIRS)
                elif m >= 2:
                    act.wait_ge(s_al, m - 1)
                act.activation(gelu[:, m % 2, :], UP[m % 2][:, :], ACT.Gelu).then_inc(s_ge, 1)

            def take_y(h):
                act.wait_ge(s_dn, PAIRS * (h + 1))
                if h:
                    act.wait_ge(s_yb, h)
                act.activation(yT[:, :], ACC[:, :], ACT.Copy).then_inc(s_yT, 1)

            def attn1_exp(h):
                act.wait_ge(s_am, 4 * h + 3)
                if h:
                    act.wait_ge(s_apT, h)
                for i in range(HALF):
                    act.activation(aexp[:, i, 0:S2], sc2[:, i * S2:(i + 1) * S2], ACT.Exp, bias=amax[:, i:i + 1],
                                   accum_out=asum[:, i:i + 1]).then_inc(s_ae, 1)

            def attn1_pT(h):
                act.wait_ge(s_apT, h + 1)
                if h:
                    act.wait_ge(s_av, h)
                act.activation(apT[0:S2, :, :].rearrange("p b t -> p (b t)"), TURN[0:S2, :], ACT.Copy).then_inc(s_aT, 1)

            def ffn_hi(m):
                act.wait_ge(s_fu, m + 1)
                if m >= RING:
                    act.wait_ge(s_fd, m - RING + 1)
                act.activation(acth[:, m % RING, :], FUP[m % 3][:, :], ACT.Relu).then_inc(s_fh, 1)

            def take_net(j):
                act.wait_ge(s_net, j + 1)
                if j == 3:
                    act.wait_ge(s_ds, 1)
                if j == 5:
                    act.wait_ge(s_vb, 1)
                act.activation(qkvT[:, j % 3, :], FACC[j % 2][:, :], ACT.Copy).then_inc(s_qkv, 1)

            def self_exp(h):
                act.wait_ge(s_dm, 2 * h + 2)
                for i in range(HALF):
                    act.activation(aexp[:, i, :], SIDE[:, i * T:(i + 1) * T], ACT.Exp, scale=SCALE, bias=amax[:, i:i + 1],
                                   accum_out=asum[:, i:i + 1]).then_inc(s_de, 1)

            def self_pT(h):
                act.wait_ge(s_dpT, h + 1)
                if h:
                    act.wait_ge(s_do, h)
                act.activation(apT[:, :, :].rearrange("p b t -> p (b t)"), TURN[:, :], ACT.Copy).then_inc(s_dT, 1)

            for m in range(PAIRS):
                moe_gelu(m)
                if m:
                    moe_hi(m - 1)
                if m == 2:
                    turn_out(B - 1)
                if m == 8:
                    split_x(1)
            moe_hi(PAIRS - 1)
            exp_logits(1)
            take_y(0)
            moe_gelu(PAIRS)
            moe_hi(PAIRS)
            moe_gelu(PAIRS + 1)
            moe_gelu(PAIRS + 2)
            moe_hi(PAIRS + 1)
            attn1_exp(0)
            moe_hi(PAIRS + 2)
            attn1_pT(0)
            for m in range(PAIRS + 3, 2 * PAIRS):
                moe_gelu(m)
                if m > PAIRS + 3:
                    moe_hi(m - 1)
                if m == PAIRS + 8:
                    split_x(2)
            moe_hi(2 * PAIRS - 1)
            take_y(1)
            w2_hi(0)
            for k in range(UPB):
                ffn_hi(k)
                if k % 4 == 1 and k // 4 + 1 < CUTS:
                    w2_hi(k // 4 + 1)
                if k >= CHUNKS and k % CHUNKS == 4:
                    take_net(k // CHUNKS - 1)
                if k == 10:
                    attn1_exp(1)
                if k == 12:
                    attn1_pT(1)
                if k == 19:
                    split_x(3)
            for k in range(UPB):
                ffn_hi(UPB + k)
                if k == 2:
                    take_net(2)
                if k >= CHUNKS and k % CHUNKS == 4:
                    take_net(3 + k // CHUNKS - 1)
                if k == 5:
                    self_exp(0)
                if k == 7:
                    self_pT(0)
                if k == 22:
                    self_exp(1)
            self_pT(1)
            take_net(5)

        @block.vector
        def _(dve):
            def ln_stats(k, batches=range(HALF)):
                l, h = NORMS[k]
                if batches[0]:
                    dve.wait_ge(s_stats, HALF * k + batches[0])
                elif k:
                    dve.wait_ge(s_mv, k)
                for i in batches:
                    dve.wait_ge(*[(s_x, 16), (s_x1, HALF * h + i + 1), (s_x2, h + 1), (s_x3, HALF * h + i + 1)][l])
                    dve.bn_stats(stats[:, i, :], xs[l][:, HALF * h + i, :]).then_inc(s_stats, 1)
                if batches[-1] == HALF - 1:
                    dve.wait_ge(s_stats, HALF * (k + 1))
                    for i in range(HALF):
                        last = dve.bn_aggr(meanvar[:, k, i, :], stats[:, i, :])
                    last.then_inc(s_mv, 1)
                    dve.wait_ge(s_mv, k + 1)
                    dve.tensor_scalar(vareps[:, k, :], meanvar[:, k, :, 1], EPS, None, ALU.add).then_inc(s_ve, 1)

            def normalize(k):
                l, h = NORMS[k]
                dve.wait_ge(s_rstd, k + 1)
                if k > 2:
                    dve.wait_ge(s_tp, k - 2)
                for i in range(HALF):
                    dve.tensor_scalar(xn[:, i, :], xs[l][:, HALF * h + i, :], meanvar[:, k, i, 0:1], rstd[:, k, i:i + 1],
                                      ALU.subtract, ALU.mult).then_inc(s_xn, 1)

            def take_xnT(q):
                dve.wait_ge(s_tp, q + 1)
                if q:
                    dve.wait_ge(*[(s_lg, 1), (s_lg, 2), (s_as, 1), (s_ns, 1), (s_as, 2)][q - 1])
                if q in (1, 2, 4):
                    dve.wait_ge(s_xl, {1: 1, 2: 2, 4: 3}[q])
                dve.tensor_copy(xnT[:, :], (SIDE0 if q == 0 else TURN)[:, :]).then_inc(s_xnT, 1)

            def repeat_x(b):
                k, i = divmod(b, HALF)
                dve.wait_ge(s_rstd, k + 1)
                if b:
                    dve.wait_ge(s_xraw, b)
                dve.tensor_scalar(xrep[:, :, :, :],
                                  x0[:, b, :].rearrange("t (g e) -> t g e", e=HD)[:, :, None, :].broadcast_to([T, 16, 4, HD]),
                                  meanvar[:, k, i, 0:1], rstd[:, k, i:i + 1], ALU.subtract, ALU.mult).then_inc(s_xrep, 1)

            def stack_x(b):
                dve.wait_ge(s_xsign, b + 1)
                if b >= 2:
                    dve.wait_ge(s_sT, 4 * b - 4)
                dve.scalar_tensor_tensor(xst[:, b % 2, :, :].rearrange("p j t -> p (j t)"), TA[:, :],
                                         c_sb[:, C_BX:C_BX + 1], usplit[:, 0, :], ALU.mult, ALU.add
                                         ).then_inc(s_xst, 1)

            def stack_k(b):
                dve.wait_ge(s_ksign, b + 1)
                if b >= 2:
                    dve.wait_ge(s_sT, 4 * b - 4)
                dve.scalar_tensor_tensor(kst[:, b % 2, :, :].rearrange("p j t -> p (j t)"), key_bank(b)[:, 0:BLOCKS * S2],
                                         c_sb[:, C_BK:C_BK + 1], usplit[:, 1, 0:BLOCKS * S2], ALU.mult, ALU.add
                                         ).then_inc(s_kst, 1)

            def value_rest(k):
                dve.wait_ge(s_vp, 2 * k + 1)
                if k == 0:
                    dve.wait_ge(s_ctx, 16)
                res = shared[0:S2, 4 * NT:6 * NT].rearrange("s (g e) -> s g e", e=HD)
                src = ctx_sb[:, :, :].rearrange("s b (h e) -> s (b h) e", e=HD) if k == 0 else res
                parts = vparts[:, :, :, :].rearrange("s b h v -> s (b h) v")
                dst = res if k == 0 else parts[:, :, 2 * HD:3 * HD]
                dve.tensor_tensor(dst, src, parts[:, :, k * HD:(k + 1) * HD], ALU.subtract).then_inc(s_vp, 1)

            def max_unit(n):
                dve.wait_ge(s_sc, n + 1)
                if n >= 4:
                    dve.wait_ge(s_sT, n - 3)
                dve.tensor_reduce(negmax[:, n % 4, :], SC[n % 2][:, 0:BLOCKS * S2].rearrange("t (j k) -> t j k", k=S2),
                                  AX.X, ALU.max, negate=True).then_inc(s_nm, 1)

            def normalize_out(b):
                O = out_bank(b)[:, 0:HEADS * VCOLS].rearrange("t (h v) -> t h v", v=VCOLS)
                dve.wait_ge(s_pv, TILES * (b + 1))
                dve.reciprocal(rden[:, :], O[:, :, 3 * HD]).then_inc(s_rd, 1)
                dve.tensor_reduce(osum[:, :].rearrange("t (h e) -> t h e", e=HD),
                                  O[:, :, 0:3 * HD].rearrange("t h (s e) -> t h e s", s=3), AX.X, ALU.add).then_inc(s_rd, 1)
                dve.wait_ge(s_rd, 2 * b + 2)
                if b:
                    dve.wait_ge(s_onp, b)
                dve.tensor_tensor(onorm[:, :].rearrange("t (h e) -> t h e", e=HD), osum[:, :].rearrange("t (h e) -> t h e", e=HD),
                                  rden[:, :, None].broadcast_to([T, HEADS, HD]), ALU.mult).then_inc(s_on, 1)

            def add_x1(b):
                dve.wait_ge(s_y0, b + 1)
                dve.wait_ge(s_xbo, 1)
                dve.tensor_tensor(xres[:, b, :], out_bank(b)[:, D:2 * D], xres[:, b, :], ALU.add).then_inc(s_x1, 1)

            def take_gsel():
                dve.wait_ge(s_mid, 16 * 6)
                dve.tensor_copy(gsel_sb[:, :, :], gsel_f32).then_inc(s_gsel, 1)

            def add_bo():
                dve.tensor_tensor(xres[:, :, :], x0[:, :, :], rows_sb[:, None, R_BO0:R_BO0 + D].broadcast_to([T, B, D]),
                                  ALU.add).then_inc(s_xbo, 1)

            def mask_scale():
                dve.wait_ge(s_mid, 16 * 6)
                dve.wait_ge(s_gsel, 1)
                dve.tensor_scalar(mscale[:, :], mask_u8[:, :], SCALE, None, ALU.mult).then_inc(s_mk, 1)

            def mask_negative():
                dve.tensor_scalar(mneg, mask_u8[:, :], -NEG, NEG, ALU.mult, ALU.add).then_inc(s_mk, 1)

            def mask_bias_scale():
                dve.wait_ge(s_ckr, 8)
                dve.wait_ge(s_mk, 2)
                dve.tensor_tensor(cmask[:, :], cB, mscale[:, :], ALU.mult).then_inc(s_mk, 1)

            def mask_bias_add():
                dve.wait_ge(s_mk, 3)
                dve.tensor_tensor(cmask[:, :], cmask[:, :], mneg, ALU.add).then_inc(s_mk, 1)

            def take_vo(h):
                dve.wait_ge(s_ck, 9 + h)
                dve.tensor_tensor(vo[:, HALF * h:HALF * (h + 1), :], SIDE0[0:S2, :].rearrange("s (b d) -> s b d", d=D),
                                  rows_sb[0:S2, None, R_BO1:R_BO1 + D].broadcast_to([S2, HALF, D]), ALU.add).then_inc(s_vo, 1)

            def gate_start(h):
                L = (SIDE0 if h == 0 else MIX)[:, 0:HALF * EXPERTS].rearrange("t (b e) -> t b e", e=EXPERTS)
                dve.wait_ge(s_lg, h + 1)
                dve.tensor_reduce(lmax[:, :], L, AX.X, ALU.max).then_inc(s_gstep, 1)
                dve.wait_ge(s_gstep, 17 * h + 1)
                if h:
                    dve.wait_ge(s_lex, h)
                dve.tensor_tensor(lshift[:, :, :], L, lmax[:, :, None].broadcast_to([T, HALF, EXPERTS]), ALU.subtract
                                  ).then_inc(s_lsh, 1)

            def gate_step(h, step):
                g0 = 17 * h
                if step == 0:
                    softmax_sum(h, g0)
                if step == 1:
                    four_largest(g0)
                if step == 2:
                    gate_off_top(g0)
                if step == 3:
                    gate_in_parts(h, g0)

            def softmax_sum(h, g0):
                dve.wait_ge(s_lex, h + 1)
                dve.tensor_reduce(lsum[:, :], lexp[:, :, :], AX.X, ALU.add).then_inc(s_gstep, 1)
                dve.wait_ge(s_gstep, g0 + 2)
                dve.reciprocal(lrec[:, :], lsum[:, :]).then_inc(s_gstep, 1)
                dve.wait_ge(s_gstep, g0 + 3)
                dve.tensor_tensor(probs[:, :, :], lexp[:, :, :], lrec[:, :, None].broadcast_to([T, HALF, EXPERTS]), ALU.mult
                                  ).then_inc(s_gstep, 1)

            def four_largest(g0):
                dve.wait_ge(s_gstep, g0 + 4)
                for i in range(HALF):
                    dve.max(top8[:, i, :], probs[:, i, :]).then_inc(s_gstep, 1)
                dve.wait_ge(s_gstep, g0 + 8)
                dve.memset(top8[:, :, TOPK:8], -1.0).then_inc(s_gstep, 1)

            def gate_off_top(g0):
                dve.wait_ge(s_gstep, g0 + 9)
                for i in range(HALF):
                    dve.match_replace(rest[:, i, :], top8[:, i, :], probs[:, i, :], 0.0).then_inc(s_gstep, 1)
                dve.wait_ge(s_gstep, g0 + 13)
                dve.tensor_tensor(gate[:, :, :], probs[:, :, :], rest[:, :, :], ALU.subtract).then_inc(s_gstep, 1)

            def gate_in_parts(h, g0):
                dve.wait_ge(s_gstep, g0 + 14)
                if h:
                    dve.wait_ge(s_gTp, h)
                dve.tensor_copy(gparts[:, :, 0, :], gate[:, :, :]).then_inc(s_gstep, 1)
                dve.wait_ge(s_gstep, g0 + 15)
                dve.tensor_tensor(gres[:, :, :], gate[:, :, :], gparts[:, :, 0, :], ALU.subtract).then_inc(s_gstep, 1)
                dve.wait_ge(s_gstep, g0 + 16)
                dve.tensor_copy(gparts[:, :, 1, :], gres[:, :, :]).then_inc(s_gstep, 1)
                dve.wait_ge(s_gstep, g0 + 17)
                dve.tensor_tensor(gparts[:, :, 2, :], gres[:, :, :], gparts[:, :, 1, :], ALU.subtract).then_inc(s_gp, 1)

            def take_gateT(h):
                dve.wait_ge(s_gTp, h + 1)
                dve.tensor_copy(gT[:, h, :], (SIDE0 if h == 0 else MIX)[0:48, :].bitcast(BF16)[:, 0:NT]).then_inc(s_gT, 1)

            def moe_gated(m):
                r = m - m // PAIRS - 1
                dve.wait_ge(s_ge, m + 1)
                dve.wait_ge(s_gb, r + 1)
                if m == 1:
                    dve.wait_ge(s_mk, 4)
                if m >= RING:
                    dve.wait_ge(s_al, m - RING + 1)
                dve.tensor_tensor(gated[:, m % RING, :], gelu[:, m % 2, :], GATE[r % 2][:, :], ALU.mult).then_inc(s_ga, 1)

            def add_x2(h):
                dve.wait_ge(s_yb, h + 1)
                half = xres[:, HALF * h:HALF * (h + 1), :].rearrange("t b d -> t (b d)")
                dve.tensor_tensor(half, TURN[:, :], half, ALU.add).then_inc(s_x2, 1)

            def attn1_mask(h):
                dve.wait_ge(s_as, h + 1)
                dve.wait_ge(s_mk, 4)
                dve.tensor_tensor(sc1, SIDE[:, 0:NK], mscale[:, h * NK:(h + 1) * NK], ALU.mult).then_inc(s_am, 1)
                dve.wait_ge(s_am, 4 * h + 1)
                if h:
                    dve.wait_ge(s_ae, HALF * h)
                dve.tensor_tensor(sc2[:, :], sc1, cmask[:, h * NK:(h + 1) * NK], ALU.add).then_inc(s_am, 1)
                dve.wait_ge(s_am, 4 * h + 2)
                dve.tensor_reduce(amax[:, :], sc2[:, :].rearrange("t (b k) -> t b k", k=S2), AX.X, ALU.max, negate=True
                                  ).then_inc(s_am, 1)

            def add_x3(h):
                dve.wait_ge(s_ae, HALF * (h + 1))
                dve.reciprocal(arec[:, :], asum[:, :]).then_inc(s_am, 1)
                dve.wait_ge(s_am, 4 * h + 4)
                dve.wait_ge(s_av, h + 1)
                for i in range(HALF):
                    b = HALF * h + i
                    dve.scalar_tensor_tensor(xres[:, b, :], MIX[:, i * T:(i + 1) * T], arec[:, i:i + 1], xres[:, b, :],
                                             ALU.mult, ALU.add).then_inc(s_x3, 1)

            def leaf_part(k):
                if k == 0:
                    dve.wait_ge(s_late, 32)
                else:
                    dve.wait_ge(s_lb, 2)
                src = sres[:, :, :] if k else leafb_sb[:, :, :]
                dve.tensor_copy(spart[:, k, :, :], src).then_inc(s_lb, 1)
                dve.wait_ge(s_lb, 2 * k + 1)
                dve.tensor_tensor(spart[:, 2, :, :] if k else sres[:, :, :], src, spart[:, k, :, :], ALU.subtract).then_inc(s_lb, 1)

            def leaf_merge(k):
                part = spart[:, k, :, :].rearrange("p a n -> p (a n)")
                merged = scomb[:, :, :].rearrange("p a n -> p (a n)")
                take = c_sb[:, C_PART + k:C_PART + k + 1]
                dve.wait_ge(s_lb, 4 + k)
                if k == 0:
                    dve.tensor_scalar(merged, part, take, None, ALU.mult).then_inc(s_lb, 1)
                else:
                    dve.scalar_tensor_tensor(merged, part, take, merged, ALU.mult, ALU.add).then_inc(s_lb, 1)

            def leaf_down():
                dve.wait_ge(s_lb, 7)
                dve.tensor_copy(ldown[:, :, :], scomb[:, :, 64:192]).then_inc(s_lb, 1)

            def leaf_up(a):
                dve.tensor_tensor(lup[:, a, :, :], scomb[:, a, None, 0:64].broadcast_to([128, LEAVES, 64]),
                                  c_sb[:, C_LEAF:C_LEAF + LEAVES, None].broadcast_to([128, LEAVES, 64]), ALU.mult
                                  ).then_inc(s_lb, 1)

            def route_root(h):
                t0 = 11 * h
                dve.wait_ge(s_ns, h + 1)
                dve.tensor_tensor(nscore[:, :, :], SIDE[:, 0:HALF * NETS * NODES].rearrange("t (b n) -> t b n", b=HALF),
                                  rows_sb[:, None, R_NB:R_NB + NETS * NODES].broadcast_to([T, HALF, NETS * NODES]), ALU.add
                                  ).then_inc(s_tree, 1)
                dve.wait_ge(s_tree, t0 + 1)
                dve.tensor_scalar(right[:, :, :].rearrange("t g n -> t (g n)"), nscore[:, :, :].rearrange("t b n -> t (b n)"),
                                  0.0, None, ALU.is_ge).then_inc(s_tree, 1)
                dve.wait_ge(s_tree, t0 + 2)
                dve.tensor_copy(lev[1][:, :, 1], right[:, :, 0]).then_inc(s_tree, 1)
                dve.tensor_scalar(lev[1][:, :, 0], right[:, :, 0], -1.0, 1.0, ALU.mult, ALU.add).then_inc(s_tree, 1)

            def route_down(h):
                t0 = 11 * h
                for d in range(1, 4):
                    n = 2 ** d
                    dve.wait_ge(s_tree, t0 + 2 + 2 * d)
                    kids = lev[d + 1][:, :, :].rearrange("t g (n two) -> t g n two", two=2)
                    dve.tensor_tensor(kids[:, :, :, 1], lev[d][:, :, :], right[:, :, n - 1:2 * n - 1], ALU.mult).then_inc(s_tree, 1)
                    dve.wait_ge(s_tree, t0 + 3 + 2 * d)
                    dve.tensor_tensor(kids[:, :, :, 0], lev[d][:, :, :], kids[:, :, :, 1], ALU.subtract).then_inc(s_tree, 1)

            def route_rows(h):
                t0 = 11 * h
                dve.wait_ge(s_tree, t0 + 10)
                leaf = lev[4][:, :, :].rearrange("t (b n) l -> t b n l", b=HALF)
                if h:
                    dve.wait_ge(s_selp, h)
                dve.tensor_scalar(selrow[:, :, 0:3, 0, :], leaf, -1.0, 1.0, ALU.mult, ALU.add).then_inc(s_tree, 1)
                for s in (1, 2, 3):
                    last = dve.tensor_copy(selrow[:, :, 0:3, s, :], leaf)
                last.then_inc(s_selrow, 1)

            def take_selT(h):
                dve.wait_ge(s_selp, h + 1)
                if h == 0:
                    dve.wait_ge(s_lb, 10)
                dve.tensor_copy(selT[:, h, :, :], SIDE[:, :].bitcast(BF16).rearrange("p (a t) -> p a t", a=2)).then_inc(s_selT, 1)

            def ffn_lo(m):
                dve.wait_ge(s_fh, m + 1)
                if m >= RING:
                    dve.wait_ge(s_fd, m - RING + 1)
                dve.scalar_tensor_tensor(actl[:, m % RING, :], FUP[m % 3][:, :], 0.0, acth[:, m % RING, :].bitcast(F32),
                                         ALU.max, ALU.subtract).then_inc(s_fl, 1)

            def self_v(h):
                dve.wait_ge(s_vb, h + 1)
                if h:
                    dve.wait_ge(s_do, h)
                dve.tensor_copy(vnat[:, :, :].rearrange("t b d -> t (b d)"), MIX[:, :]).then_inc(s_vn, 1)

            def self_max(h):
                dve.wait_ge(s_ds, h + 1)
                dve.tensor_reduce(dmax[:, :], SIDE[:, :].rearrange("t (b k) -> t b k", k=T), AX.X, ALU.max).then_inc(s_dm, 1)
                dve.wait_ge(s_dm, 2 * h + 1)
                dve.tensor_scalar(amax[:, :], dmax[:, :], -SCALE, None, ALU.mult).then_inc(s_dm, 1)

            def self_rec(h):
                dve.wait_ge(s_de, HALF * (h + 1))
                dve.reciprocal(arec[:, :], asum[:, :]).then_inc(s_dr, 1)

            def self_out(h):
                dve.wait_ge(s_dr, h + 1)
                dve.wait_ge(s_do, h + 1)
                for i in range(HALF):
                    b = HALF * h + i
                    dve.scalar_tensor_tensor(xres[:, b, :], MIX[:, i * T:(i + 1) * T], arec[:, i:i + 1], xres[:, b, :],
                                             ALU.mult, ALU.add).then_inc(s_out, 1)

            dve.memset(probh[:, 0, :], 0.0).then_inc(s_zero, 1)
            ln_stats(0)
            ln_stats(1)
            dve.wait_ge(s_fold, 2)
            dve.tensor_copy(brep[:, :, :].rearrange("p j (t c e) -> p (j t) c e", t=TILES, c=4),
                            OUT[:, 0:D].rearrange("p (g e) -> p g e", e=HD)[:, :, None, :].broadcast_to([128, 16, 4, HD])
                            ).then_inc(s_brep, 1)
            dve.tensor_copy(cvo[:, :], OUT[:, D:2 * D]).then_inc(s_cvo, 1)
            repeat_x(0)
            value_rest(0)
            repeat_x(1)
            stack_k(0)
            stack_x(0)
            for n in range(UNITS):
                b, p = divmod(n, TILES)
                max_unit(n)
                if n == 0:
                    value_rest(1)
                if p == 0 and b + 1 < B:
                    stack_x(b + 1)
                if p == 1 and b + 2 < B:
                    repeat_x(b + 2)
                if p == 2 and b >= 2:
                    add_x1(b - 2)
                if p == 2 and b + 1 < B:
                    stack_k(b + 1)
                if p == 3 and b:
                    normalize_out(b - 1)
                if n == 2:
                    take_gsel()
                if n == 3:
                    add_bo()
                if n == 5:
                    mask_scale()
                if n == 8:
                    mask_negative()
                if n == 20:
                    mask_bias_scale()
                if n == 24:
                    mask_bias_add()
                if n in (21, 23):
                    take_vo((n - 21) // 2)
                if n == 19:
                    ln_stats(2, range(3))
                if n == 22:
                    ln_stats(2, range(3, 4))
                if n == 26:
                    normalize(2)
                if n == 27:
                    take_xnT(0)
                if n == 28:
                    gate_start(0)
                if n == 30:
                    gate_step(0, 0)
                    gate_step(0, 1)
                if n == 31:
                    gate_step(0, 2)
                    gate_step(0, 3)
            add_x1(B - 2)
            take_gateT(0)
            ln_stats(3, range(3))
            normalize_out(B - 1)
            for m in range(1, PAIRS):
                moe_gated(m)
                if m == 1:
                    leaf_part(0)
                if m == 3:
                    add_x1(B - 1)
                    ln_stats(3, range(3, 4))
                    leaf_part(1)
                if m == 5:
                    normalize(3)
                    leaf_merge(0)
                if m == 6:
                    leaf_merge(1)
                if m == 7:
                    take_xnT(1)
            leaf_merge(2)
            leaf_down()
            gate_start(1)
            leaf_up(0)
            add_x2(0)
            ln_stats(4)
            gate_step(1, 0)
            gate_step(1, 1)
            normalize(4)
            gate_step(1, 2)
            gate_step(1, 3)
            take_xnT(2)
            take_gateT(1)
            moe_gated(PAIRS + 1)
            attn1_mask(0)
            moe_gated(PAIRS + 2)
            leaf_up(1)
            for m in range(PAIRS + 3, 2 * PAIRS):
                moe_gated(m)
                if m == PAIRS + 3:
                    add_x3(0)
                    ln_stats(5)
                if m == PAIRS + 5:
                    normalize(5)
                if m == PAIRS + 6:
                    take_xnT(3)
            route_root(0)
            route_down(0)
            route_rows(0)
            take_selT(0)
            for k in range(UPB):
                ffn_lo(k)
                if k == 2:
                    add_x2(1)
                if k == 3:
                    ln_stats(6)
                if k == 5:
                    normalize(6)
                if k == 7:
                    take_xnT(4)
                if k == 9:
                    attn1_mask(1)
                if k == 14:
                    add_x3(1)
                if k == 15:
                    ln_stats(7)
                if k == 16:
                    normalize(7)
                if k == 18:
                    take_xnT(5)
                if k == 19:
                    route_root(1)
                if k == 20:
                    route_down(1)
                if k == 21:
                    route_rows(1)
            take_selT(1)
            for k in range(UPB):
                ffn_lo(UPB + k)
                if k == 3:
                    self_max(0)
                if k == 4:
                    self_v(0)
                if k == 6:
                    self_rec(0)
                if k == 8:
                    self_out(0)
                if k == 20:
                    self_max(1)
            self_rec(1)
            self_v(1)
            self_out(1)

        @block.tensor
        def _(pe):
            def split_product(dst, w, x_, w_cols, first, last):
                (wh, wl), (x_hi, x_lo) = w, x_
                pe.matmul(dst, wl[:, w_cols], x_hi, start=first, stop=False)
                pe.matmul(dst, wh[:, w_cols], x_lo, start=False, stop=False)
                return pe.matmul(dst, wh[:, w_cols], x_hi, start=False, stop=last)

            def turn_x(b):
                pe.wait_ge(s_xrep, b + 1)
                if b:
                    pe.wait_ge(s_xst, b)
                    pe.wait_ge(s_kst, b)
                rep = xrep[:, :, :, :].rearrange("t g c e -> t (g c e)")
                for j in range(BLOCKS):
                    last = pe.transpose(TA[:, j * T:(j + 1) * T], rep[:, j * 128:(j + 1) * 128], ident)
                last.then_inc(s_xraw, 1)

            def raise_k(b):
                pe.wait_ge(s_brep, 1)
                if b:
                    pe.wait_ge(s_xst, b + 1)
                for j in range(BLOCKS):
                    last = pe.matmul(key_bank(b)[:, j * S2:(j + 1) * S2], brep[:, j, :], ctxT_sb[:, b * S2:(b + 1) * S2],
                                     start=True, stop=True)
                last.then_inc(s_kraw, 1)

            def keys(p, j, b):
                return kst[32 * p:32 * p + 32, b % 2, j, :]

            def queries(p, j, b):
                return xst[32 * p:32 * p + 32, b % 2, j, :]

            def scores(n):
                b, p = divmod(n, TILES)
                pe.wait_ge(s_xst, b + 1)
                pe.wait_ge(s_kst, b + 1)
                if n >= 2:
                    pe.wait_ge(s_nm, n - 1)
                for j in range(BLOCKS):
                    last = pe.matmul(SC[n % 2][:, j * S2:(j + 1) * S2], queries(p, j, b), keys(p, j, b), start=True, stop=True,
                                     tile_position=(32 * p, 0))
                last.then_inc(s_sc, 1)

            def scoresT(n):
                b, p = divmod(n, TILES)
                pe.wait_ge(s_nm, n + 1)
                if n >= 2:
                    pe.wait_ge(s_p, n - 1)
                for j in range(BLOCKS):
                    pe.matmul(SCT[n % 2][0:S2, j * T:(j + 1) * T], negmax[:, n % 4, j:j + 1].broadcast_to([T, S2]), idb[:, :],
                              start=(j == 0), stop=False, skip_group_check=True)
                for j in range(BLOCKS):
                    last = pe.matmul(SCT[n % 2][0:S2, j * T:(j + 1) * T], keys(p, j, b), queries(p, j, b),
                                     start=False, stop=True, tile_position=(32 * p, 0), skip_group_check=True)
                last.then_inc(s_sT, 1)

            def values(n):
                b, p = divmod(n, TILES)
                pe.wait_ge(s_ph, n + 1)
                pe.wait_ge(s_pl, n + 1)
                if n == 0:
                    pe.wait_ge(s_vp, 4)
                    pe.wait_ge(s_memset, 2)
                    pe.wait_ge(s_cvo, 1)
                if p == 0 and b >= 2:
                    pe.wait_ge(s_x1, b - 1)
                for j in range(BLOCKS):
                    h = BLOCKS * j + p
                    dst = out_bank(b)[:, h * VCOLS:(h + 1) * VCOLS]
                    pe.matmul(dst, probl[:, n % 3, j * T:(j + 1) * T], vparts[:, b, h, :], start=True, stop=False)
                    last = pe.matmul(dst, probh[:, n % 3, j * T:(j + 1) * T], vparts[:, b, h, :], start=False, stop=True)
                last.then_inc(s_pv, 1)

            def turn_out(b):
                pe.wait_ge(s_on, b + 1)
                pe.transpose(out_bank(b)[:, 0:T], onorm[:, :], ident).then_inc(s_onp, 1)

            def project_out(b):
                pe.wait_ge(s_onT, b + 1)
                pe.matmul(out_bank(b)[:, D:2 * D], onT[:, :], cvo[:, :], start=True, stop=True).then_inc(s_y0, 1)

            def context_product(i):
                h = i % 2
                if i:
                    pe.wait_ge(s_ckr, i)
                lhsT, rhs = [(attnw_sb[:, 1, :], ctxT_sb), (attnw_sb[:, 2, :], ctxT_sb), (attnw_sb[:, 0, :], kT1),
                             (cols_sb[:, V_BQ:V_BQ + 1].broadcast_to([128, 128]), kT1)][i // 2]
                pe.matmul(SIDE0[:, 0:NK], lhsT, rhs[:, h * NK:(h + 1) * NK], start=True, stop=True).then_inc(s_ck, 1)

            def context_values(h):
                pe.wait_ge(s_ckr, 8)
                if h:
                    pe.wait_ge(s_vo, h)
                for i in range(HALF):
                    b = HALF * h + i
                    last = pe.matmul(SIDE0[0:S2, i * D:(i + 1) * D], vT1[:, b * S2:(b + 1) * S2], attnw_sb[:, 3, :],
                                     start=True, stop=True)
                last.then_inc(s_ck, 1)

            def turn_xn(q):
                pe.wait_ge(s_xn, HALF * (q + 1))
                pe.wait_ge(*[(s_vo, 2), (s_x1, B), (s_xnT, 2), (s_aT, 1), (s_xnT, 4), (s_aT, 2)][q])
                for i in range(HALF):
                    last = pe.transpose((SIDE0 if q == 0 else TURN)[:, i * T:(i + 1) * T], xn[:, i, :], ident)
                last.then_inc(s_tp, 1)

            def logits(h):
                pe.wait_ge(s_xnT, h + 1)
                for i in range(HALF):
                    last = pe.matmul((SIDE0 if h == 0 else MIX)[:, i * EXPERTS:(i + 1) * EXPERTS], xnT[:, i * T:(i + 1) * T],
                                     router_sb[:, :], start=True, stop=True)
                last.then_inc(s_lg, 1)

            def gateT(h):
                pe.wait_ge(s_gp, h + 1)
                for i in range(HALF):
                    last = pe.transpose((SIDE0 if h == 0 else MIX)[0:48, :].bitcast(BF16)[:, i * T:(i + 1) * T],
                                        gparts[:, i, :, :].rearrange("t s e -> t (s e)"), idb[:, :])
                last.then_inc(s_gTp, 1)

            def moe_up(m):
                h, c = divmod(m, PAIRS)
                if c == 0:
                    pe.wait_ge(s_xl, h + 1)
                if m >= 2:
                    pe.wait_ge(s_ge, m - 1)
                split_product(UP[m % 2][:, :], (up0h, up0l), (xh[:, h, :], xl[:, h, :]), slice(c * 128, (c + 1) * 128), True, True
                              ).then_inc(s_up, 1)

            def moe_gate(m):
                r = m - m // PAIRS - 1
                if m % PAIRS == 1:
                    pe.wait_ge(s_gT, m // PAIRS + 1)
                if r >= 2:
                    pe.wait_ge(s_ga, r - 1)
                pe.matmul(GATE[r % 2][:, :], gsel_sb[:, m % PAIRS - 1, :], gT[:, m // PAIRS, :], start=True, stop=True
                          ).then_inc(s_gb, 1)

            def moe_down(m):
                h, c = divmod(m, PAIRS)
                pe.wait_ge(s_al, m + 1)
                if c == 0:
                    pe.wait_ge(*((s_yT, h) if h else (s_x1, B - 1)))
                split_product(ACC[:, :], (down0h, down0l), (acth[:, m % RING, :], actl[:, m % RING, :]),
                              slice(c * 128, (c + 1) * 128), c == 0, c == PAIRS - 1).then_inc(s_dn, 1)

            def turn_y(h):
                pe.wait_ge(s_yT, h + 1)
                pe.wait_ge(s_xnT, 2 * h + 2)
                for i in range(HALF):
                    last = pe.transpose(TURN[:, i * T:(i + 1) * T], yT[:, i * T:(i + 1) * T], ident)
                last.then_inc(s_yb, 1)

            def attn1_scores(h):
                pe.wait_ge(s_xnT, 3 + 2 * h)
                if h:
                    pe.wait_ge(s_selT, 1)
                for i in range(HALF):
                    b = HALF * h + i
                    last = pe.matmul(SIDE[:, i * S2:(i + 1) * S2], xnT[:, i * T:(i + 1) * T], aK[:, b * S2:(b + 1) * S2],
                                     start=True, stop=True)
                last.then_inc(s_as, 1)

            def attn1_pT(h):
                pe.wait_ge(s_ae, HALF * (h + 1))
                for i in range(HALF):
                    last = pe.transpose(TURN[0:S2, i * T:(i + 1) * T], aexp[:, i, 0:S2], ident)
                last.then_inc(s_apT, 1)

            def attn1_values(h):
                pe.wait_ge(s_aT, h + 1)
                pe.wait_ge(*((s_x3, HALF * h) if h else (s_gT, 2)))
                for i in range(HALF):
                    b = HALF * h + i
                    last = pe.matmul(MIX[:, i * T:(i + 1) * T], apT[0:S2, i, :], vo[:, b, :], start=True, stop=True)
                last.then_inc(s_av, 1)

            def node_scores(h):
                pe.wait_ge(s_xnT, 4 + 2 * h)
                pe.wait_ge(s_late, 32)
                pe.wait_ge(s_am, 4 * h + 1)
                for i in range(HALF):
                    last = pe.matmul(SIDE[:, i * NETS * NODES:(i + 1) * NETS * NODES], xnT[:, i * T:(i + 1) * T],
                                     nodew_sb[:, :], start=True, stop=True)
                last.then_inc(s_ns, 1)

            def turn_sel(h):
                pe.wait_ge(s_selrow, h + 1)
                pe.wait_ge(s_selzero, 1)
                for a in range(2):
                    for i in range(HALF):
                        last = pe.transpose(SIDE[:, :].bitcast(BF16)[:, a * NT + i * T:a * NT + (i + 1) * T],
                                            selrow[:, i, 2 * a:2 * a + 2, :, :].rearrange("t n s l -> t (n s l)"), idb[:, :])
                last.then_inc(s_selp, 1)

            def net_rows(net):
                return slice(SEL * (net % 2), SEL * (net % 2) + SEL), net // 2

            def ffn_up(m):
                h, k = divmod(m, UPB)
                if k == 0:
                    pe.wait_ge(s_xl, 3 + h)
                if m == 0:
                    pe.wait_ge(s_lo1, CUTS)
                    pe.wait_ge(s_ge, 2 * PAIRS)
                if m == 2:
                    pe.wait_ge(s_ga, 2 * (PAIRS - 1))
                if m >= 3:
                    pe.wait_ge(s_fl, m - 2)
                split_product(FUP[m % 3][:, :], (w1h, w1l), (xh[:, h, :], xl[:, h, :]), slice(k * 128, (k + 1) * 128), True, False)

            def ffn_select(m):
                h, k = divmod(m, UPB)
                net, c = divmod(k, CHUNKS)
                rows_, a = net_rows(net)
                if k == 0:
                    pe.wait_ge(s_selT, h + 1)
                    pe.wait_ge(s_lb, 10)
                pe.matmul(FUP[m % 3][:, :], lup[rows_, a, 2 * c:2 * c + 2, :].rearrange("r l e -> r (l e)"), selT[rows_, h, a, :],
                          start=False, stop=True).then_inc(s_fu, 1)

            def ffn_down(m):
                h, k = divmod(m, UPB)
                net, c = divmod(k, CHUNKS)
                j = NETS * h + net
                acc = FACC[j % 2]
                rows_, a = net_rows(net)
                pe.wait_ge(s_fl, m + 1)
                if h == 0 and k % (CUT // 128) == 0:
                    pe.wait_ge(s_lo2, k // (CUT // 128) + 1)
                if c == 0:
                    pe.wait_ge(*((s_qkv, j - 1) if j >= 2 else (s_yT, 2) if j == 0 else (s_ga, 2 * (PAIRS - 1))))
                split_product(acc[:, :], (w2h, w2l), (acth[:, m % RING, :], actl[:, m % RING, :]), slice(k * 128, (k + 1) * 128),
                              c == 0, False).then_inc(s_fd, 1)
                if c == CHUNKS - 1:
                    pe.matmul(acc[:, :], ldown[rows_, a, :], selT[rows_, h, a, :], start=False, stop=True).then_inc(s_net, 1)

            def self_turn_v(h):
                pe.wait_ge(s_qkv, NETS * (h + 1))
                pe.wait_ge(*((s_out, HALF) if h else (s_x3, B)))
                for i in range(HALF):
                    last = pe.transpose(MIX[:, i * T:(i + 1) * T], qkvT[:, 2, i * T:(i + 1) * T], ident)
                last.then_inc(s_vb, 1)

            def self_scores(h):
                pe.wait_ge(s_qkv, NETS * h + 2)
                pe.wait_ge(*((s_de, HALF) if h else (s_selT, 2)))
                for i in range(HALF):
                    last = pe.matmul(SIDE[:, i * T:(i + 1) * T], qkvT[:, 0, i * T:(i + 1) * T], qkvT[:, 1, i * T:(i + 1) * T],
                                     start=True, stop=True)
                last.then_inc(s_ds, 1)

            def self_pT(h):
                pe.wait_ge(s_de, HALF * (h + 1))
                pe.wait_ge(*((s_dT, 1) if h else (s_xnT, 6)))
                for i in range(HALF):
                    last = pe.transpose(TURN[:, i * T:(i + 1) * T], aexp[:, i, :], ident)
                last.then_inc(s_dpT, 1)

            def self_values(h):
                pe.wait_ge(s_dT, h + 1)
                pe.wait_ge(s_vn, h + 1)
                for i in range(HALF):
                    last = pe.matmul(MIX[:, i * T:(i + 1) * T], apT[:, i, :], vnat[:, i, :], start=True, stop=True)
                last.then_inc(s_do, 1)

            def warm_up(count):
                for _ in range(count):
                    pe.matmul(SC[1][:, :], probh[:, 0, 0:128], probh[:, 0, :], start=True, stop=True)

            pe.wait_ge(s_zero, 1)
            warm_up(WARM0)
            pe.wait_ge(s_early, 16 * 4)
            pe.matmul(OUT[:, 0:D], blockw_sb[:, 1, :], blockw_sb[:, 0, :], start=True, stop=True).then_inc(s_fold, 1)
            pe.matmul(OUT[:, D:2 * D], blockw_sb[:, 2, :], woT_sb[:, :], start=True, stop=True).then_inc(s_fold, 1)
            turn_x(0)
            raise_k(0)
            warm_up(WARM1)
            scores(0)
            pe.wait_ge(s_idb, 1)
            for n in range(UNITS):
                b, p = divmod(n, TILES)
                if n == 0:
                    turn_x(1)
                if n + 1 < UNITS:
                    scores(n + 1)
                if p == 1 and b + 1 < B:
                    raise_k(b + 1)
                if p == 3 and b + 2 < B:
                    turn_x(b + 2)
                scoresT(n)
                if n >= 2:
                    values(n - 2)
                if p == 0 and b >= 2:
                    turn_out(b - 2)
                if p == 1 and b >= 2:
                    project_out(b - 2)
                if n == 4:
                    pe.wait_ge(s_mid, 16 * 6)
                if n in range(4, 20, 2):
                    context_product((n - 4) // 2)
                if n in (20, 22):
                    context_values((n - 20) // 2)
                if n == 26:
                    turn_xn(0)
                if n == 27:
                    logits(0)

            pe.wait_ge(s_lo0, 2 * CUTS0)
            pe.wait_ge(s_nm, UNITS)
            moe_up(0)
            turn_out(B - 2)
            values(UNITS - 2)
            pe.wait_ge(s_p, UNITS)
            moe_up(1)
            gateT(0)
            project_out(B - 2)
            moe_gate(1)
            values(UNITS - 1)
            for m in range(2, PAIRS):
                moe_up(m)
                moe_gate(m)
                if m == 2:
                    turn_out(B - 1)
                if m == 3:
                    project_out(B - 1)
                if m >= LAG0:
                    moe_down(m - LAG0)
                if m == 7:
                    turn_xn(1)

            moe_down(PAIRS - 3)
            logits(1)
            moe_down(PAIRS - 2)
            moe_down(PAIRS - 1)
            turn_y(0)
            moe_up(PAIRS)
            moe_up(PAIRS + 1)
            turn_xn(2)
            moe_up(PAIRS + 2)
            gateT(1)
            moe_gate(PAIRS + 1)
            attn1_scores(0)
            moe_gate(PAIRS + 2)
            moe_down(PAIRS)
            moe_up(PAIRS + 3)
            moe_down(PAIRS + 1)
            moe_gate(PAIRS + 3)
            attn1_pT(0)
            attn1_values(0)
            moe_down(PAIRS + 2)
            for m in range(PAIRS + 4, 2 * PAIRS):
                if m == PAIRS + 7:
                    turn_xn(3)
                if m == PAIRS + 8:
                    node_scores(0)
                moe_up(m)
                moe_gate(m)
                if m >= PAIRS + 5:
                    moe_down(m - 2)
            moe_down(2 * PAIRS - 2)
            ffn_up(0)
            ffn_up(1)
            turn_sel(0)
            moe_down(2 * PAIRS - 1)
            ffn_up(2)

            for m in range(2 * UPB + LAG):
                if m == 2:
                    turn_y(1)
                if 3 <= m < 2 * UPB:
                    ffn_up(m)
                if m < 2 * UPB:
                    ffn_select(m)
                if m >= LAG:
                    ffn_down(m - LAG)
                if m == 7:
                    turn_xn(4)
                if m == 9:
                    attn1_scores(1)
                if m == 12:
                    attn1_pT(1)
                if m == 14:
                    attn1_values(1)
                if m == 18:
                    turn_xn(5)
                if m == 19:
                    node_scores(1)
                if m == 23:
                    turn_sel(1)
                if m == UPB + 3:
                    self_scores(0)
                if m == UPB + 4:
                    self_turn_v(0)
                if m == UPB + 6:
                    self_pT(0)
                if m == UPB + 8:
                    self_values(0)
                if m == UPB + 21:
                    self_scores(1)
                if m == UPB + 23:
                    self_pT(1)
            self_turn_v(1)
            self_values(1)


def _constants():
    import numpy as np
    row = np.arange(128)
    kind = (row // HD) % 4
    c = np.zeros((128, C_END), np.float32)
    c[:, C_ID:C_ID + 128] = np.eye(128)
    x_lo, k_lo = kind >= 2, kind % 2 == 1
    c[:, C_SX], c[:, C_BX] = np.where(x_lo, -1, 1), x_lo
    c[:, C_SK], c[:, C_BK] = np.where(k_lo, -1, 1), k_lo
    group = (row % SEL) // LEAVES
    c[:, C_PART] = group <= 1
    c[:, C_PART + 1] = group == 2
    c[:, C_PART + 2] = group == 3
    c[:, C_LEAF:C_LEAF + LEAVES] = (row % LEAVES)[:, None] == np.arange(LEAVES)[None, :]
    g = np.zeros((48, PAIRS - 1, 2, 64), np.float32)
    for e in range(EXPERTS):
        g[e::EXPERTS, e // 2, e % 2, :] = 1
    return c, g.reshape(48, PAIRS - 1, 128)


def _layout(a):
    import numpy as np
    f = {n: np.asarray(v) for n, v in a.items()}
    consts, gsel = _constants()
    blockw = np.zeros((128, 3, 128), np.float32)
    for h in range(HEADS):
        s = slice(h * HD, (h + 1) * HD)
        for k, n in enumerate(("Wq", "Wk", "Wv")):
            blockw[s, k, s] = f["L0_xattn_" + n]
    up = np.concatenate([f["L0_ffn_shared_up"], f["L0_ffn_routed_up"]])
    down = np.concatenate([f["L0_ffn_shared_down"], f["L0_ffn_routed_down"]])
    w1 = np.stack([f[f"L1_ffn_{n}_w1"] for n in "qkv"])
    w2 = np.stack([f[f"L1_ffn_{n}_w2"] for n in "qkv"])
    leafb = np.zeros((4, 4, LEAVES, 192), np.float32)
    leafb[:, 0, :, 0:64] = -BIG
    for j, n in enumerate("qkv"):
        leafb[j, 1:, :, 0:64] = f[f"L1_ffn_{n}_b1"]
        leafb[j, 1:, :, 64:] = f[f"L1_ffn_{n}_b2"]
    arrays = {
        "x": f["x"], "ctx": f["ctx_1024"],
        "ctxT": f["ctx_1024"].transpose(2, 0, 1).reshape(D, B * S2),
        "mask": f["mask_BxS2_bk0"].reshape(1, B * S2),
        "consts": consts, "gsel": gsel, "blockw": blockw,
        "woT": f["L0_xattn_Wo"].T,
        "up0": up.transpose(2, 0, 1).reshape(D, PAIRS * 128),
        "down0": down.transpose(0, 2, 1).reshape(PAIRS, 128, D).transpose(1, 0, 2).reshape(128, PAIRS * D),
        "router": f["L0_ffn_router_w"].T,
        "attnw": np.stack([f["L1_xattn_Wq"].T, f["L1_xattn_Wk"], f["L1_xattn_Wv"], f["L1_xattn_Wo"]], 1),
        "cols": np.stack([f["L1_xattn_bk"], f["L1_xattn_bv"], f["L1_xattn_bq"]], 1),
        "rows": np.concatenate([f["L0_xattn_bo"], f["L1_xattn_bo"]] + [f[f"L1_ffn_{n}_node_b"] for n in "qkv"])[None],
        "w1": w1.transpose(2, 0, 1, 3).reshape(D, UPB * 128),
        "w2": w2.reshape(NETS * CHUNKS, 128, D).transpose(1, 0, 2).reshape(128, UPB * D),
        "nodew": np.concatenate([f[f"L1_ffn_{n}_node_w"] for n in "qkv"]).T,
        "leafb": leafb.reshape(2, 128, 192).transpose(1, 0, 2),
    }
    return {n: np.ascontiguousarray(v) for n, v in arrays.items()}


def kernel(**inputs):
    import numpy as _np
    import concourse.bacc as _bacc
    from concourse import mybir as _mybir
    from concourse.bass_utils import run_bass_kernel_spmd as _run

    nc = _bacc.Bacc("TRN2", target_bir_lowering=False, num_devices=1)
    arrays, args = {}, []
    for name, a in _layout(inputs).items():
        arrays[f"in_{name}_dram"] = a
        args.append(nc.dram_tensor(f"in_{name}_dram", a.shape, _mybir.dt.from_np(a.dtype), kind="ExternalInput").ap())
    args.append(nc.dram_tensor("out_0_dram", (B, T, D), _mybir.dt.from_np(_np.dtype("float32")), kind="ExternalOutput").ap())
    build(nc, *args)
    r = _run(nc, [arrays], core_ids=[0])
    return r.results[0]["out_0_dram"]
```
